# Optimizing a Trainium2 kernel written in Bass

```python
import numpy as np
import jax
import jax.numpy as jnp

def _softmax(x, axis=-1):
    return jax.nn.softmax(x, axis=axis)

def _gelu(x):
    return jax.nn.gelu(x, approximate=True)

def _silu(x):
    return jax.nn.silu(x)

def _sigmoid(x):
    return jax.nn.sigmoid(x)

def _layernorm(x, axis=-1, eps=1e-05):
    m = jnp.mean(x, axis=axis, keepdims=True)
    v = jnp.var(x, axis=axis, keepdims=True)
    return (x - m) / jnp.sqrt(v + eps)

def _scatter_add(tgt, idx, src, axis=0):
    return tgt.at[idx].add(src)

def _segment_sum(src, seg, n):
    return jax.ops.segment_sum(src, seg, n)
kernel_name = 'mk_seq_preln_d2_jaxref_r8_2044e9'

def setup_inputs(seed: int=0):
    np.random.seed(seed)
    _w = jnp.asarray

    def _L0_attn_setup():
        import jax, jax.numpy as jnp
        import numpy as np
        B, S, H = (2, 512, 128)
        NKH, NVH, DK, DV = (8, 16, 64, 64)
        KEY_DIM = NKH * DK
        VAL_DIM = NVH * DV
        CONV_DIM = 2 * KEY_DIM + VAL_DIM
        KSZ = 4
        EPS = 1e-06

        def _forward(hidden_states, W_qkv, conv_w, W_z, W_b, W_a, dt_bias, A_log, norm_weight, W_out):
            b, s, _ = hidden_states.shape
            mixed = hidden_states @ W_qkv.T
            x = mixed.transpose(0, 2, 1)
            y = jax.lax.conv_general_dilated(x, conv_w, (1,), [(KSZ - 1, 0)], dimension_numbers=('NCH', 'OIH', 'NCH'), feature_group_count=CONV_DIM)
            mixed = jax.nn.silu(y).transpose(0, 2, 1)
            z = (hidden_states @ W_z.T).reshape(b, s, NVH, DV)
            beta = jax.nn.sigmoid(hidden_states @ W_b.T)
            a = hidden_states @ W_a.T
            g = -jnp.exp(A_log) * jax.nn.softplus(a + dt_bias)
            q, k, v = jnp.split(mixed, [KEY_DIM, 2 * KEY_DIM], axis=-1)
            q = q.reshape(b, s, NKH, DK)
            k = k.reshape(b, s, NKH, DK)
            v = v.reshape(b, s, NVH, DV)
            rep = NVH // NKH
            if rep > 1:
                q = jnp.repeat(q, rep, axis=2)
                k = jnp.repeat(k, rep, axis=2)
            q = q * DK ** (-0.5)

            def step(Sst, inp):
                q_t, k_t, v_t, g_t, b_t = inp
                Sst = Sst * jnp.exp(g_t)[..., None, None]
                kv = jnp.einsum('bhkv,bhk->bhv', Sst, k_t)
                delta = (v_t - kv) * b_t[..., None]
                Sst = Sst + k_t[..., None] * delta[..., None, :]
                o = jnp.einsum('bhkv,bhk->bhv', Sst, q_t)
                return (Sst, o)
            S0 = jnp.zeros((b, NVH, DK, DV), jnp.float32)
            xs = (q.transpose(1, 0, 2, 3), k.transpose(1, 0, 2, 3), v.transpose(1, 0, 2, 3), g.transpose(1, 0, 2), beta.transpose(1, 0, 2))
            _, o = jax.lax.scan(step, S0, xs)
            o = o.transpose(1, 0, 2, 3)
            h_ = o * jax.nn.silu(z)
            var = jnp.mean(h_ * h_, axis=-1, keepdims=True)
            h_ = h_ * jax.lax.rsqrt(var + EPS) * norm_weight
            return h_.reshape(b, s, VAL_DIM) @ W_out.T
        key = jax.random.key(seed)
        ks = jax.random.split(key, 8)
        s = 0.02
        return {'hidden_states': jax.random.normal(ks[0], (B, S, H), jnp.float32), 'W_qkv': jax.random.normal(ks[1], (CONV_DIM, H), jnp.float32) * s, 'conv_w': jax.random.normal(ks[2], (CONV_DIM, 1, KSZ), jnp.float32) * 0.1, 'W_z': jax.random.normal(ks[3], (VAL_DIM, H), jnp.float32) * s, 'W_b': jax.random.normal(ks[4], (NVH, H), jnp.float32) * s, 'W_a': jax.random.normal(ks[5], (NVH, H), jnp.float32) * s, 'dt_bias': jnp.ones((NVH,), jnp.float32), 'A_log': jnp.log(jax.random.uniform(ks[6], (NVH,), jnp.float32, 0.1, 16.0)), 'norm_weight': jnp.ones((DV,), jnp.float32), 'W_out': jax.random.normal(ks[7], (H, VAL_DIM), jnp.float32) * s}
    _L0_attn_in = _L0_attn_setup()

    def _L0_ffn_setup():
        import jax, jax.numpy as jnp
        import numpy as np
        from jax import lax
        D = 128
        H = 176
        E = 8
        K = 2
        ROUTER_SCALE = 1.0

        def _expert(x, w1, b1, w3, b3, w2, b2):
            h = jax.nn.silu((x @ w1 + b1) * (x @ w3 + b3))
            return h @ w2 + b2
        key = jax.random.key(seed)
        ks = jax.random.split(key, 16)
        s = 0.02
        inp = {'x': jax.random.normal(ks[0], (2, 256, D), dtype=jnp.float32), 'gate_w': jax.random.normal(ks[1], (E, D), dtype=jnp.float32) * s, 'gate_b': jax.random.normal(ks[2], (E,), dtype=jnp.float32) * s, 'w1': jax.random.normal(ks[3], (E, D, H), dtype=jnp.float32) * s, 'b1': jax.random.normal(ks[4], (E, H), dtype=jnp.float32) * s, 'w3': jax.random.normal(ks[5], (E, D, H), dtype=jnp.float32) * s, 'b3': jax.random.normal(ks[6], (E, H), dtype=jnp.float32) * s, 'w2': jax.random.normal(ks[7], (E, H, D), dtype=jnp.float32) * s, 'b2': jax.random.normal(ks[8], (E, D), dtype=jnp.float32) * s, 'sw1': jax.random.normal(ks[9], (D, H), dtype=jnp.float32) * s, 'sb1': jax.random.normal(ks[10], (H,), dtype=jnp.float32) * s, 'sw3': jax.random.normal(ks[11], (D, H), dtype=jnp.float32) * s, 'sb3': jax.random.normal(ks[12], (H,), dtype=jnp.float32) * s, 'sw2': jax.random.normal(ks[13], (H, D), dtype=jnp.float32) * s, 'sb2': jax.random.normal(ks[14], (D,), dtype=jnp.float32) * s}
        return inp
    _L0_ffn_in = _L0_ffn_setup()

    def _L1_attn_setup():
        import math
        import jax, jax.numpy as jnp
        import numpy as np
        D_MODEL = 128
        N_HEADS = 16
        D_HEAD = D_MODEL // N_HEADS
        SEQ = 512
        BATCH = 1
        BASE = 10000.0
        EPS = 1e-05

        def _layernorm(x, g, b):
            mu = jnp.mean(x, axis=-1, keepdims=True)
            var = jnp.mean(jnp.square(x - mu), axis=-1, keepdims=True)
            return (x - mu) * jax.lax.rsqrt(var + EPS) * g + b

        def _rotate(x, cos, sin):
            b, H, n, dh = x.shape
            xr = x.reshape(b, H, n, dh // 2, 2)
            x1, x2 = (xr[..., 0], xr[..., 1])
            r1 = x1 * cos - x2 * sin
            r2 = x1 * sin + x2 * cos
            return jnp.stack([r1, r2], axis=-1).reshape(b, H, n, dh)

        def _block(x, ln1_g, ln1_b, ln2_g, ln2_b, Wqkv, Wo, W1, b1, W2, b2):
            b, n, d = x.shape
            H, dh = (N_HEADS, D_HEAD)
            h = _layernorm(x, ln1_g, ln1_b)
            qkv = (h @ Wqkv).reshape(b, n, 3, H, dh)
            q = jnp.transpose(qkv[:, :, 0], (0, 2, 1, 3))
            k = jnp.transpose(qkv[:, :, 1], (0, 2, 1, 3))
            v = jnp.transpose(qkv[:, :, 2], (0, 2, 1, 3))
            inv_freq = BASE ** (-(jnp.arange(0, dh, 2, dtype=jnp.float32) / dh))
            theta = jnp.arange(n, dtype=jnp.float32)[:, None] * inv_freq[None, :]
            cos, sin = (jnp.cos(theta), jnp.sin(theta))
            q = _rotate(q, cos, sin)
            k = _rotate(k, cos, sin)
            s = jnp.einsum('bhqd,bhkd->bhqk', q, k) / math.sqrt(dh)
            causal = jnp.tril(jnp.ones((n, n), dtype=bool))
            s = jnp.where(causal, s, -jnp.inf)
            a = jax.nn.softmax(s, axis=-1)
            o = jnp.einsum('bhqk,bhkd->bqhd', a, v).reshape(b, n, d)
            x = x + o @ Wo
            h2 = _layernorm(x, ln2_g, ln2_b)
            f = jax.nn.gelu(h2 @ W1 + b1, approximate=False) @ W2 + b2
            return x + f
        key = jax.random.key(seed)
        ks = jax.random.split(key, 8)
        d, h = (D_MODEL, 4 * D_MODEL)
        s = 0.02
        return {'x': jax.random.normal(ks[0], (BATCH, SEQ, d), jnp.float32), 'ln1_g': jnp.ones((d,), jnp.float32), 'ln1_b': jnp.zeros((d,), jnp.float32), 'ln2_g': jnp.ones((d,), jnp.float32), 'ln2_b': jnp.zeros((d,), jnp.float32), 'Wqkv': jax.random.normal(ks[1], (d, 3 * d), jnp.float32) * s, 'Wo': jax.random.normal(ks[2], (d, d), jnp.float32) * s, 'W1': jax.random.normal(ks[3], (d, h), jnp.float32) * s, 'b1': jnp.zeros((h,), jnp.float32), 'W2': jax.random.normal(ks[4], (h, d), jnp.float32) * s, 'b2': jnp.zeros((d,), jnp.float32)}
    _L1_attn_in = _L1_attn_setup()

    def _L1_ffn_setup():
        import jax, jax.numpy as jnp
        import numpy as np
        H, F, E_SHARED, E_ROUTED, K = (128, 512, 1, 8, 2)

        def _expert(x, w_up, w_down):
            h = jax.nn.gelu(jnp.einsum('bsh,hf->bsf', x, w_up), approximate=False)
            return jnp.einsum('bsf,fh->bsh', h, w_down)
        key = jax.random.key(seed)
        ks = jax.random.split(key, 6)
        x = jax.random.normal(ks[0], (4, 256, H), dtype=jnp.float32)
        s = 0.02
        shared_up = jax.random.normal(ks[1], (E_SHARED, H, F), dtype=jnp.float32) * s
        shared_down = jax.random.normal(ks[2], (E_SHARED, F, H), dtype=jnp.float32) * s
        routed_up = jax.random.normal(ks[3], (E_ROUTED, H, F), dtype=jnp.float32) * s
        routed_down = jax.random.normal(ks[4], (E_ROUTED, F, H), dtype=jnp.float32) * s
        router_w = jax.random.normal(ks[5], (H, E_ROUTED), dtype=jnp.float32) * s
        return {'x': x, 'shared_up': shared_up, 'shared_down': shared_down, 'routed_up': routed_up, 'routed_down': routed_down, 'router_w': router_w}
    _L1_ffn_in = _L1_ffn_setup()
    _d = {'L0_attn_hidden_states': _L0_attn_in['hidden_states'], 'L0_attn_W_qkv': _L0_attn_in['W_qkv'], 'L0_attn_conv_w': _L0_attn_in['conv_w'], 'L0_attn_W_z': _L0_attn_in['W_z'], 'L0_attn_W_b': _L0_attn_in['W_b'], 'L0_attn_W_a': _L0_attn_in['W_a'], 'L0_attn_dt_bias': _L0_attn_in['dt_bias'], 'L0_attn_A_log': _L0_attn_in['A_log'], 'L0_attn_norm_weight': _L0_attn_in['norm_weight'], 'L0_attn_W_out': _L0_attn_in['W_out'], 'L0_ffn_gate_w': _L0_ffn_in['gate_w'], 'L0_ffn_gate_b': _L0_ffn_in['gate_b'], 'L0_ffn_w1': _L0_ffn_in['w1'], 'L0_ffn_b1': _L0_ffn_in['b1'], 'L0_ffn_w3': _L0_ffn_in['w3'], 'L0_ffn_b3': _L0_ffn_in['b3'], 'L0_ffn_w2': _L0_ffn_in['w2'], 'L0_ffn_b2': _L0_ffn_in['b2'], 'L0_ffn_sw1': _L0_ffn_in['sw1'], 'L0_ffn_sb1': _L0_ffn_in['sb1'], 'L0_ffn_sw3': _L0_ffn_in['sw3'], 'L0_ffn_sb3': _L0_ffn_in['sb3'], 'L0_ffn_sw2': _L0_ffn_in['sw2'], 'L0_ffn_sb2': _L0_ffn_in['sb2'], 'L1_attn_ln1_g': _L1_attn_in['ln1_g'], 'L1_attn_ln1_b': _L1_attn_in['ln1_b'], 'L1_attn_ln2_g': _L1_attn_in['ln2_g'], 'L1_attn_ln2_b': _L1_attn_in['ln2_b'], 'L1_attn_Wqkv': _L1_attn_in['Wqkv'], 'L1_attn_Wo': _L1_attn_in['Wo'], 'L1_attn_W1': _L1_attn_in['W1'], 'L1_attn_b1': _L1_attn_in['b1'], 'L1_attn_W2': _L1_attn_in['W2'], 'L1_attn_b2': _L1_attn_in['b2'], 'L1_ffn_shared_up': _L1_ffn_in['shared_up'], 'L1_ffn_shared_down': _L1_ffn_in['shared_down'], 'L1_ffn_routed_up': _L1_ffn_in['routed_up'], 'L1_ffn_routed_down': _L1_ffn_in['routed_down'], 'L1_ffn_router_w': _L1_ffn_in['router_w']}
    _x0 = _d['L0_attn_hidden_states']
    _d['L0_attn_hidden_states'] = jax.random.normal(jax.random.fold_in(jax.random.key(seed), 1), (8, 256, 128), dtype=_x0.dtype)
    del _x0
    return _d

def reference(L0_attn_hidden_states, L0_attn_W_qkv, L0_attn_conv_w, L0_attn_W_z, L0_attn_W_b, L0_attn_W_a, L0_attn_dt_bias, L0_attn_A_log, L0_attn_norm_weight, L0_attn_W_out, L0_ffn_gate_w, L0_ffn_gate_b, L0_ffn_w1, L0_ffn_b1, L0_ffn_w3, L0_ffn_b3, L0_ffn_w2, L0_ffn_b2, L0_ffn_sw1, L0_ffn_sb1, L0_ffn_sw3, L0_ffn_sb3, L0_ffn_sw2, L0_ffn_sb2, L1_attn_ln1_g, L1_attn_ln1_b, L1_attn_ln2_g, L1_attn_ln2_b, L1_attn_Wqkv, L1_attn_Wo, L1_attn_W1, L1_attn_b1, L1_attn_W2, L1_attn_b2, L1_ffn_shared_up, L1_ffn_shared_down, L1_ffn_routed_up, L1_ffn_routed_down, L1_ffn_router_w):

    def _L0_attn_ref(hidden_states, W_qkv, conv_w, W_z, W_b, W_a, dt_bias, A_log, norm_weight, W_out):
        import jax, jax.numpy as jnp
        import numpy as np
        B, S, H = (2, 512, 128)
        NKH, NVH, DK, DV = (8, 16, 64, 64)
        KEY_DIM = NKH * DK
        VAL_DIM = NVH * DV
        CONV_DIM = 2 * KEY_DIM + VAL_DIM
        KSZ = 4
        EPS = 1e-06

        def _forward(hidden_states, W_qkv, conv_w, W_z, W_b, W_a, dt_bias, A_log, norm_weight, W_out):
            b, s, _ = hidden_states.shape
            mixed = hidden_states @ W_qkv.T
            x = mixed.transpose(0, 2, 1)
            y = jax.lax.conv_general_dilated(x, conv_w, (1,), [(KSZ - 1, 0)], dimension_numbers=('NCH', 'OIH', 'NCH'), feature_group_count=CONV_DIM)
            mixed = jax.nn.silu(y).transpose(0, 2, 1)
            z = (hidden_states @ W_z.T).reshape(b, s, NVH, DV)
            beta = jax.nn.sigmoid(hidden_states @ W_b.T)
            a = hidden_states @ W_a.T
            g = -jnp.exp(A_log) * jax.nn.softplus(a + dt_bias)
            q, k, v = jnp.split(mixed, [KEY_DIM, 2 * KEY_DIM], axis=-1)
            q = q.reshape(b, s, NKH, DK)
            k = k.reshape(b, s, NKH, DK)
            v = v.reshape(b, s, NVH, DV)
            rep = NVH // NKH
            if rep > 1:
                q = jnp.repeat(q, rep, axis=2)
                k = jnp.repeat(k, rep, axis=2)
            q = q * DK ** (-0.5)

            def step(Sst, inp):
                q_t, k_t, v_t, g_t, b_t = inp
                Sst = Sst * jnp.exp(g_t)[..., None, None]
                kv = jnp.einsum('bhkv,bhk->bhv', Sst, k_t)
                delta = (v_t - kv) * b_t[..., None]
                Sst = Sst + k_t[..., None] * delta[..., None, :]
                o = jnp.einsum('bhkv,bhk->bhv', Sst, q_t)
                return (Sst, o)
            S0 = jnp.zeros((b, NVH, DK, DV), jnp.float32)
            xs = (q.transpose(1, 0, 2, 3), k.transpose(1, 0, 2, 3), v.transpose(1, 0, 2, 3), g.transpose(1, 0, 2), beta.transpose(1, 0, 2))
            _, o = jax.lax.scan(step, S0, xs)
            o = o.transpose(1, 0, 2, 3)
            h_ = o * jax.nn.silu(z)
            var = jnp.mean(h_ * h_, axis=-1, keepdims=True)
            h_ = h_ * jax.lax.rsqrt(var + EPS) * norm_weight
            return h_.reshape(b, s, VAL_DIM) @ W_out.T
        return _forward(hidden_states, W_qkv, conv_w, W_z, W_b, W_a, dt_bias, A_log, norm_weight, W_out)

    def _L0_ffn_ref(x, gate_w, gate_b, w1, b1, w3, b3, w2, b2, sw1, sb1, sw3, sb3, sw2, sb2):
        import jax, jax.numpy as jnp
        import numpy as np
        from jax import lax
        D = 128
        H = 176
        E = 8
        K = 2
        ROUTER_SCALE = 1.0

        def _expert(x, w1, b1, w3, b3, w2, b2):
            h = jax.nn.silu((x @ w1 + b1) * (x @ w3 + b3))
            return h @ w2 + b2
        shape = x.shape
        xf = x.reshape(-1, D)
        T = xf.shape[0]
        scores = jax.nn.softmax(xf @ gate_w.T, axis=-1)
        biased = scores + gate_b
        _, idx = lax.top_k(biased, K)
        w = jnp.take_along_axis(scores, idx, axis=-1) * ROUTER_SCALE
        rw = jnp.zeros((T, E), dtype=xf.dtype).at[jnp.arange(T)[:, None], idx].add(w)
        h = jax.nn.silu((jnp.einsum('td,edh->teh', xf, w1) + b1) * (jnp.einsum('td,edh->teh', xf, w3) + b3))
        oe = jnp.einsum('teh,ehd->ted', h, w2) + b2
        y = jnp.einsum('te,ted->td', rw, oe)
        z = _expert(xf, sw1, sb1, sw3, sb3, sw2, sb2)
        return (y + z).reshape(shape)

    def _L1_attn_ref(x, ln1_g, ln1_b, ln2_g, ln2_b, Wqkv, Wo, W1, b1, W2, b2):
        import math
        import jax, jax.numpy as jnp
        import numpy as np
        D_MODEL = 128
        N_HEADS = 16
        D_HEAD = D_MODEL // N_HEADS
        SEQ = 512
        BATCH = 1
        BASE = 10000.0
        EPS = 1e-05

        def _layernorm(x, g, b):
            mu = jnp.mean(x, axis=-1, keepdims=True)
            var = jnp.mean(jnp.square(x - mu), axis=-1, keepdims=True)
            return (x - mu) * jax.lax.rsqrt(var + EPS) * g + b

        def _rotate(x, cos, sin):
            b, H, n, dh = x.shape
            xr = x.reshape(b, H, n, dh // 2, 2)
            x1, x2 = (xr[..., 0], xr[..., 1])
            r1 = x1 * cos - x2 * sin
            r2 = x1 * sin + x2 * cos
            return jnp.stack([r1, r2], axis=-1).reshape(b, H, n, dh)

        def _block(x, ln1_g, ln1_b, ln2_g, ln2_b, Wqkv, Wo, W1, b1, W2, b2):
            b, n, d = x.shape
            H, dh = (N_HEADS, D_HEAD)
            h = _layernorm(x, ln1_g, ln1_b)
            qkv = (h @ Wqkv).reshape(b, n, 3, H, dh)
            q = jnp.transpose(qkv[:, :, 0], (0, 2, 1, 3))
            k = jnp.transpose(qkv[:, :, 1], (0, 2, 1, 3))
            v = jnp.transpose(qkv[:, :, 2], (0, 2, 1, 3))
            inv_freq = BASE ** (-(jnp.arange(0, dh, 2, dtype=jnp.float32) / dh))
            theta = jnp.arange(n, dtype=jnp.float32)[:, None] * inv_freq[None, :]
            cos, sin = (jnp.cos(theta), jnp.sin(theta))
            q = _rotate(q, cos, sin)
            k = _rotate(k, cos, sin)
            s = jnp.einsum('bhqd,bhkd->bhqk', q, k) / math.sqrt(dh)
            causal = jnp.tril(jnp.ones((n, n), dtype=bool))
            s = jnp.where(causal, s, -jnp.inf)
            a = jax.nn.softmax(s, axis=-1)
            o = jnp.einsum('bhqk,bhkd->bqhd', a, v).reshape(b, n, d)
            x = x + o @ Wo
            h2 = _layernorm(x, ln2_g, ln2_b)
            f = jax.nn.gelu(h2 @ W1 + b1, approximate=False) @ W2 + b2
            return x + f
        return _block(x, ln1_g, ln1_b, ln2_g, ln2_b, Wqkv, Wo, W1, b1, W2, b2)

    def _L1_ffn_ref(x, shared_up, shared_down, routed_up, routed_down, router_w):
        import jax, jax.numpy as jnp
        import numpy as np
        H, F, E_SHARED, E_ROUTED, K = (128, 512, 1, 8, 2)

        def _expert(x, w_up, w_down):
            h = jax.nn.gelu(jnp.einsum('bsh,hf->bsf', x, w_up), approximate=False)
            return jnp.einsum('bsf,fh->bsh', h, w_down)
        shared_out = jnp.zeros_like(x)
        for i in range(E_SHARED):
            shared_out = shared_out + _expert(x, shared_up[i], shared_down[i])
        probs = jax.nn.softmax(jnp.einsum('bsh,he->bse', x, router_w), axis=-1)
        top_k_prob, top_k_idx = jax.lax.top_k(probs, K)
        onehot = jax.nn.one_hot(top_k_idx, E_ROUTED, dtype=x.dtype)
        gates = jnp.einsum('bsk,bske->bse', top_k_prob, onehot)
        routed_out = jnp.zeros_like(x)
        for e in range(E_ROUTED):
            y = _expert(x, routed_up[e], routed_down[e])
            routed_out = routed_out + gates[..., e:e + 1] * y
        return shared_out + routed_out + x
    x = L0_attn_hidden_states
    x = x + _L0_attn_ref(_layernorm(x, axis=-1), L0_attn_W_qkv, L0_attn_conv_w, L0_attn_W_z, L0_attn_W_b, L0_attn_W_a, L0_attn_dt_bias, L0_attn_A_log, L0_attn_norm_weight, L0_attn_W_out)
    x = x + _L0_ffn_ref(_layernorm(x, axis=-1), L0_ffn_gate_w, L0_ffn_gate_b, L0_ffn_w1, L0_ffn_b1, L0_ffn_w3, L0_ffn_b3, L0_ffn_w2, L0_ffn_b2, L0_ffn_sw1, L0_ffn_sb1, L0_ffn_sw3, L0_ffn_sb3, L0_ffn_sw2, L0_ffn_sb2)
    x = x + _L1_attn_ref(_layernorm(x, axis=-1), L1_attn_ln1_g, L1_attn_ln1_b, L1_attn_ln2_g, L1_attn_ln2_b, L1_attn_Wqkv, L1_attn_Wo, L1_attn_W1, L1_attn_b1, L1_attn_W2, L1_attn_b2)
    x = x + _L1_ffn_ref(_layernorm(x, axis=-1), L1_ffn_shared_up, L1_ffn_shared_down, L1_ffn_routed_up, L1_ffn_routed_down, L1_ffn_router_w)
    return x

_drawn_inputs = setup_inputs


def setup_inputs(seed=0):
    import zlib

    import numpy as np

    out = dict(_drawn_inputs(seed))
    spreads = {'L0_attn_dt_bias': (1.0, 0.6),
     'L0_attn_norm_weight': (1.0, 0.6),
     'L1_attn_ln1_g': (1.0, 0.6),
     'L1_attn_ln1_b': (0.0, 0.8),
     'L1_attn_ln2_g': (1.0, 0.6),
     'L1_attn_ln2_b': (0.0, 2.0),
     'L1_attn_b1': (0.0, 2.0),
     'L1_attn_b2': (0.0, 0.667)}
    factors = {'L0_attn_W_qkv': 8.0,
     'L0_attn_conv_w': 8.0,
     'L0_attn_W_z': 8.0,
     'L0_attn_W_b': 32.6,
     'L0_attn_W_a': 26.68,
     'L0_attn_A_log': 45.146,
     'L0_attn_W_out': 8.0,
     'L0_ffn_gate_w': 8.0,
     'L0_ffn_gate_b': 8.0,
     'L0_ffn_w1': 8.0,
     'L0_ffn_b1': 8.0,
     'L0_ffn_w3': 8.0,
     'L0_ffn_b3': 8.0,
     'L0_ffn_w2': 8.0,
     'L0_ffn_b2': 25.085,
     'L0_ffn_sw1': 8.0,
     'L0_ffn_sb1': 8.0,
     'L0_ffn_sw3': 8.0,
     'L0_ffn_sb3': 8.0,
     'L0_ffn_sw2': 8.0,
     'L0_ffn_sb2': 14.772,
     'L1_attn_Wqkv': 8.0,
     'L1_attn_Wo': 8.0,
     'L1_ffn_shared_up': 3.211,
     'L1_ffn_shared_down': 3.142,
     'L1_ffn_routed_up': 8.0,
     'L1_ffn_routed_down': 8.0,
     'L1_ffn_router_w': 8.0,
     'L1_attn_W1': 4.607,
     'L1_attn_W2': 2.769}
    for name, (base, spread) in spreads.items():
        noise = np.random.default_rng([zlib.crc32(name.encode()), seed]).standard_normal(out[name].shape)
        drawn = base * np.exp(spread * noise) if base else spread * noise
        out[name] = jnp.asarray(drawn.astype(out[name].dtype))
    for name, factor in factors.items():
        out[name] = (out[name] * factor).astype(out[name].dtype)
    return out
```

```python
from contextlib import ExitStack

import numpy as np
import concourse.bass as bass
from concourse import mybir

F32 = mybir.dt.float32
BF16 = mybir.dt.bfloat16
ALU = mybir.AluOpType
ACT = mybir.ActivationFunctionType
X_AXIS = mybir.AxisListType.X
XY_AXIS = mybir.AxisListType.XY

P = 128
SEQS, SEQ = 8, 256
CH = SEQ // P
KH, VH, DH = 8, 16, 64
QK_TILES, V_TILES = 4, 8
MIX = 2 * QK_TILES + V_TILES
TAPS = 4
BATCH = 4
NB = VH // BATCH
LEVELS = [2, 4, 8, 16, 32, 64]
NL = len(LEVELS)
E = 8
H1, H1R = 176, 48
UP0 = 14
AH, AD, AP = 16, 8, 32
AG = 4
HT1 = 4
NEG = -1e30

C_ID, C_ID0, C_NM1 = 0, 128, 256
C_LM = 384
C_COS = C_LM + 64 * NL
C_SIN = C_COS + CH * 2 * AD
C_CAUSAL = C_SIN + CH * 2 * AD
C_RESET = C_CAUSAL + 128
C_END = C_RESET + CH * E

ATANH = [1.0 / k for k in (15, 13, 11, 9, 7, 5, 3)]

A_MOST = 80.0

DVE_STEPS = 173
POOL_STEPS = 9


def constants():
    c = np.zeros((P, C_END), np.float32)
    i = np.arange(P)
    c[:, C_ID:C_ID + P] = np.eye(P)
    c[:, C_ID0:C_ID0 + P] = np.eye(P)
    c[0, C_ID0] = 0
    c[i[0::2], C_NM1 + i[1::2]] = -1
    for l, n in enumerate(LEVELS):
        even = i[(i // n) % 2 == 0]
        row = i[:, None] // n
        c[:, C_LM + 64 * l:C_LM + 64 * (l + 1)] = -((row % 2 == 1) & (even[None, :] // n == row - 1)).astype(np.float32)
    inv_freq = np.float32(10000.0) ** (-(np.arange(0, AD, 2, dtype=np.float32) / np.float32(AD)))
    theta = np.arange(SEQ, dtype=np.float32)[:, None] * inv_freq[None, :].astype(np.float32)
    cos, sin = np.repeat(np.cos(theta), 2, 1), np.repeat(np.sin(theta), 2, 1)
    sin[:, 0::2] *= -1
    for j in range(CH):
        for q, scale in enumerate((AD ** -0.5, 1.0)):
            at = (j * 2 + q) * AD
            c[:, C_COS + at:C_COS + at + AD] = cos[j * P:(j + 1) * P] * scale
            c[:, C_SIN + at:C_SIN + at + AD] = sin[j * P:(j + 1) * P] * scale
    c[:, C_CAUSAL:C_CAUSAL + P] = np.where(i[None, :] > i[:, None], NEG, 0)
    c[:, C_RESET:] = 1
    c[:, C_RESET:C_END:E] = 0
    return c


class Steps:

    def __init__(self, engine, sem, seq, per_seq):
        self.engine, self.sem, self.seq, self.per_seq, self.n = engine, sem, seq, per_seq, 0

    def did(self, instruction):
        self.n += 1
        instruction.then_inc(self.sem, 1)

    def settle(self, but=0):
        if self.n > but:
            self.engine.wait_ge(self.sem, self.seq * self.per_seq + self.n - but)


def program(nc, t, out, stages=4):
    n_ln, n_ht, n_rt = ((1, 1, 0), (2, 2, 1), (5, 4, 1), (6, 5, 2))[stages - 1]
    n_up, n_down = ((0, 0), (0, 0), (4, 1), (40, 10))[stages - 1]
    with ExitStack() as ctx:
        def sb(name, shape, dt=F32):
            return ctx.enter_context(nc.sbuf_tensor(name, shape, dt))

        def sem(name):
            return ctx.enter_context(nc.semaphore(name))

        con = sb("con", [P, C_END])
        ident, ident0, nm1 = con[:, C_ID:C_ID + P], con[:, C_ID0:C_ID0 + P], con[:, C_NM1:C_NM1 + P]
        ident_bf = sb("ident_bf", [P, P], BF16)
        causal_bf = sb("causal_bf", [P, AG, P], BF16)
        reset = con[:, C_RESET:C_END]
        half_power = sb("half_power", [P, VH * CH])

        w_mix = sb("w_mix", [P, MIX * P])
        w_z = sb("w_z", [P, VH * DH])
        w_ba = sb("w_ba", [P, 2 * VH])
        conv_w = sb("conv_w", [P, MIX, TAPS])
        dt_bias = sb("dt_bias", [P, VH])
        a_log = sb("a_log", [P, VH])
        exp_a = sb("exp_a", [P, 2, VH])
        w_out = sb("w_out", [P, V_TILES, P])
        norm_w = sb("norm_w", [P, 1])

        gate_w = sb("gate_w", [P, E])
        gate_b = sb("gate_b", [P, E])
        w1 = sb("w1", [P, UP0 * P])
        w3 = sb("w3", [P, UP0 * P])
        b1 = sb("b1", [P, UP0])
        b3 = sb("b3", [P, UP0])
        w2 = sb("w2", [P, E + 1, P])
        w2r = sb("w2r", [P, E // 2 + 1, P])
        b2 = sb("b2", [E + 1, P])

        ln_gb = sb("ln_gb", [P, 4])
        a_wqkv = sb("a_wqkv", [P, 3 * P])
        a_wo = sb("a_wo", [P, P])
        a_w1 = sb("a_w1", [P, HT1 * P])
        a_b1 = sb("a_b1", [P, HT1])
        a_w2 = sb("a_w2", [P, HT1, P])
        a_b2 = sb("a_b2", [P, P])

        m_up = sb("m_up", [P, E + 1, HT1 * P])
        m_down = sb("m_down", [P, E + 1, HT1, P])
        m_rt = sb("m_rt", [P, E])

        x_in = sb("x_in", [P, CH, P])
        x_res = sb("x_res", [P, CH, P])
        h_tok = sb("h_tok", [P, CH, P])
        h0 = sb("h0", [P, CH, P])
        hT = sb("hT", [P, SEQ])
        stats = sb("stats", [P, CH, 6])
        mv = sb("mv", [P, CH, 2])
        var_eps = sb("var_eps", [P, CH])
        rstd = sb("rstd", [P, CH])

        mix = sb("mix", [P, MIX, SEQ])
        z_silu = sb("z_silu", [P, CH, VH * DH])
        exp_in = sb("exp_in", [P, CH, 2 * VH])
        exp_out = sb("exp_out", [P, CH, 2 * VH])
        pre = sb("pre", [P, CH, VH])
        sp_s = sb("sp_s", [P, CH, VH])
        sp_z = sb("sp_z", [P, CH, VH])
        sp_p = sb("sp_p", [P, CH, VH])
        beta = sb("beta", [P, CH, VH])
        decay = sb("decay", [P, CH, VH])
        log_decay = sb("log_decay", [P, CH, VH])
        decT = sb("decT", [VH, P])
        gamT = sb("gamT", [P, P])
        pad = sb("pad", [P, 1])
        zerosT = sb("zerosT", [VH, P])
        gam = sb("gam", [P, VH])
        dmat_all = sb("dmat_all", [P, NB, BATCH, P])
        at_all = sb("at_all", [P, NB, BATCH, P])
        pt_all = sb("pt_all", [P, NB, BATCH, P])
        um_all = sb("um_all", [P, NB, BATCH, P])
        dmat = [dmat_all[:, b, :, :] for b in range(NB)]
        at = [at_all[:, b, :, :] for b in range(NB)]
        pt = [pt_all[:, b, :, :] for b in range(NB)]
        um = [um_all[:, b, :, :] for b in range(NB)]
        tm = [sb(f"tm{b}", [P, BATCH, P // 2]) for b in range(NB)]
        xm = [[sb(f"xm{l}_{b}", [P, BATCH, P]) for b in range(2)] for l in range(NL)]
        k_tok = sb("k_tok", [P, QK_TILES, P])
        v_tok = sb("v_tok", [P, CH, VH, DH])
        eps = sb("eps", [P, VH, DH])
        w_eps = sb("w_eps", [P, VH, DH])
        state = sb("state", [P, QK_TILES, P])
        kstate = w_eps
        qstate = sb("qstate", [P, VH, DH])
        hz = z_silu[:, :, :].rearrange("p c (h d) -> p c h d", d=DH)
        hsq = at_all[:, 0:2, :, :].rearrange("p a h n -> p (a h n)").rearrange("p (h d) -> p h d", d=DH)
        ssq = sb("ssq", [P, VH])
        o_rstd = sb("o_rstd", [P, VH])
        hzT = w_eps[:, :, :].rearrange("p (m a) d -> p m (a d)", a=2)

        logit = sb("logit", [P, CH, E])
        rmax = sb("rmax", [P, CH])
        rexp = sb("rexp", [P, CH, E])
        rsum = sb("rsum", [P, CH])
        score = sb("score", [P, CH, E])
        biased = sb("biased", [P, CH, E])
        top = sb("top", [P, CH, 8])
        over2 = sb("over2", [P, CH, E])
        is2 = sb("is2", [P, CH, E])
        rank = sb("rank", [P, CH, E])
        room = sb("room", [P, CH])
        rw = sb("rw", [P, CH, E + 1])
        rwT = sb("rwT", [E + 1, SEQ])
        gate3 = [eps[:, 4 * j:4 * (j + 1), :].rearrange("p a d -> p (a d)") for j in range(4)]
        prod = [qstate[:, 8 * j:8 * (j + 1), :].rearrange("p (i a) d -> p i (a d)", i=2) for j in range(2)]
        hid0 = mix[:, 0:UP0, :]
        hid1 = [dmat_all[:, 2 * j:2 * j + 2, :, :].rearrange("p a h n -> p (a h n)")
                .rearrange("p (i n) -> p i n", i=HT1) for j in range(2)]

        qk_tok = mix[:, 0:8, :].rearrange("p m n -> p (m n)")\
            .rearrange("p (c q h d) -> p c q h d", c=CH, q=2, d=AP)
        rot, rot2 = (state[:, 2 * j:2 * j + 2, :].rearrange("p q (h d) -> p q h d", d=AD) for j in range(2))
        v_aug = sb("v_aug", [P, CH, AH, AD + 1])
        qT = v_tok[:, 0, :, :].rearrange("p (g a) d -> p g (a d)", g=AG)
        kT = v_tok[:, 1, :, :].rearrange("p (g a) d -> p g (a d)", g=AG)
        smax = sb("smax", [P, 2, AG])
        shifted = [at_all[:, 2 * j:2 * j + 2, :, :] for j in range(2)]
        probs = [pt_all[:, 2 * j:2 * j + 2, :, :] for j in range(2)]
        probsT = [um_all[:, 2 * j:2 * j + 2, :, :] for j in range(2)]
        a_den = sb("a_den", [P, CH, AH])
        a_out = k_tok[:, 0:2, :].rearrange("p c (h d) -> p c h d", d=AD)
        a_outT = k_tok[:, 2:4, :].rearrange("p c n -> p (c n)")
        xp = sb("xp", [P, CH, P])

        ps = ctx.enter_context(nc.psum_tensor("ps", [P, 8, 512], F32))

        names = """consts_in w_a_in w_b_in w_c_in w_d_in small_in x_loaded x_stored
            setup_pool setup_dve setup_act alog_split a_shifted norm_scaled
            dve_step pool_step act_step
            ln_var ln_rstd h_ready hT_psum hT_ready
            ba_psum exp_in_ready exp_done logdec_ready decay_ready decay_tok beta_ready
            mix_psum seeded conv_done silu_done z_psum z_done
            decT_psum decT_ready gamT_ready gam_psum gam_ready
            ktok_psum ktok_ready vtok_psum vtok_ready
            diag_ready arow_psum scan_done kk_psum at_ready u_first
            t_psum t_ready x_psum x_ready u_psum u_ready
            e_psum e_ready we_ready o_psum hz_ready s_psum s_ready ks_psum ks_done qs_psum qs_done r_ready
            hz_sq ssq_ready o_var o_rstd_ready hn_ready hzT_psum hzT_ready y_psum x_updated
            lg_psum shift_ready rexp_done rw_ready rwT_psum rwT_ready
            up_psum gate_done prod_ready hid_ready down_psum mixed_in
            qkv_psum rot_ready vaug_ready qkT_psum qT_ready kT_ready
            s_scores shifted_ready probs_ready pT_psum pT_ready av_psum aout_ready aoT_psum aoT_ready
            wo_psum xp_ready h_pool
            mup_psum mgelu mdown_psum mlp_added mdown_used x_final""".split()
        s = {n: sem(n) for n in names}

        block = ctx.enter_context(nc.Block())

        def even_odd(ap, n, odd):
            return ap.rearrange("p h (b r n) -> p h b r n", r=2, n=n)[:, :, :, odd, :]

        def even_odd1(ap, n, odd):
            return ap.rearrange("p (b r n) -> p b r n", r=2, n=n)[:, :, odd, :]

        def blocks(ap, n):
            return ap.rearrange("p (h b n) -> p h b n", h=BATCH, n=n)

        def over_heads(ap, n):
            return ap.unsqueeze(1).to_broadcast([ap.shape[0], n, ap.shape[1]])

        def over_last(ap, n):
            return ap.unsqueeze(2).to_broadcast([ap.shape[0], ap.shape[1], n])

        def over_last3(ap, n):
            return ap.unsqueeze(3).to_broadcast([ap.shape[0], ap.shape[1], ap.shape[2], n])

        def tokens(dram, seq):
            return dram[bass.ds(seq, 1), :, :].rearrange("a (c p) d -> p (a c) d", p=P)

        def khead(k):
            return k % QK_TILES, DH * (k // QK_TILES)

        @block.sync
        def _(sp):
            sp.dma_start(con[:, :], t["consts"]).then_inc(s["consts_in"], 16)
            sp.dma_start(w_ba[:, :], t["w_ba"]).then_inc(s["w_a_in"], 16)
            sp.dma_start(w_mix[:, :], t["w_mix"]).then_inc(s["w_a_in"], 16)
            sp.dma_start(w_z[:, :], t["w_z"]).then_inc(s["w_a_in"], 16)
            sp.dma_start(w_out[:, :, :], t["w_out"]).then_inc(s["w_a_in"], 16)
            sp.dma_start(x_in[:, :, :], tokens(t["x"], 0)).then_inc(s["x_loaded"], 16)
            with sp.Fori(0, SEQS - 1) as it:
                sp.wait_ge(s["x_updated"], CH * it + CH)
                sp.dma_start(x_in[:, :, :], tokens(t["x"], it + 1)).then_inc(s["x_loaded"], 16)
                sp.wait_ge(s["x_final"], it + 1)
                sp.dma_start(tokens(out, it), x_res[:, :, :]).then_inc(s["x_stored"], 16)
            sp.wait_ge(s["x_final"], SEQS)
            sp.dma_start(tokens(out, SEQS - 1), x_res[:, :, :]).then_inc(s["x_stored"], 16)
            sp.wait_ge(s["x_stored"], 16 * SEQS + 1)
            if stages < 4:
                sp.wait_ge(s["w_c_in"], 144)
                sp.wait_ge(s["w_b_in"], 144)
                sp.wait_ge(s["w_d_in"], 80)

        @block.gpsimd
        def _(pool):
            for dst, name in ((w1[:, :], "w1"), (w3[:, :], "w3"), (b1[:, :], "b1"), (b3[:, :], "b3"),
                              (w2[:, :, :], "w2"), (w2r[:, :, :], "w2r"), (b2[:, :], "b2"), (gate_w[:, :], "gate_w")):
                pool.dma_start(dst, t[name]).then_inc(s["w_b_in"], 16)
            pool.dma_start(gate_b[:, :], t["gate_b"].partition_broadcast(P)).then_inc(s["w_b_in"], 16)
            pool.memset(half_power[:, :], -0.5)
            pool.memset(x_res[:, :, :], 0.0).then_inc(s["x_stored"], 1)
            pool.memset(v_aug[:, :, :, AD:AD + 1], 1.0)
            pool.memset(rw[:, :, E:E + 1], 1.0)
            pool.memset(gamT[:, :], 0.0)
            pool.memset(zerosT[:, :], 0.0).then_inc(s["setup_pool"], 1)
            for l in range(NL):
                for b in range(2):
                    pool.memset(xm[l][b][:, :, :], 0.0).then_inc(s["setup_pool"], 1)
            pool.wait_ge(s["w_a_in"], 64)
            pool.wait_ge(s["small_in"], 16 * 6)
            pool.tensor_scalar(w_out[:, :, :], w_out[:, :, :], norm_w[:, 0:1], None, ALU.mult)\
                .then_inc(s["norm_scaled"], 1)
            pool.wait_ge(s["consts_in"], 16)

            with pool.Fori(0, SEQS) as it:
                me = Steps(pool, s["pool_step"], it, POOL_STEPS)

                def inverse_root(k):
                    pool.wait_ge(s["ln_var"], it * n_ln + k + 1)
                    pool.tensor_tensor(rstd[:, :], var_eps[:, :], half_power[:, 0:CH], ALU.pow)\
                        .then_inc(s["ln_rstd"], 1)

                inverse_root(0)
                for c in range(CH):
                    for b in range(NB):
                        if c == 0 and b == 0:
                            pool.wait_ge(s["beta_ready"], it + 1)
                        if c == 1:
                            pool.wait_ge(s["e_ready"], it * CH * NB + b + 1)
                            hs = slice(BATCH * b, BATCH * (b + 1))
                            pool.tensor_tensor(w_eps[:, hs, :], eps[:, hs, :],
                                               dmat[b][:, :, P - 1:P].to_broadcast([P, BATCH, DH]), ALU.mult)\
                                .then_inc(s["we_ready"], 1)
                            pool.wait_ge(s["we_ready"], it * NB + b + 1)
                        pool.tensor_tensor(dmat[b], over_heads(ident, BATCH),
                                           over_last(beta[:, c, BATCH * b:BATCH * (b + 1)], P), ALU.mult)\
                            .then_inc(s["diag_ready"], 1)
                    for b in range(NB):
                        pool.wait_ge(s["at_ready"], it * CH * NB + NB * c + b + 1)
                        me.did(pool.tensor_tensor(um[b], at[b], over_heads(nm1, BATCH), ALU.mult))
                        me.settle()
                        pool.tensor_tensor(um[b], um[b], over_heads(ident, BATCH), ALU.add)\
                            .then_inc(s["u_first"], 1)
                for c in range(CH):
                    pool.wait_ge(s["o_var"], it * CH + c + 1)
                    pool.tensor_tensor(o_rstd[:, :], ssq[:, :], half_power[:, 0:VH], ALU.pow)\
                        .then_inc(s["o_rstd_ready"], 1)
                if stages >= 2:
                    inverse_root(1)
                if stages >= 3:
                    inverse_root(2)
                    inverse_root(3)
                    inverse_root(4)
                    pool.wait_ge(s["xp_ready"], it + 1)
                    me.did(pool.tensor_tensor(x_res[:, :, :], x_res[:, :, :], xp[:, :, :], ALU.add))
                    me.settle()
                    pool.tensor_tensor(x_res[:, :, :], x_res[:, :, :], over_heads(a_b2[:, :], CH), ALU.add)\
                        .then_inc(s["h_pool"], 1)
                if stages >= 4:
                    inverse_root(5)
                    pool.wait_ge(s["h_ready"], it * n_ln + 6)
                    pool.tensor_tensor(x_res[:, :, :], x_res[:, :, :], h_tok[:, :, :], ALU.add)\
                        .then_inc(s["h_pool"], 1)
                if stages >= 2:
                    pass
            assert me.n == POOL_STEPS, ("POOL_STEPS", me.n)

        @block.scalar
        def _(act):
            act.dma_start(conv_w[:, :, :], t["conv_w"]).then_inc(s["small_in"], 16)
            act.dma_start(dt_bias[:, :], t["dt_bias"].partition_broadcast(P)).then_inc(s["small_in"], 16)
            act.dma_start(a_log[:, :], t["A_log"].partition_broadcast(P)).then_inc(s["small_in"], 16)
            for j in range(2):
                act.dma_start(norm_w[DH * j:DH * (j + 1), :], t["norm_weight"].rearrange("(d a) -> d a", a=1))\
                    .then_inc(s["small_in"], 16)
            act.dma_start(a_b1[:, :], t["a_b1"]).then_inc(s["small_in"], 16)
            for j, name in enumerate(("ln1_g", "ln1_b", "ln2_g", "ln2_b")):
                act.dma_start(ln_gb[:, j:j + 1], t[name].rearrange("(d a) -> d a", a=1)).then_inc(s["w_c_in"], 16)
            act.dma_start(a_wqkv[:, :], t["a_wqkv"]).then_inc(s["w_c_in"], 16)
            act.dma_start(a_wo[:, :], t["a_wo"]).then_inc(s["w_c_in"], 16)
            act.dma_start(a_w1[:, :], t["a_w1"]).then_inc(s["w_c_in"], 16)
            act.dma_start(a_w2[:, :, :], t["a_w2"]).then_inc(s["w_c_in"], 16)
            act.dma_start(a_b2[:, :], t["a_b2"].partition_broadcast(P)).then_inc(s["w_c_in"], 16)
            act.dma_start(m_up[:, 0, :], t["shared_up"][0, :, :]).then_inc(s["w_d_in"], 16)
            act.dma_start(m_up[:, 1:E + 1, :], t["routed_up"]).then_inc(s["w_d_in"], 16)
            act.dma_start(m_down[:, 0, :, :], t["shared_down"]).then_inc(s["w_d_in"], 16)
            act.dma_start(m_down[:, 1:E + 1, :, :], t["routed_down"]).then_inc(s["w_d_in"], 16)
            act.dma_start(m_rt[:, :], t["router_w"]).then_inc(s["w_d_in"], 16)
            act.wait_ge(s["small_in"], 16 * 6)
            act.wait_ge(s["alog_split"], 2)
            act.activation(exp_a[:, :, :], exp_a[:, :, :], ACT.Exp).then_inc(s["setup_act"], 1)

            with act.Fori(0, SEQS) as it:
                def transpose_out(k, gb=None):
                    act.wait_ge(s["hT_psum"], it * n_ht + k + 1)
                    src = ps[:, 7, 0:SEQ]
                    if gb is None:
                        act.activation(hT[:, :], src, ACT.Copy).then_inc(s["hT_ready"], 1)
                    else:
                        act.wait_ge(s["w_c_in"], 16 * 9)
                        act.activation(hT[:, :], src, ACT.Identity, bias=ln_gb[:, 2 * gb + 1:2 * gb + 2],
                                       scale=ln_gb[:, 2 * gb:2 * gb + 1]).then_inc(s["hT_ready"], 1)

                transpose_out(0)
                act.wait_ge(s["exp_in_ready"], it + 1)
                act.activation(exp_out[:, :, :], exp_in[:, :, :], ACT.Exp).then_inc(s["exp_done"], 1)

                def seed(p):
                    act.wait_ge(s["mix_psum"], it * MIX // 2 + p + 1)
                    for j in range(2):
                        m = 2 * p + j
                        act.activation(mix[:, m, :], ps[:, p % 4, j * SEQ:(j + 1) * SEQ], ACT.Copy,
                                       scale=conv_w[:, m, TAPS - 1:TAPS]).then_inc(s["seeded"], 1)

                for p in range(4):
                    seed(p)
                act.wait_ge(s["logdec_ready"], it + 1)
                act.activation(decay[:, :, :], log_decay[:, :, :], ACT.Exp).then_inc(s["decay_ready"], 1)
                for p in range(MIX // 2):
                    act.wait_ge(s["conv_done"], it * MIX // 2 + p + 1)
                    act.activation(mix[:, 2 * p:2 * p + 2, :], mix[:, 2 * p:2 * p + 2, :], ACT.Silu)\
                        .then_inc(s["silu_done"], 1)
                    if p < 4:
                        seed(p + 4)
                for q in range(2 * CH):
                    act.wait_ge(s["z_psum"], it * 2 * CH + q + 1)
                    act.activation(z_silu[:, q // 2, 512 * (q % 2):512 * (q % 2 + 1)], ps[:, 4 + q % 2, :], ACT.Silu)\
                        .then_inc(s["z_done"], 1)
                act.wait_ge(s["ktok_psum"], it + 1)
                act.activation(k_tok[:, :, :], ps[:, 7, :].rearrange("p (a b) -> p a b", b=P), ACT.Copy)\
                    .then_inc(s["ktok_ready"], 1)
                for c in range(CH):
                    act.wait_ge(s["vtok_psum"], it * CH + c + 1)
                    for j in range(2):
                        act.activation(v_tok[:, c, 8 * j:8 * (j + 1), :],
                                       ps[:, 4 + j, :].rearrange("p (a b) -> p a b", b=DH), ACT.Copy)\
                            .then_inc(s["vtok_ready"], 1)

                for c in range(CH):
                    for l in range(NL):
                        for b in range(NB):
                            act.wait_ge(s["t_psum"], ((it * CH + c) * NL + l) * NB + b + 1)
                            n = LEVELS[l]
                            act.activation(tm[b][:, :, :].rearrange("p h (b n) -> p h b n", n=n),
                                           even_odd(ps[:, b, :].rearrange("p (h m) -> p h m", h=BATCH), n, 0),
                                           ACT.Copy).then_inc(s["t_ready"], 1)
                    for b in range(NB):
                        act.wait_ge(s["e_psum"], it * CH * NB + NB * c + b + 1)
                        act.activation(eps[:, BATCH * b:BATCH * (b + 1), :],
                                       ps[:, b, 0:BATCH * DH].rearrange("p (a b) -> p a b", b=DH), ACT.Copy)\
                            .then_inc(s["e_ready"], 1)
                    if c == 0:
                        act.wait_ge(s["s_psum"], it + 1)
                        act.activation(state[:, :, :], ps[:, 6, :].rearrange("p (a b) -> p a b", b=P), ACT.Copy)\
                            .then_inc(s["s_ready"], 1)
                for c in range(CH):
                    act.wait_ge(s["hz_ready"], it * CH + c + 1)
                    act.activation(hsq[:, :, :], hz[:, c, :, :], ACT.Square).then_inc(s["hz_sq"], 1)
                    act.wait_ge(s["hzT_psum"], it * CH + c + 1)
                    for j in range(2):
                        act.activation(hzT[:, 4 * j:4 * (j + 1), :],
                                       ps[:, 6 + j, :].rearrange("p (a b) -> p a b", b=P), ACT.Copy)\
                            .then_inc(s["hzT_ready"], 1)

                def router(k):
                    act.wait_ge(s["shift_ready"], it * n_rt + k + 1)
                    act.activation(rexp[:, :, :], logit[:, :, :], ACT.Exp).then_inc(s["rexp_done"], 1)

                if stages >= 2:
                    transpose_out(1)
                    router(0)
                    act.wait_ge(s["w_b_in"], 16 * 9)
                    for i in range(UP0):
                        act.wait_ge(s["up_psum"], it * UP0 + i + 1)
                        act.activation(gate3[i % 4], ps[:, i % 4, SEQ:2 * SEQ], ACT.Identity,
                                       bias=b3[:, i:i + 1]).then_inc(s["gate_done"], 1)
                        if i % 2 == 1:
                            act.wait_ge(s["prod_ready"], it * UP0 + i + 1)
                            act.activation(hid0[:, i - 1:i + 1, :], prod[(i // 2) % 2], ACT.Silu)\
                                .then_inc(s["hid_ready"], 1)
                if stages >= 3:
                    transpose_out(2, gb=0)
                    for c in range(CH):
                        act.wait_ge(s["qkv_psum"], it * CH + c + 1)
                        act.activation(v_aug[:, c, :, 0:AD],
                                       ps[:, c, 2 * P:3 * P].rearrange("p (h d) -> p h d", d=AD), ACT.Copy)\
                            .then_inc(s["vaug_ready"], 1)
                    for c in range(CH):
                        act.wait_ge(s["qkT_psum"], it * CH + c + 1)
                        for q, dst in enumerate((qT, kT)):
                            act.activation(dst[:, :, c * P:(c + 1) * P],
                                           ps[:, 4 + 2 * c + q, :].rearrange("p (g n) -> p g n", n=P), ACT.Copy)\
                                .then_inc(s["qT_ready"], 1)

                    def probabilities(u):
                        c = u // AG
                        act.wait_ge(s["shifted_ready"], it * 2 * AG + u + 1)
                        act.activation(probs[u % 2][:, 0:c + 1, :, :], shifted[u % 2][:, 0:c + 1, :, :], ACT.Exp)\
                            .then_inc(s["probs_ready"], 1)

                    def turned(u):
                        c = u // AG
                        act.wait_ge(s["pT_psum"], it * 2 * AG + u + 1)
                        act.activation(probsT[u % 2][:, 0:c + 1, :, :],
                                       ps[:, 4:5 + c, :].rearrange("p k (g n) -> p k g n", n=P), ACT.Copy)\
                            .then_inc(s["pT_ready"], 1)

                    for u in range(2 * AG):
                        probabilities(u)
                        if u >= 1:
                            turned(u - 1)
                    turned(2 * AG - 1)
                    act.wait_ge(s["aoT_psum"], it + 1)
                    act.activation(a_outT, ps[:, 7, 0:SEQ], ACT.Copy).then_inc(s["aoT_ready"], 1)
                    transpose_out(3, gb=1)
                    for i in range(HT1):
                        act.wait_ge(s["mup_psum"], it * n_up + i + 1)
                        act.activation(hid1[0][:, i, :], ps[:, i, 0:SEQ], ACT.Gelu,
                                       bias=a_b1[:, i:i + 1]).then_inc(s["mgelu"], 1)
                if stages >= 4:
                    transpose_out(4)
                    router(1)
                    for e in range(E + 1):
                        for j in range(2):
                            act.wait_ge(s["mup_psum"], it * n_up + HT1 * (e + 1) + 2 * j + 2)
                            act.activation(hid1[e % 2][:, 2 * j:2 * j + 2, :],
                                           ps[:, 2 * (e % 2) + j, :].rearrange("p (a b) -> p a b", b=SEQ), ACT.Gelu)\
                                .then_inc(s["mgelu"], 2)

        @block.tensor
        def _(pe):
            pe.wait_ge(s["consts_in"], 16)
            pe.wait_ge(s["setup_pool"], 1 + 2 * NL)
            pe.wait_ge(s["setup_dve"], 2)
            pe.wait_ge(s["w_a_in"], 64)
            pe.wait_ge(s["norm_scaled"], 1)

            with pe.Fori(0, SEQS) as it:
                def turn_tokens(k, src, ln):
                    pe.wait_ge(s["h_ready"], it * n_ln + ln + 1)
                    for c in range(CH):
                        mm = pe.transpose(ps[:, 7, c * P:(c + 1) * P], src[:, c, :], ident)
                    mm.then_inc(s["hT_psum"], 1)
                    pe.wait_ge(s["hT_ready"], it * n_ht + k + 1)

                turn_tokens(0, h_tok, 0)
                for c in range(CH):
                    mm = pe.matmul(ps[:, 6, 32 * c:32 * (c + 1)], hT[:, c * P:(c + 1) * P], w_ba[:, :],
                                   start=True, stop=True)
                mm.then_inc(s["ba_psum"], 1)
                for p in range(MIX // 2):
                    if p >= 4:
                        pe.wait_ge(s["conv_done"], it * MIX // 2 + p - 3)
                    for j in range(2):
                        m = 2 * p + j
                        mm = pe.matmul(ps[:, p % 4, j * SEQ:(j + 1) * SEQ], w_mix[:, m * P:(m + 1) * P], hT[:, :],
                                       start=True, stop=True)
                    mm.then_inc(s["mix_psum"], 1)
                for q in range(2 * CH):
                    if q >= 2:
                        pe.wait_ge(s["z_done"], it * 2 * CH + q - 1)
                    pe.matmul(ps[:, 4 + q % 2, :], hT[:, (q // 2) * P:(q // 2 + 1) * P],
                              w_z[:, 512 * (q % 2):512 * (q % 2 + 1)], start=True, stop=True).then_inc(s["z_psum"], 1)
                pe.wait_ge(s["decay_ready"], it + 1)
                pe.transpose(ps[0:VH, 6, 0:P], decay[:, 1, :], ident).then_inc(s["decT_psum"], 1)
                pe.wait_ge(s["gamT_ready"], it + 1)
                pe.transpose(ps[:, 6, 0:P], gamT[:, :], ident).then_inc(s["gam_psum"], 1)
                pe.wait_ge(s["silu_done"], it * MIX // 2 + 4)
                for m in range(QK_TILES):
                    mm = pe.transpose(ps[:, 7, m * P:(m + 1) * P], mix[:, QK_TILES + m, 0:P], ident)
                mm.then_inc(s["ktok_psum"], 1)
                pe.wait_ge(s["silu_done"], it * MIX // 2 + 8)
                for c in range(CH):
                    if c == 0:
                        pe.wait_ge(s["z_done"], it * 2 * CH + 4)
                    else:
                        pe.wait_ge(s["vtok_ready"], (it * CH + c) * 2)
                    for m in range(V_TILES):
                        mm = pe.transpose(ps[:, 4 + m // 4, (m % 4) * P:(m % 4 + 1) * P],
                                          mix[:, 2 * QK_TILES + m, c * P:(c + 1) * P], ident)
                    mm.then_inc(s["vtok_psum"], 1)

                def chunk_inverse(c):
                    cs = slice(c * P, (c + 1) * P)
                    wave = it * CH * NB + NB * c
                    for b in range(NB):
                        if c == 1:
                            pe.wait_ge(s["e_ready"], wave - NB + b + 1)
                        for h in range(BATCH):
                            mm = pe.matmul(ps[:, b, h * P:(h + 1) * P],
                                           decay[:, c, BATCH * b + h:BATCH * b + h + 1].to_broadcast([P, P]), ident0,
                                           start=True, stop=True)
                        mm.then_inc(s["arow_psum"], 1)
                    for b in range(NB):
                        pe.wait_ge(s["scan_done"], wave + b + 1)
                        for k in range(2):
                            m, r = khead(2 * b + k)
                            kk = mix[r:r + DH, QK_TILES + m, cs]
                            pe.matmul(ps[:, b, k * 2 * P:k * 2 * P + P], kk, kk, start=True, stop=True)
                            mm = pe.matmul(ps[:, b, k * 2 * P + P:(k + 1) * 2 * P], kk, mix[r:r + DH, m, cs],
                                           start=True, stop=True)
                        mm.then_inc(s["kk_psum"], 1)
                    for l in range(NL):
                        n = LEVELS[l]
                        step = ((it * CH + c) * NL + l) * NB
                        for b in range(NB):
                            if l == 0:
                                pe.wait_ge(s["u_first"], wave + b + 1)
                            else:
                                pe.wait_ge(s["u_ready"], step - NB + b + 1)
                            for h in range(BATCH):
                                mm = pe.transpose(ps[:, b, h * P:(h + 1) * P], um[b][:, h, :], ident)
                            mm.then_inc(s["t_psum"], 1)
                        for b in range(NB):
                            pe.wait_ge(s["t_ready"], step + b + 1)
                            for h in range(BATCH):
                                mm = pe.matmul(ps[:, b, h * DH:(h + 1) * DH], at[b][:, h, :], tm[b][:, h, :],
                                               start=True, stop=True)
                            mm.then_inc(s["x_psum"], 1)
                        for b in range(NB):
                            pe.wait_ge(s["x_ready"], step + b + 1)
                            for h in range(BATCH):
                                mm = pe.matmul(ps[:, b, h * DH:(h + 1) * DH], xm[l][b % 2][:, h, :],
                                               even_odd1(um[b][:, h, :], n, 1), start=True, stop=True)
                            mm.then_inc(s["u_psum"], 1)

                def solve(c):
                    for b in range(NB):
                        pe.wait_ge(s["u_ready"], ((it * CH + c) * NL + NL - 1) * NB + b + 1)
                        if c == 1 and b == 0:
                            pe.wait_ge(s["r_ready"], it * 2 + 1)
                        if c == 1 and b == 2:
                            pe.wait_ge(s["r_ready"], it * 2 + 2)
                        for h in range(BATCH):
                            v = BATCH * b + h
                            mm = pe.matmul(ps[:, b, h * DH:(h + 1) * DH], um[b][:, h, :], v_tok[:, c, v, :],
                                           start=True, stop=True)
                        mm.then_inc(s["e_psum"], 1)

                def outputs(c):
                    for b in range(NB):
                        pe.wait_ge(s["e_ready"], it * CH * NB + NB * c + b + 1)
                        for h in range(BATCH):
                            v = BATCH * b + h
                            mm = pe.matmul(ps[:, 4 + v // 8, (v % 8) * DH:(v % 8 + 1) * DH], pt[b][:, h, :],
                                           eps[:, v, :], start=True, stop=True)
                    mm.then_inc(s["o_psum"], 1)

                chunk_inverse(0)
                pe.wait_ge(s["vtok_ready"], (it + 1) * CH * 2)
                solve(0)
                outputs(0)
                pe.wait_ge(s["gam_ready"], it + 1)
                pe.wait_ge(s["ktok_ready"], it + 1)
                for k in range(KH):
                    m, r = khead(k)
                    if k % 2 == 0:
                        pe.wait_ge(s["we_ready"], it * NB + k // 2 + 1)
                    mm = pe.matmul(ps[r:r + DH, 6, m * P:(m + 1) * P], k_tok[:, m, r:r + DH],
                                   w_eps[:, 2 * k:2 * k + 2, :].rearrange("p a b -> p (a b)"), start=True, stop=True)
                mm.then_inc(s["s_psum"], 1)
                chunk_inverse(1)
                pe.wait_ge(s["s_ready"], it + 1)
                pe.wait_ge(s["hz_ready"], it * CH + 1)
                for q, (base, done) in enumerate(((4, "ks_psum"), (6, "qs_psum"))):
                    for k in range(KH):
                        m, r = khead(k)
                        mm = pe.matmul(ps[:, base + k // 4, m * P:(m + 1) * P],
                                       mix[r:r + DH, (QK_TILES if q == 0 else 0) + m, P:2 * P], state[r:r + DH, m, :],
                                       start=True, stop=True)
                    mm.then_inc(s[done], 1)
                solve(1)
                outputs(1)
                for c in range(CH):
                    pe.wait_ge(s["hn_ready"], it * CH + c + 1)
                    if c == 0:
                        pe.wait_ge(s["qs_done"], it + 1)
                    else:
                        pe.wait_ge(s["hzT_ready"], (it * CH + c) * 2)
                    for m in range(V_TILES):
                        mm = pe.transpose(ps[:, 6 + m // 4, (m % 4) * P:(m % 4 + 1) * P],
                                          hz[:, c, 2 * m:2 * m + 2, :].rearrange("p a b -> p (a b)"), ident)
                    mm.then_inc(s["hzT_psum"], 1)
                    pe.wait_ge(s["hzT_ready"], (it * CH + c + 1) * 2)
                    for m in range(V_TILES):
                        mm = pe.matmul(ps[:, c, 0:P], hzT[:, m, :], w_out[:, m, :], start=(m == 0),
                                       stop=(m == V_TILES - 1))
                    mm.then_inc(s["y_psum"], 1)

                def route(k, w, loaded, n_loads):
                    if k == 0:
                        pe.wait_ge(s[loaded], 16 * n_loads)
                    else:
                        pe.wait_ge(s[loaded], 16 * n_loads)
                    for c in range(CH):
                        mm = pe.matmul(ps[:, 6, E * c:E * (c + 1)], hT[:, c * P:(c + 1) * P], w, start=True, stop=True)
                    mm.then_inc(s["lg_psum"], 1)

                if stages >= 2:
                    turn_tokens(1, h_tok, 1)
                    route(0, gate_w[:, :], "w_b_in", 9)
                    for i in range(UP0):
                        if i >= 4:
                            pe.wait_ge(s["prod_ready"], it * UP0 + i - 3)
                        pe.matmul(ps[:, i % 4, 0:SEQ], w1[:, i * P:(i + 1) * P], hT[:, :], start=True, stop=True)
                        pe.matmul(ps[:, i % 4, SEQ:2 * SEQ], w3[:, i * P:(i + 1) * P], hT[:, :], start=True, stop=True)\
                            .then_inc(s["up_psum"], 1)
                    pe.wait_ge(s["rw_ready"], it * n_rt + 1)
                    for c in range(CH):
                        mm = pe.transpose(ps[0:E + 1, 6, c * P:(c + 1) * P], rw[:, c, :], ident)
                    mm.then_inc(s["rwT_psum"], 1)
                    pe.wait_ge(s["hid_ready"], (it + 1) * UP0 // 2)
                    for c in range(CH):
                        cs = slice(c * P, (c + 1) * P)
                        for e in range(E):
                            o = ps[:, (4 if c == 0 else 0) + e % 2, (e // 2) * P:(e // 2 + 1) * P]
                            r = DH * (e % 2)
                            pe.matmul(o, hid0[:, e, cs], w2[:, e, :], start=True, stop=False)
                            mm = pe.matmul(o, hid0[r:r + H1R, E + e // 2, cs], w2r[r:r + H1R, e // 2, :],
                                           start=False, stop=True)
                        if c == 0:
                            pe.wait_ge(s["rwT_ready"], it + 1)
                        o = ps[:, 7, c * P:(c + 1) * P]
                        pe.matmul(o, hid0[:, E + 4, cs], w2[:, E, :], start=True, stop=False)
                        pe.matmul(o, hid0[0:H1R, E + 5, cs], w2r[0:H1R, E // 2, :], start=False, stop=False)
                        pe.matmul(o, rwT[:, cs], b2[:, :], start=False, stop=True).then_inc(s["down_psum"], 1)
                if stages >= 3:
                    turn_tokens(2, h_tok, 3)
                    pe.wait_ge(s["w_c_in"], 16 * 9)
                    for c in range(CH):
                        pe.matmul(ps[:, c, 0:3 * P], hT[:, c * P:(c + 1) * P], a_wqkv[:, :], start=True, stop=True)\
                            .then_inc(s["qkv_psum"], 1)
                    for c in range(CH):
                        pe.wait_ge(s["rot_ready"], it * CH + c + 1)
                        for q in range(2):
                            for g in range(AG):
                                mm = pe.transpose(ps[:, 4 + 2 * c + q, g * P:(g + 1) * P],
                                                  qk_tok[:, c, q, AG * g:AG * (g + 1), :].rearrange("p h d -> p (h d)"),
                                                  ident)
                        mm.then_inc(s["qkT_psum"], 1)
                    pe.wait_ge(s["vaug_ready"], (it + 1) * CH)

                    def scores(u):
                        c, j = u // AG, u % AG
                        if u >= 2:
                            pe.wait_ge(s["shifted_ready"], it * 2 * AG + u - 1)
                        for kc in range(c + 1):
                            bank = 2 * (u % 2) + kc
                            diagonal = kc == c
                            if diagonal:
                                pe.matmul(ps[:, bank, :], ident_bf[:, :], causal_bf[:, :, :].rearrange("p g n -> p (g n)"),
                                          start=True, stop=False, skip_group_check=True)
                            for g in range(AG):
                                mm = pe.matmul(ps[:, bank, g * P:(g + 1) * P], qT[32 * j:32 * j + AD, g, c * P:(c + 1) * P],
                                               kT[32 * j:32 * j + AD, g, kc * P:(kc + 1) * P],
                                               start=not diagonal, stop=True, skip_group_check=True)
                        mm.then_inc(s["s_scores"], 1)

                    def turn_probs(u):
                        c = u // AG
                        pe.wait_ge(s["probs_ready"], it * 2 * AG + u + 1)
                        if u >= 1:
                            pe.wait_ge(s["pT_ready"], it * 2 * AG + u)
                        for kc in range(c + 1):
                            for g in range(AG):
                                mm = pe.transpose(ps[:, 4 + kc, g * P:(g + 1) * P], probs[u % 2][:, kc, g, :], ident)
                        mm.then_inc(s["pT_psum"], 1)

                    def values(u):
                        c, j = u // AG, u % AG
                        pe.wait_ge(s["pT_ready"], it * 2 * AG + u + 1)
                        for g in range(AG):
                            h = AG * g + j
                            for kc in range(c + 1):
                                mm = pe.matmul(ps[:, 6, (c * AH + h) * (AD + 1):(c * AH + h + 1) * (AD + 1)],
                                               probsT[u % 2][:, kc, g, :], v_aug[:, kc, h, :],
                                               start=(kc == 0), stop=(kc == c))
                        mm.then_inc(s["av_psum"], 1)

                    pe.wait_ge(s["qT_ready"], (it + 1) * CH * 2)
                    for u in range(2 * AG + 2):
                        if u < 2 * AG:
                            scores(u)
                        if 1 <= u <= 2 * AG:
                            turn_probs(u - 1)
                        if u >= 2:
                            values(u - 2)
                    pe.wait_ge(s["aout_ready"], it + 1)
                    for c in range(CH):
                        mm = pe.transpose(ps[:, 7, c * P:(c + 1) * P],
                                          a_out[:, c, :, :].rearrange("p h d -> p (h d)"), ident)
                    mm.then_inc(s["aoT_psum"], 1)
                    pe.wait_ge(s["aoT_ready"], it + 1)
                    for c in range(CH):
                        mm = pe.matmul(ps[:, 0, c * P:(c + 1) * P], a_outT[:, c * P:(c + 1) * P], a_wo[:, :],
                                       start=True, stop=True)
                    mm.then_inc(s["wo_psum"], 1)
                    turn_tokens(3, h_tok, 4)
                    for i in range(HT1):
                        pe.matmul(ps[:, i, 0:SEQ], a_w1[:, i * P:(i + 1) * P], hT[:, :],
                                  start=True, stop=True).then_inc(s["mup_psum"], 1)
                    pe.wait_ge(s["mgelu"], it * n_up + HT1)
                    for c in range(CH):
                        for i in range(HT1):
                            mm = pe.matmul(ps[:, 4, c * P:(c + 1) * P], hid1[0][:, i, c * P:(c + 1) * P], a_w2[:, i, :],
                                           start=(i == 0), stop=(i == HT1 - 1))
                    mm.then_inc(s["mdown_psum"], 1)
                if stages >= 4:
                    turn_tokens(4, h_tok, 5)
                    route(1, m_rt[:, :], "w_d_in", 5)

                    def up(e):
                        for i in range(HT1):
                            if e >= 2 and i % 2 == 0:
                                pe.wait_ge(s["mgelu"], it * n_up + HT1 * (e - 1) + i + 2)
                            pe.matmul(ps[:, 2 * (e % 2) + i // 2, SEQ * (i % 2):SEQ * (i % 2 + 1)],
                                      m_up[:, e, i * P:(i + 1) * P], hT[:, :], start=True, stop=True)\
                                .then_inc(s["mup_psum"], 1)

                    def down(e):
                        pe.wait_ge(s["mgelu"], it * n_up + HT1 * (e + 2))
                        if e >= 2:
                            pe.wait_ge(s["mdown_used"], it * E + e - 1)
                        for c in range(CH):
                            for i in range(HT1):
                                mm = pe.matmul(ps[:, 4 + e % 2, c * P:(c + 1) * P], hid1[e % 2][:, i, c * P:(c + 1) * P],
                                               m_down[:, e, i, :], start=(i == 0), stop=(i == HT1 - 1))
                        mm.then_inc(s["mdown_psum"], 1)

                    up(0)
                    for e in range(E + 1):
                        if e < E:
                            up(e + 1)
                        down(e)

        @block.vector
        def _(dve):
            dve.wait_ge(s["consts_in"], 16)
            dve.tensor_copy(ident_bf[:, :], ident).then_inc(s["setup_dve"], 1)
            dve.tensor_copy(causal_bf[:, :, :], over_heads(con[:, C_CAUSAL:C_CAUSAL + P], AG)).then_inc(s["setup_dve"], 1)
            dve.wait_ge(s["setup_pool"], 1 + 2 * NL)
            dve.wait_ge(s["small_in"], 16 * 6)
            dve.tensor_scalar(exp_a[:, 0, :], a_log[:, :], A_MOST, None, ALU.min).then_inc(s["alog_split"], 1)
            dve.tensor_scalar(exp_a[:, 1, :], a_log[:, :], A_MOST + 70.0, A_MOST, ALU.min, ALU.subtract)\
                .then_inc(s["a_shifted"], 1)
            dve.wait_ge(s["a_shifted"], 1)
            dve.tensor_scalar(exp_a[:, 1, :], exp_a[:, 1, :], 0.0, None, ALU.max).then_inc(s["alog_split"], 1)
            dve.wait_ge(s["setup_act"], 1)

            with dve.Fori(0, SEQS) as it:
                me = Steps(dve, s["dve_step"], it, DVE_STEPS)

                def norm(k, src, dst, epsilon):
                    for c in range(CH):
                        me.did(dve.bn_stats(stats[:, c, :], src[:, c, :]))
                    me.settle()
                    dve.memset(pad[:, :], 0.0)
                    for c in range(CH):
                        me.did(dve.bn_aggr(mv[:, c, :], stats[:, c, :]))
                    me.settle()
                    dve.tensor_scalar(var_eps[:, :], mv[:, :, 1], epsilon, None, ALU.add).then_inc(s["ln_var"], 1)
                    dve.wait_ge(s["ln_rstd"], it * n_ln + k + 1)
                    for c in range(CH):
                        ins = dve.tensor_scalar(dst[:, c, :], src[:, c, :], mv[:, c, 0:1], rstd[:, c:c + 1],
                                                ALU.subtract, ALU.mult)
                        if c < CH - 1:
                            me.did(ins)
                    ins.then_inc(s["h_ready"], 1)

                dve.wait_ge(s["x_loaded"], 16 * it + 16)
                norm(0, x_in, h_tok, 1e-5)
                dve.wait_ge(s["ba_psum"], it + 1)
                ba = ps[:, 6, 0:CH * 2 * VH].rearrange("p (c n) -> p c n", c=CH)
                me.did(dve.tensor_scalar(exp_in[:, :, 0:VH], ba[:, :, 0:VH], -1.0, 88.0, ALU.mult, ALU.min))
                me.did(dve.tensor_tensor(pre[:, :, :], ba[:, :, VH:2 * VH], over_heads(dt_bias[:, :], CH), ALU.add))
                me.settle()
                dve.scalar_tensor_tensor(exp_in[:, :, VH:2 * VH], pre[:, :, :], -1.0, pre[:, :, :], ALU.mult, ALU.min)\
                    .then_inc(s["exp_in_ready"], 1)
                dve.wait_ge(s["exp_done"], it + 1)
                u = exp_out[:, :, VH:2 * VH]
                me.did(dve.tensor_scalar(sp_s[:, :, :], u, 2.0, None, ALU.add))
                me.did(dve.tensor_scalar(beta[:, :, :], exp_out[:, :, 0:VH], 1.0, None, ALU.add))
                me.settle(1)
                me.did(dve.reciprocal(sp_s[:, :, :], sp_s[:, :, :]))
                me.settle()
                dve.reciprocal(beta[:, :, :], beta[:, :, :]).then_inc(s["beta_ready"], 1)
                me.did(dve.tensor_tensor(sp_s[:, :, :], sp_s[:, :, :], u, ALU.mult))
                me.settle()
                me.did(dve.tensor_tensor(sp_z[:, :, :], sp_s[:, :, :], sp_s[:, :, :], ALU.mult))
                me.settle()
                me.did(dve.tensor_scalar(sp_p[:, :, :], sp_z[:, :, :], ATANH[0], None, ALU.mult))
                for a in ATANH[1:]:
                    me.settle()
                    me.did(dve.scalar_tensor_tensor(sp_p[:, :, :], sp_p[:, :, :], a, sp_z[:, :, :], ALU.add, ALU.mult))
                me.settle()
                me.did(dve.scalar_tensor_tensor(sp_p[:, :, :], sp_p[:, :, :], 1.0, sp_s[:, :, :], ALU.add, ALU.mult))
                me.did(dve.tensor_scalar(pre[:, :, :], pre[:, :, :], 0.0, None, ALU.max))
                me.settle()
                me.did(dve.scalar_tensor_tensor(sp_p[:, :, :], sp_p[:, :, :], 2.0, pre[:, :, :], ALU.mult, ALU.add))
                me.settle()
                me.did(dve.tensor_tensor(log_decay[:, :, :], sp_p[:, :, :], over_heads(exp_a[:, 0, :], CH), ALU.mult))
                me.settle()
                me.did(dve.tensor_scalar(log_decay[:, :, :], log_decay[:, :, :], 1e4, -1.0, ALU.min, ALU.mult))
                me.settle()
                me.did(dve.tensor_tensor(log_decay[:, :, :], log_decay[:, :, :], over_heads(exp_a[:, 1, :], CH), ALU.mult))
                me.settle()
                dve.tensor_scalar(log_decay[:, :, :], log_decay[:, :, :], -200.0, None, ALU.max)\
                    .then_inc(s["logdec_ready"], 1)
                for p in range(MIX // 2):
                    dve.wait_ge(s["seeded"], it * MIX + 2 * p + 2)
                    for sh in range(1, TAPS):
                        for j in range(2):
                            m = 2 * p + j
                            if sh > 1:
                                me.settle(1)
                            ins = dve.scalar_tensor_tensor(
                                mix[:, m, sh:SEQ], ps[:, p % 4, j * SEQ:(j + 1) * SEQ - sh],
                                conv_w[:, m, TAPS - 1 - sh:TAPS - sh], mix[:, m, sh:SEQ], ALU.mult, ALU.add)
                            if sh < TAPS - 1 or j == 0:
                                me.did(ins)
                    ins.then_inc(s["conv_done"], 1)
                dve.wait_ge(s["decT_psum"], it + 1)
                me.did(dve.tensor_copy(decT[:, :], ps[0:VH, 6, 0:P]))
                me.settle()
                dve.tensor_tensor_scan(gamT[0:VH, :], decT[:, :], zerosT[:, :], 1.0, ALU.mult, ALU.add)\
                    .then_inc(s["gamT_ready"], 1)
                dve.wait_ge(s["gam_psum"], it + 1)
                dve.tensor_copy(gam[:, :], ps[:, 6, 0:VH]).then_inc(s["gam_ready"], 1)

                def chunk_inverse(c):
                    wave = it * CH * NB + NB * c
                    for b in range(NB):
                        dve.wait_ge(s["diag_ready"], wave + b + 1)
                        dve.wait_ge(s["arow_psum"], wave + b + 1)
                        d = dmat[b].rearrange("p h n -> p (h n)")
                        dve.tensor_tensor_scan(d, ps[:, b, :], d, 0.0, ALU.mult, ALU.add).then_inc(s["scan_done"], 1)
                    for b in range(NB):
                        dve.wait_ge(s["scan_done"], wave + b + 1)
                        dve.wait_ge(s["kk_psum"], wave + b + 1)
                        kq = ps[:, b, :].rearrange("p (k q n) -> p k q n", k=2, q=2)
                        d = dmat[b].rearrange("p (k v) n -> p k v n", k=2)
                        for q, dst in ((1, pt), (0, at)):
                            src = kq[:, :, q:q + 1, :].to_broadcast([P, 2, 2, P])
                            ins = dve.tensor_tensor(dst[b][:, :, :].rearrange("p (k v) n -> p k v n", k=2), src, d, ALU.mult)
                            if q == 1:
                                me.did(ins)
                        ins.then_inc(s["at_ready"], 1)
                    for l in range(NL):
                        n = LEVELS[l]
                        step = ((it * CH + c) * NL + l) * NB
                        mask = con[:, C_LM + 64 * l:C_LM + 64 * (l + 1)].rearrange("p (b n) -> p b n", n=n)\
                            .unsqueeze(1).to_broadcast([P, BATCH, DH // n, n])
                        for b in range(NB):
                            dve.wait_ge(s["x_psum"], step + b + 1)
                            if b >= 2:
                                dve.wait_ge(s["u_psum"], step + b - 1)
                            dve.tensor_tensor(even_odd(xm[l][b % 2][:, :, :], n, 0), blocks(ps[:, b, 0:BATCH * DH], n),
                                              mask, ALU.mult).then_inc(s["x_ready"], 1)
                        for b in range(NB):
                            dve.wait_ge(s["u_psum"], step + b + 1)
                            uo = even_odd(um[b], n, 1)
                            dve.tensor_tensor(uo, blocks(ps[:, b, 0:BATCH * DH], n), uo, ALU.add)\
                                .then_inc(s["u_ready"], 1)

                def banks(first):
                    return ps[:, first:first + 2, :].rearrange("p k (h d) -> p (k h) d", d=DH)

                def gated(c):
                    z = z_silu[:, c, :].rearrange("p (h d) -> p h d", d=DH)
                    if c == 0:
                        dve.scalar_tensor_tensor(hz[:, c, :, :], banks(4), DH ** -0.5, z, ALU.mult, ALU.mult)\
                            .then_inc(s["hz_ready"], 1)
                    else:
                        me.did(dve.tensor_tensor(qstate[:, :, :], banks(4), qstate[:, :, :], ALU.add))
                        me.settle()
                        dve.scalar_tensor_tensor(hz[:, c, :, :], qstate[:, :, :], DH ** -0.5, z, ALU.mult, ALU.mult)\
                            .then_inc(s["hz_ready"], 1)

                def rms(c):
                    dve.wait_ge(s["hz_sq"], it * CH + c + 1)
                    me.did(dve.tensor_reduce(ssq[:, :], hsq[:, :, :], X_AXIS, ALU.add))
                    me.settle()
                    dve.tensor_scalar(ssq[:, :], ssq[:, :], 1.0 / DH, 1e-6, ALU.mult, ALU.add).then_inc(s["o_var"], 1)
                    dve.wait_ge(s["o_rstd_ready"], it * CH + c + 1)
                    dve.tensor_tensor(hz[:, c, :, :], hz[:, c, :, :], over_last(o_rstd[:, :], DH), ALU.mult)\
                        .then_inc(s["hn_ready"], 1)

                chunk_inverse(0)
                dve.wait_ge(s["o_psum"], it * CH + 1)
                gated(0)
                chunk_inverse(1)
                dve.wait_ge(s["ks_psum"], it + 1)
                g16 = over_last(gam[:, :], DH)
                me.did(dve.tensor_tensor(kstate[:, :, :], banks(4), g16, ALU.mult))
                me.settle()
                for j in range(2):
                    hs = slice(8 * j, 8 * (j + 1))
                    dve.tensor_tensor(v_tok[:, 1, hs, :], v_tok[:, 1, hs, :], kstate[:, hs, :], ALU.subtract)\
                        .then_inc(s["r_ready"], 1)
                dve.wait_ge(s["qs_psum"], it + 1)
                dve.tensor_tensor(qstate[:, :, :], banks(6), g16, ALU.mult).then_inc(s["qs_done"], 1)
                rms(0)
                dve.wait_ge(s["qs_done"], it + 1)
                dve.wait_ge(s["o_psum"], it * CH + 2)
                gated(1)
                rms(1)
                dve.wait_ge(s["x_stored"], 16 * it + 1)
                for c in range(CH):
                    dve.wait_ge(s["y_psum"], it * CH + c + 1)
                    dst = x_res
                    ins = dve.tensor_tensor(dst[:, c, :], ps[:, c, 0:P], x_in[:, c, :], ALU.add)
                    ins.then_inc(s["x_updated"], 1)
                dve.wait_ge(s["x_updated"], CH * it + CH)
                if stages == 1:
                    dve.tensor_copy(h0[:, :, :], x_res[:, :, :]).then_inc(s["x_final"], 1)

                def route(k, with_bias):
                    dve.wait_ge(s["lg_psum"], it * n_rt + k + 1)
                    lg = ps[:, 6, 0:CH * E].rearrange("p (c e) -> p c e", c=CH)
                    me.did(dve.tensor_reduce(rmax[:, :], lg, X_AXIS, ALU.max))
                    me.settle()
                    dve.tensor_tensor(logit[:, :, :], lg, over_last(rmax[:, :], E), ALU.subtract)\
                        .then_inc(s["shift_ready"], 1)
                    dve.wait_ge(s["rexp_done"], it * n_rt + k + 1)
                    me.did(dve.tensor_reduce(rsum[:, :], rexp[:, :, :], X_AXIS, ALU.add))
                    me.settle()
                    me.did(dve.reciprocal(rsum[:, :], rsum[:, :]))
                    me.settle()
                    me.did(dve.tensor_tensor(score[:, :, :], rexp[:, :, :], over_last(rsum[:, :], E), ALU.mult))
                    me.settle()
                    chosen = score
                    if with_bias:
                        me.did(dve.tensor_tensor(biased[:, :, :], score[:, :, :], over_heads(gate_b[:, :], CH), ALU.add))
                        me.settle()
                        chosen = biased
                    dve.memset(pad[:, :], 0.0)
                    for c in range(CH):
                        me.did(dve.max(top[:, c, :], chosen[:, c, :]))
                    me.settle()
                    second = top[:, :, 1:2].to_broadcast([P, CH, E])
                    me.did(dve.tensor_tensor(over2[:, :, :], chosen[:, :, :], second, ALU.is_gt))
                    me.did(dve.tensor_tensor(is2[:, :, :], chosen[:, :, :], second, ALU.is_equal))
                    me.settle()
                    me.did(dve.tensor_tensor_scan(rank[:, :, :].rearrange("p c e -> p (c e)"), reset,
                                                  is2[:, :, :].rearrange("p c e -> p (c e)"), 0.0, ALU.mult, ALU.add))
                    me.did(dve.tensor_reduce(room[:, :], over2[:, :, :], X_AXIS, ALU.add))
                    me.settle()
                    me.did(dve.tensor_scalar(room[:, :], room[:, :], -1.0, 2.0, ALU.mult, ALU.add))
                    me.settle()
                    me.did(dve.tensor_tensor(rank[:, :, :], rank[:, :, :], over_last(room[:, :], E), ALU.is_le))
                    me.settle()
                    me.did(dve.tensor_tensor(is2[:, :, :], is2[:, :, :], rank[:, :, :], ALU.mult))
                    me.settle()
                    me.did(dve.tensor_tensor(is2[:, :, :], is2[:, :, :], over2[:, :, :], ALU.add))
                    me.settle()
                    dve.tensor_tensor(rw[:, :, 0:E], score[:, :, :], is2[:, :, :], ALU.mult).then_inc(s["rw_ready"], 1)

                if stages >= 2:
                    norm(1, x_res, h_tok, 1e-5)
                    dve.wait_ge(s["w_b_in"], 16 * 9)
                    route(0, True)
                    for i in range(UP0):
                        dve.wait_ge(s["gate_done"], it * UP0 + i + 1)
                        if i >= 4 and i % 2 == 0:
                            dve.wait_ge(s["hid_ready"], it * UP0 // 2 + i // 2 - 1)
                        dve.scalar_tensor_tensor(prod[(i // 2) % 2][:, i % 2, :], ps[:, i % 4, 0:SEQ], b1[:, i:i + 1],
                                                 gate3[i % 4], ALU.add, ALU.mult).then_inc(s["prod_ready"], 1)
                    dve.wait_ge(s["rwT_psum"], it + 1)
                    dve.tensor_copy(rwT[:, :], ps[0:E + 1, 6, 0:SEQ]).then_inc(s["rwT_ready"], 1)
                    dve.wait_ge(s["rw_ready"], it * n_rt + 1)
                    dve.wait_ge(s["down_psum"], (it + 1) * CH)
                    for c in range(CH):
                        me.did(dve.tensor_tensor(x_res[:, c, :], x_res[:, c, :], ps[:, 7, c * P:(c + 1) * P], ALU.add))
                    for e in range(E):
                        for c in range(CH):
                            me.settle(1)
                            o = ps[:, (4 if c == 0 else 0) + e % 2, (e // 2) * P:(e // 2 + 1) * P]
                            me.did(dve.scalar_tensor_tensor(x_res[:, c, :], o, rw[:, c, e:e + 1], x_res[:, c, :],
                                                            ALU.mult, ALU.add))
                    me.settle()
                    if stages == 2:
                        dve.tensor_copy(h0[:, :, :], x_res[:, :, :]).then_inc(s["x_final"], 1)
                if stages >= 3:
                    norm(2, x_res, h0, 1e-5)
                    dve.wait_ge(s["h_ready"], it * n_ln + 3)
                    norm(3, h0, h_tok, 1e-5)
                    for c in range(CH):
                        dve.wait_ge(s["vaug_ready"], it * CH + c + 1)
                        qk = ps[:, c, 0:2 * P].rearrange("p (q h d) -> p q h d", q=2, d=AD)
                        at_c = c * 2 * AD
                        cos = con[:, C_COS + at_c:C_COS + at_c + 2 * AD].rearrange("p (q d) -> p q d", d=AD)\
                            .unsqueeze(2).to_broadcast([P, 2, AH, AD])
                        sin = con[:, C_SIN + at_c:C_SIN + at_c + 2 * AD].rearrange("p (q d) -> p q d", d=AD)\
                            .unsqueeze(2).to_broadcast([P, 2, AH, AD])
                        if c > 0:
                            dve.wait_ge(s["rot_ready"], it * CH + c)
                        me.did(dve.tensor_tensor(rot[:, :, :, :], qk, cos, ALU.mult))
                        for o in range(2):
                            me.did(dve.tensor_tensor(rot2[:, :, :, o::2], qk[:, :, :, 1 - o::2], sin[:, :, :, o::2], ALU.mult))
                        me.settle()
                        dve.tensor_tensor(qk_tok[:, c, :, :, 0:AD], rot[:, :, :, :], rot2[:, :, :, :], ALU.add)\
                            .then_inc(s["rot_ready"], 1)
                    for u in range(2 * AG):
                        c = u // AG
                        dve.wait_ge(s["s_scores"], it * 2 * AG + u + 1)
                        sc = ps[:, 2 * (u % 2):2 * (u % 2) + c + 1, :].rearrange("p k (g n) -> p g k n", n=P)
                        me.did(dve.tensor_reduce(smax[:, u % 2, :], sc, XY_AXIS, ALU.max))
                        me.settle()
                        if u >= 2:
                            dve.wait_ge(s["probs_ready"], it * 2 * AG + u - 1)
                        dve.tensor_tensor(shifted[u % 2][:, 0:c + 1, :, :].rearrange("p k g n -> p g k n"), sc,
                                          smax[:, u % 2, :].unsqueeze(2).unsqueeze(3).to_broadcast([P, AG, c + 1, P]),
                                          ALU.subtract).then_inc(s["shifted_ready"], 1)
                    dve.wait_ge(s["av_psum"], (it + 1) * 2 * AG)
                    av = ps[:, 6, 0:CH * AH * (AD + 1)].rearrange("p (c h d) -> p c h d", c=CH, d=AD + 1)
                    me.did(dve.reciprocal(a_den[:, :, :], av[:, :, :, AD]))
                    me.settle()
                    dve.tensor_tensor(a_out[:, :, :, :], av[:, :, :, 0:AD], over_last3(a_den[:, :, :], AD), ALU.mult)\
                        .then_inc(s["aout_ready"], 1)
                    dve.wait_ge(s["wo_psum"], it + 1)
                    dve.tensor_tensor(xp[:, :, :], ps[:, 0, 0:SEQ].rearrange("p (c d) -> p c d", c=CH), h0[:, :, :], ALU.add)\
                        .then_inc(s["xp_ready"], 1)
                    dve.wait_ge(s["xp_ready"], it + 1)
                    norm(4, xp, h_tok, 1e-5)
                    dve.wait_ge(s["h_pool"], it * (stages - 2) + 1)
                    dve.wait_ge(s["mdown_psum"], it * n_down + 1)
                    dve.tensor_tensor(x_res[:, :, :], ps[:, 4, 0:SEQ].rearrange("p (c d) -> p c d", c=CH),
                                      x_res[:, :, :], ALU.add).then_inc(s["mlp_added"], 1)
                    dve.wait_ge(s["mlp_added"], it + 1)
                    if stages == 3:
                        dve.tensor_copy(h0[:, :, :], x_res[:, :, :]).then_inc(s["x_final"], 1)
                if stages >= 4:
                    norm(5, x_res, h_tok, 1e-5)
                    route(1, False)
                    dve.wait_ge(s["rw_ready"], it * n_rt + 2)
                    dve.wait_ge(s["h_pool"], it * 2 + 2)
                    for e in range(E + 1):
                        dve.wait_ge(s["mdown_psum"], it * n_down + 2 + e)
                        if e > 0:
                            dve.wait_ge(s["mdown_used"], it * E + e)
                        if e == 0:
                            dve.tensor_tensor(x_res[:, :, :], ps[:, 4, 0:SEQ].rearrange("p (c d) -> p c d", c=CH),
                                              x_res[:, :, :], ALU.add).then_inc(s["mdown_used"], 1)
                            continue
                        for c in range(CH):
                            ins = dve.scalar_tensor_tensor(x_res[:, c, :], ps[:, 4 + e % 2, c * P:(c + 1) * P],
                                                           rw[:, c, e - 1:e], x_res[:, c, :], ALU.mult, ALU.add)
                            if c < CH - 1:
                                me.did(ins)
                        ins.then_inc(s["mdown_used" if e < E else "x_final"], 1)
            assert me.n == DVE_STEPS, ("DVE_STEPS", me.n)


def hidden_tiles(routed, shared):
    w = np.zeros((P, UP0, P), routed.dtype)
    w[:, 0:E] = routed[:, :, :P].transpose(1, 0, 2)
    w[:, E:E + 4, 0:H1R] = routed[0::2, :, P:].transpose(1, 0, 2)
    w[:, E:E + 4, DH:DH + H1R] = routed[1::2, :, P:].transpose(1, 0, 2)
    w[:, E + 4] = shared[:, :P]
    w[:, E + 5, 0:H1R] = shared[:, P:]
    return w.reshape(P, UP0 * P)


def bias_tiles(routed, shared):
    b = np.zeros((P, UP0), routed.dtype)
    b[:, 0:E] = routed[:, :P].T
    b[0:H1R, E:E + 4] = routed[0::2, P:].T
    b[DH:DH + H1R, E:E + 4] = routed[1::2, P:].T
    b[:, E + 4] = shared[:P]
    b[0:H1R, E + 5] = shared[P:]
    return b


def rest_rows(routed, shared):
    w = np.zeros((P, E // 2 + 1, P), routed.dtype)
    w[0:H1R, 0:4] = routed[0::2, P:].transpose(1, 0, 2)
    w[DH:DH + H1R, 0:4] = routed[1::2, P:].transpose(1, 0, 2)
    w[0:H1R, 4] = shared[P:]
    return w


def layouts(i):
    a = {k: np.asarray(v) for k, v in i.items()}
    L0, F0, A1, F1 = "L0_attn_", "L0_ffn_", "L1_attn_", "L1_ffn_"
    qk_order = np.concatenate([np.arange(DH) + DH * (m + QK_TILES * r) for m in range(QK_TILES) for r in range(2)])
    order = np.concatenate([qk_order, KH * DH + qk_order, np.arange(VH * DH) + 2 * KH * DH])
    return {
        "consts": constants(),
        "x": a[L0 + "hidden_states"],
        "w_mix": a[L0 + "W_qkv"][order].T,
        "conv_w": a[L0 + "conv_w"][order, 0].reshape(MIX, P, TAPS).transpose(1, 0, 2),
        "w_z": a[L0 + "W_z"].T,
        "w_ba": np.concatenate([a[L0 + "W_b"], a[L0 + "W_a"]]).T,
        "dt_bias": a[L0 + "dt_bias"], "A_log": a[L0 + "A_log"], "norm_weight": a[L0 + "norm_weight"],
        "w_out": a[L0 + "W_out"].T.reshape(V_TILES, P, P).transpose(1, 0, 2),
        "gate_w": a[F0 + "gate_w"].T, "gate_b": a[F0 + "gate_b"],
        "w1": hidden_tiles(a[F0 + "w1"], a[F0 + "sw1"]), "w3": hidden_tiles(a[F0 + "w3"], a[F0 + "sw3"]),
        "b1": bias_tiles(a[F0 + "b1"], a[F0 + "sb1"]), "b3": bias_tiles(a[F0 + "b3"], a[F0 + "sb3"]),
        "w2": np.concatenate([a[F0 + "w2"][:, :P], a[F0 + "sw2"][None, :P]]).transpose(1, 0, 2),
        "w2r": rest_rows(a[F0 + "w2"], a[F0 + "sw2"]),
        "b2": np.concatenate([a[F0 + "b2"], a[F0 + "sb2"][None]]),
        "ln1_g": a[A1 + "ln1_g"], "ln1_b": a[A1 + "ln1_b"], "ln2_g": a[A1 + "ln2_g"], "ln2_b": a[A1 + "ln2_b"],
        "a_wqkv": a[A1 + "Wqkv"], "a_wo": a[A1 + "Wo"], "a_w1": a[A1 + "W1"],
        "a_b1": a[A1 + "b1"].reshape(HT1, P).T, "a_w2": a[A1 + "W2"].reshape(HT1, P, P).transpose(1, 0, 2),
        "a_b2": a[A1 + "b2"],
        "shared_up": a[F1 + "shared_up"],
        "routed_up": a[F1 + "routed_up"].transpose(1, 0, 2),
        "shared_down": a[F1 + "shared_down"][0].reshape(HT1, P, P).transpose(1, 0, 2),
        "routed_down": a[F1 + "routed_down"].reshape(E, HT1, P, P).transpose(2, 0, 1, 3),
        "router_w": a[F1 + "router_w"],
    }


def kernel(**inputs):
    import concourse.bacc as _bacc
    from concourse.bass_utils import run_bass_kernel_spmd as _run

    nc = _bacc.Bacc("TRN2", target_bir_lowering=False, num_devices=1)
    arrays, t = {}, {}
    for name, v in layouts(inputs).items():
        v = np.ascontiguousarray(v)
        arrays[f"in_{name}"] = v
        t[name] = nc.dram_tensor(f"in_{name}", v.shape, mybir.dt.from_np(v.dtype), kind="ExternalInput").ap()
    out = nc.dram_tensor("out_x", (SEQS, SEQ, P), F32, kind="ExternalOutput").ap()
    program(nc, t, out)
    r = _run(nc, [arrays], core_ids=[0])
    return r.results[0]["out_x"]
```

```python
from contextlib import ExitStack

import numpy as np
import concourse.bass as bass
from concourse import mybir

F32 = mybir.dt.float32
BF16 = mybir.dt.bfloat16
ALU = mybir.AluOpType
ACT = mybir.ActivationFunctionType
X_AXIS = mybir.AxisListType.X
XY_AXIS = mybir.AxisListType.XY

P = 128
SEQS, SEQ = 8, 256
CH = SEQ // P
PAIRS, G = SEQS // 2, 2 * CH
KH, VH, DH = 8, 16, 64
QK_TILES, V_TILES = 4, 8
MIX = 2 * QK_TILES + V_TILES
NP = MIX // 2
TAPS = 4
BATCH = 4
NB = VH // BATCH
LEVELS = [2, 4, 8, 16, 32, 64]
NL = len(LEVELS)
E = 8
H1, H1R = 176, 48
UP0 = 14
AH, AD, AP = 16, 8, 32
AG = 4
HT1 = 4
NEG = -1e30

C_ID, C_ID0, C_NM1 = 0, 128, 256
C_LM = 384
C_COS = C_LM + 64 * NL
C_SIN = C_COS + CH * 2 * AD
C_CAUSAL = C_SIN + CH * 2 * AD
C_RESET = C_CAUSAL + 128
C_END = C_RESET + G * E

ATANH = [1.0 / k for k in (15, 13, 11, 9, 7, 5, 3)]

A_MOST = 80.0
N_LN, N_HT, N_RT = 5, 4, 2
UNITS = G * AG
N_UP = HT1 * (E + 2)
N_DOWN = E + 2
DVE_FIRST, POOL_FIRST = (0, 1), (2, 3)
PAIR_BANK = (6, 7, 4, 7, 4, 5, 7, 4)
DOWN0 = (4, 0, 2, 4)
ARENA = 33792

DVE_STEPS = 82
DVE_STEPS2 = 175
POOL_STEPS = 4
POOL_STEPS2 = 1


def constants():
    c = np.zeros((P, C_END), np.float32)
    i = np.arange(P)
    c[:, C_ID:C_ID + P] = np.eye(P)
    c[:, C_ID0:C_ID0 + P] = np.eye(P)
    c[0, C_ID0] = 0
    c[i[0::2], C_NM1 + i[1::2]] = -1
    for l, n in enumerate(LEVELS):
        even = i[(i // n) % 2 == 0]
        row = i[:, None] // n
        c[:, C_LM + 64 * l:C_LM + 64 * (l + 1)] = -((row % 2 == 1) & (even[None, :] // n == row - 1)).astype(np.float32)
    inv_freq = np.float32(10000.0) ** (-(np.arange(0, AD, 2, dtype=np.float32) / np.float32(AD)))
    theta = np.arange(SEQ, dtype=np.float32)[:, None] * inv_freq[None, :].astype(np.float32)
    cos, sin = np.repeat(np.cos(theta), 2, 1), np.repeat(np.sin(theta), 2, 1)
    sin[:, 0::2] *= -1
    for j in range(CH):
        for q, scale in enumerate((AD ** -0.5, 1.0)):
            at = (j * 2 + q) * AD
            c[:, C_COS + at:C_COS + at + AD] = cos[j * P:(j + 1) * P] * scale
            c[:, C_SIN + at:C_SIN + at + AD] = sin[j * P:(j + 1) * P] * scale
    c[:, C_CAUSAL:C_CAUSAL + P] = np.where(i[None, :] > i[:, None], NEG, 0)
    c[:, C_RESET:] = 1
    c[:, C_RESET:C_END:E] = 0
    return c


class Steps:

    def __init__(self, engine, sem, seq, per_seq):
        self.engine, self.sem, self.seq, self.per_seq, self.n = engine, sem, seq, per_seq, 0

    def did(self, instruction):
        self.n += 1
        instruction.then_inc(self.sem, 1)

    def settle(self, but=0):
        if self.n > but:
            self.engine.wait_ge(self.sem, self.seq * self.per_seq + self.n - but)


def program(nc, t, out):
    with ExitStack() as ctx:
        def sb(name, shape, dt=F32):
            return ctx.enter_context(nc.sbuf_tensor(name, shape, dt))

        def sem(name):
            return ctx.enter_context(nc.semaphore(name))

        con = sb("con", [P, C_END])
        ident, ident0, nm1 = con[:, C_ID:C_ID + P], con[:, C_ID0:C_ID0 + P], con[:, C_NM1:C_NM1 + P]
        ident_bf = sb("ident_bf", [P, P], BF16)
        causal_bf = sb("causal_bf", [P, AG, P], BF16)
        reset = con[:, C_RESET:C_END]
        half_power = sb("half_power", [P, VH * CH])

        w_ba = sb("w_ba", [P, 2 * VH])
        conv_w = sb("conv_w", [P, MIX, TAPS])
        dt_bias = sb("dt_bias", [P, VH])
        a_log = sb("a_log", [P, VH])
        exp_a = sb("exp_a", [P, 2, VH])
        norm_w = sb("norm_w", [P, 1])

        gate_w = sb("gate_w", [P, E])
        gate_b = sb("gate_b", [P, E])
        w1 = sb("w1", [P, UP0 * P])
        w3 = sb("w3", [P, UP0 * P])
        b1 = sb("b1", [P, UP0])
        b3 = sb("b3", [P, UP0])
        w2 = sb("w2", [P, E + 1, P])
        w2r = sb("w2r", [P, E // 2 + 1, P])
        b2 = sb("b2", [E + 1, P])

        ln_gb = sb("ln_gb", [P, 4])
        a_wqkv = sb("a_wqkv", [P, 3 * P])
        a_wo = sb("a_wo", [P, P])
        a_w1 = sb("a_w1", [P, HT1 * P])
        a_b1 = sb("a_b1", [P, HT1])
        a_w2 = sb("a_w2", [P, HT1, P])
        a_b2 = sb("a_b2", [P, P])

        m_up = sb("m_up", [P, E + 1, HT1 * P])
        m_rt = sb("m_rt", [P, E])

        x_ln = sb("x_ln", [P, CH, P])
        x_in = sb("x_in", [P, CH, P])
        x_res = sb("x_res", [P, CH, P])
        h_tok = sb("h_tok", [P, G, P])
        hT = sb("hT", [P, G * P])
        stats = sb("stats", [P, G, 6])
        mv = sb("mv", [P, G, 2])
        var_eps = sb("var_eps", [P, G])
        rstd = sb("rstd", [P, G])

        arena = sb("arena", [P, ARENA])
        taken = {1: 0, 2: 0}

        def carve(phase, shape, at=None):
            n = int(np.prod(shape))
            if at is None:
                at = taken[phase]
            taken[phase] = max(taken[phase], at + n)
            assert at + n <= ARENA
            names = "abcd"[:len(shape)]
            v = arena[:, at:at + n]
            if len(shape) == 1:
                return v
            return v.rearrange(f"p ({' '.join(names)}) -> p {' '.join(names)}", **dict(zip(names[1:], shape[1:])))

        w_mix = carve(1, [MIX * P])
        w_z = carve(1, [VH * DH])
        w_out = carve(1, [V_TILES, P])
        conv_next = carve(1, [2 * QK_TILES, SEQ])
        mix = carve(1, [MIX, SEQ])
        z_silu = carve(1, [CH, VH * DH])
        exp_in = sb("exp_in", [P, CH, 2 * VH])
        exp_out = sb("exp_out", [P, CH, 2 * VH])
        pre = sb("pre", [P, CH, VH])
        sp_s = sb("sp_s", [P, CH, VH])
        sp_z = sb("sp_z", [P, CH, VH])
        sp_p = sb("sp_p", [P, CH, VH])
        beta = sb("beta", [P, CH, VH])
        decay = sb("decay", [P, CH, VH])
        log_decay = sb("log_decay", [P, CH, VH])
        decT = sb("decT", [VH, P])
        gamT = sb("gamT", [P, P])
        pad = sb("pad", [P, 1])
        zerosT = sb("zerosT", [VH, P])
        gam = sb("gam", [P, VH])
        dmat_all = carve(1, [NB, BATCH, P])
        at_all = carve(1, [NB, BATCH, P])
        pt_all = carve(1, [NB, BATCH, P])
        um_all = carve(1, [NB, BATCH, P])
        dmat = [dmat_all[:, b, :, :] for b in range(NB)]
        at = [at_all[:, b, :, :] for b in range(NB)]
        pt = [pt_all[:, b, :, :] for b in range(NB)]
        um = [um_all[:, b, :, :] for b in range(NB)]
        tm = [carve(1, [BATCH, P // 2]) for b in range(NB)]
        xm = [[carve(1, [BATCH, P]) for b in range(2)] for l in range(NL)]
        k_tok = carve(1, [QK_TILES, P])
        v_tok = carve(1, [CH, VH, DH])
        eps = carve(1, [VH, DH])
        w_eps = carve(1, [VH, DH])
        state = carve(1, [QK_TILES, P])
        kstate = w_eps
        qstate = carve(1, [VH, DH])
        hz = z_silu[:, :, :].rearrange("p c (h d) -> p c h d", d=DH)
        hsq = eps
        ssq = sb("ssq", [P, VH])
        o_rstd = sb("o_rstd", [P, VH])
        hzT = w_eps[:, :, :].rearrange("p (m a) d -> p m (a d)", a=2)

        logit = sb("logit", [P, G, E])
        rmax = sb("rmax", [P, G])
        rexp = sb("rexp", [P, G, E])
        rsum = sb("rsum", [P, G])
        score = sb("score", [P, G, E])
        biased = sb("biased", [P, G, E])
        top = sb("top", [P, G, 8])
        over2 = sb("over2", [P, G, E])
        is2 = sb("is2", [P, G, E])
        rank = sb("rank", [P, G, E])
        room = sb("room", [P, G])
        rw = sb("rw", [P, G, E + 1])
        rwT = sb("rwT", [E + 1, G * P])
        hid0 = carve(2, [UP0, G * P])
        gate3 = [carve(2, [G * P]) for _ in range(4)]
        prod = [carve(2, [2, G * P]) for _ in range(2)]
        qk_tok = carve(2, [G * 2, AH, AP], at=0).rearrange("p (c q) h d -> p c q h d", q=2)
        qT = carve(2, [AG, G * P], at=G * 2 * AH * AP)
        kT = carve(2, [AG, G * P], at=G * 2 * AH * AP + AG * G * P)
        shifted = [carve(2, [CH, AG, P]) for _ in range(2)]
        probs = [carve(2, [CH, AG, P]) for _ in range(2)]
        probsT = [carve(2, [CH, AG, P]) for _ in range(2)]
        rot = carve(2, [2, AH, AD])
        rot2 = carve(2, [2, AH, AD])
        a_out = carve(2, [G, AH, AD])
        a_outT = carve(2, [G * P])
        pair_in = carve(2, [G, P])
        x2 = carve(2, [G, P])
        h0 = carve(2, [G, P])
        xp = carve(2, [G, P])
        hid1 = [carve(2, [HT1, G * P]) for _ in range(2)]
        pool_pad = sb("pool_pad", [P, 2])
        m_down = carve(2, [E + 1, HT1, P])
        v_aug = carve(2, [G, AH, AD + 1])
        smax = sb("smax", [P, 2, AG])
        a_den = sb("a_den", [P, G, AH])

        ps = ctx.enter_context(nc.psum_tensor("ps", [P, 8, 512], F32))

        names = """consts_in ln_loaded u_first_pool pro_step_pool pro_step v_silu qk_silu m_down_in w_a_in w_b_in w_c_in w_d_in small_in x_loaded x1_stored pair_loaded x_stored
            setup_pool setup_dve setup_act alog_split a_shifted norm_scaled
            dve_step pool_step dve_step2 pool_step2 d_ln_var d_ln_rstd d_h_ready d_hT_psum d_hT_ready merged
            ln_var ln_rstd h_ready hT_psum hT_ready
            ba_psum exp_in_ready exp_done logdec_ready decay_ready decay_tok beta_ready
            mix_psum seeded conv_done silu_done z_psum z_done
            decT_psum decT_ready gamT_ready gam_psum gam_ready
            ktok_psum ktok_ready vtok_psum vtok_ready
            diag_ready arow_psum scan_done kk_psum at_ready u_first
            t_psum t_ready x_psum x_ready u_psum u_ready
            e_psum e_ready we_ready o_psum hz_ready s_psum s_ready ks_psum ks_done qs_psum qs_done r_ready
            hz_sq ssq_ready o_var o_rstd_ready hn_ready hzT_psum hzT_ready y_psum x_updated
            lg_psum shift_ready rexp_done rw_ready rwT_psum rwT_ready
            up_psum gate_done prod_ready hid_ready down_psum mixed_in
            qkv_psum rot_ready vaug_ready qkT_psum qT_ready kT_ready
            s_scores shifted_ready probs_ready pT_psum pT_ready av_psum aout_ready aoT_psum aoT_ready
            wo_psum xp_ready h_pool
            mup_psum mgelu mdown_psum mlp_added mdown_used x_final""".split()
        s = {n: sem(n) for n in names}

        block = ctx.enter_context(nc.Block())

        def even_odd(ap, n, odd):
            return ap.rearrange("p h (b r n) -> p h b r n", r=2, n=n)[:, :, :, odd, :]

        def even_odd1(ap, n, odd):
            return ap.rearrange("p (b r n) -> p b r n", r=2, n=n)[:, :, odd, :]

        def blocks(ap, n):
            return ap.rearrange("p (h b n) -> p h b n", h=BATCH, n=n)

        def over_heads(ap, n):
            return ap.unsqueeze(1).to_broadcast([ap.shape[0], n, ap.shape[1]])

        def over_last(ap, n):
            return ap.unsqueeze(2).to_broadcast([ap.shape[0], ap.shape[1], n])

        def over_last3(ap, n):
            return ap.unsqueeze(3).to_broadcast([ap.shape[0], ap.shape[1], ap.shape[2], n])

        def tokens(dram, seq):
            return dram[bass.ds(seq, 1), :, :].rearrange("a (c p) d -> p (a c) d", p=P)

        def pair(dram, i):
            return dram[bass.ds(2 * i, 2), :, :].rearrange("a (c p) d -> p (a c) d", p=P)

        def conv_tile(m):
            return conv_next[:, m, :] if m < 2 * QK_TILES else mix[:, m, :]

        def unit(u):
            return u // (CH * AG), u // AG % CH, u % AG

        def khead(k):
            return k % QK_TILES, DH * (k // QK_TILES)

        @block.sync
        def _(sp):
            sp.dma_start(con[:, :], t["consts"]).then_inc(s["consts_in"], 16)
            sp.dma_start(x_ln[:, :, :], tokens(t["x"], 0)).then_inc(s["ln_loaded"], 16)
            sp.dma_start(w_ba[:, :], t["w_ba"]).then_inc(s["w_a_in"], 16)
            sp.dma_start(w_mix, t["w_mix"]).then_inc(s["w_a_in"], 16)
            sp.dma_start(w_z, t["w_z"]).then_inc(s["w_a_in"], 16)
            sp.dma_start(w_out[:, :, :], t["w_out"]).then_inc(s["w_a_in"], 16)
            sp.dma_start(x_in[:, :, :], tokens(t["x"], 0)).then_inc(s["x_loaded"], 16)
            sp.wait_ge(s["d_h_ready"], 1)
            sp.dma_start(x_ln[:, :, :], tokens(t["x"], 1)).then_inc(s["ln_loaded"], 16)

            def delta_rule(it, ahead):
                if ahead > 1:
                    sp.wait_ge(s["d_h_ready"], it + 2)
                    sp.dma_start(x_ln[:, :, :], tokens(t["x"], it + 2)).then_inc(s["ln_loaded"], 16)
                sp.wait_ge(s["x_updated"], CH * it + CH + 1)
                sp.dma_start(tokens(out, it), x_res[:, :, :]).then_inc(s["x1_stored"], 16)
                if ahead > 0:
                    sp.dma_start(x_in[:, :, :], tokens(t["x"], it + 1)).then_inc(s["x_loaded"], 16)

            with sp.Fori(0, SEQS - 2) as it:
                delta_rule(it, 2)
            delta_rule(SEQS - 2, 1)
            delta_rule(SEQS - 1, 0)
            sp.wait_ge(s["x1_stored"], 16 * SEQS + 1)
            sp.dma_start(pair_in[:, :, :], pair(out, 0)).then_inc(s["pair_loaded"], 16)
            sp.dma_start(m_down[:, 0, :, :], t["shared_down"]).then_inc(s["m_down_in"], 16)
            sp.dma_start(m_down[:, 1:E + 1, :, :], t["routed_down"]).then_inc(s["m_down_in"], 16)
            with sp.Fori(0, PAIRS - 1) as it:
                sp.wait_ge(s["merged"], G * it + G)
                sp.dma_start(pair_in[:, :, :], pair(out, it + 1)).then_inc(s["pair_loaded"], 16)
                sp.wait_ge(s["x_final"], it + 1)
                sp.dma_start(pair(out, it), x2[:, :, :]).then_inc(s["x_stored"], 16)
            sp.wait_ge(s["x_final"], PAIRS)
            sp.dma_start(pair(out, PAIRS - 1), x2[:, :, :]).then_inc(s["x_stored"], 16)
            sp.wait_ge(s["x_stored"], 16 * PAIRS + 1)

        @block.gpsimd
        def _(pool):
            for dst, name in ((w1[:, :], "w1"), (w3[:, :], "w3"), (b1[:, :], "b1"), (b3[:, :], "b3"),
                              (w2[:, :, :], "w2"), (w2r[:, :, :], "w2r"), (b2[:, :], "b2"), (gate_w[:, :], "gate_w")):
                pool.dma_start(dst, t[name]).then_inc(s["w_b_in"], 16)
            pool.dma_start(gate_b[:, :], t["gate_b"].partition_broadcast(P)).then_inc(s["w_b_in"], 16)
            pool.memset(half_power[:, :], -0.5)
            pool.memset(pool_pad[:, 0:1], 0.0).then_inc(s["x_updated"], 1)
            pool.memset(x_res[:, :, :], 0.0).then_inc(s["x1_stored"], 1)
            pool.memset(pool_pad[:, 1:2], 0.0).then_inc(s["x_stored"], 1)
            pool.memset(rw[:, :, E:E + 1], 1.0)
            pool.memset(gamT[:, :], 0.0)
            pool.memset(zerosT[:, :], 0.0).then_inc(s["setup_pool"], 1)
            for l in range(NL):
                for b in range(2):
                    pool.memset(xm[l][b][:, :, :], 0.0).then_inc(s["setup_pool"], 1)
            pool.wait_ge(s["w_a_in"], 64)
            pool.wait_ge(s["small_in"], 16 * 6)
            pool.tensor_scalar(w_out[:, :, :], w_out[:, :, :], norm_w[:, 0:1], None, ALU.mult)\
                .then_inc(s["norm_scaled"], 1)
            pool.wait_ge(s["consts_in"], 16)

            def inverse_root_of_norm(i):
                pool.wait_ge(s["d_ln_var"], i + 1)
                pool.tensor_tensor(rstd[:, 0:CH], var_eps[:, 0:CH], half_power[:, 0:CH], ALU.pow)\
                    .then_inc(s["d_ln_rstd"], 1)

            def diagonal(c, b):
                pool.tensor_tensor(dmat[b], over_heads(ident, BATCH),
                                   over_last(beta[:, c, BATCH * b:BATCH * (b + 1)], P), ALU.mult)\
                    .then_inc(s["diag_ready"], 1)

            def first_blocks(me, i, c):
                for b in POOL_FIRST:
                    pool.wait_ge(s["at_ready"], i * CH * NB + NB * c + b + 1)
                    me.did(pool.tensor_tensor(um[b], at[b], over_heads(nm1, BATCH), ALU.mult))
                    me.settle()
                    pool.tensor_tensor(um[b], um[b], over_heads(ident, BATCH), ALU.add).then_inc(s["u_first_pool"], 1)

            def delta_rule(it, more):
                me = Steps(pool, s["pool_step"], it, POOL_STEPS)
                i = it + 1
                if more:
                    inverse_root_of_norm(i)
                for b in range(NB):
                    pool.wait_ge(s["e_ready"], it * CH * NB + b + 1)
                    hs = slice(BATCH * b, BATCH * (b + 1))
                    pool.tensor_tensor(w_eps[:, hs, :], eps[:, hs, :],
                                       dmat[b][:, :, P - 1:P].to_broadcast([P, BATCH, DH]), ALU.mult)\
                        .then_inc(s["we_ready"], 1)
                    pool.wait_ge(s["we_ready"], it * NB + b + 1)
                    diagonal(1, b)
                first_blocks(me, it, 1)
                pool.wait_ge(s["o_var"], it * CH + 1)
                pool.tensor_tensor(o_rstd[:, :], ssq[:, :], half_power[:, 0:VH], ALU.pow).then_inc(s["o_rstd_ready"], 1)
                if more:
                    pool.wait_ge(s["beta_ready"], i + 1)
                    for b in range(NB):
                        pool.wait_ge(s["at_ready"], i * CH * NB - NB + b + 1)
                        diagonal(0, b)
                pool.wait_ge(s["o_var"], it * CH + 2)
                pool.tensor_tensor(o_rstd[:, :], ssq[:, :], half_power[:, 0:VH], ALU.pow).then_inc(s["o_rstd_ready"], 1)
                if more:
                    first_blocks(me, i, 0)
                    assert me.n == POOL_STEPS, ("POOL_STEPS", me.n)

            me = Steps(pool, s["pro_step_pool"], 0, 0)
            inverse_root_of_norm(0)
            pool.wait_ge(s["beta_ready"], 1)
            for b in range(NB):
                diagonal(0, b)
            first_blocks(me, 0, 0)
            with pool.Fori(0, SEQS - 1) as it:
                delta_rule(it, True)
            delta_rule(SEQS - 1, False)

            with pool.Fori(0, PAIRS) as it:
                me = Steps(pool, s["pool_step2"], it, POOL_STEPS2)

                def inverse_root(k):
                    pool.wait_ge(s["ln_var"], it * N_LN + k + 1)
                    pool.tensor_tensor(rstd[:, :], var_eps[:, :], half_power[:, 0:G], ALU.pow)\
                        .then_inc(s["ln_rstd"], 1)

                inverse_root(0)
                pool.memset(v_aug[:, :, :, AD:AD + 1], 1.0)
                for k in range(1, 4):
                    inverse_root(k)
                pool.wait_ge(s["xp_ready"], it + 1)
                me.did(pool.tensor_tensor(x2[:, :, :], x2[:, :, :], xp[:, :, :], ALU.add))
                me.settle()
                pool.tensor_tensor(x2[:, :, :], x2[:, :, :], over_heads(a_b2[:, :], G), ALU.add)\
                    .then_inc(s["h_pool"], 1)
                inverse_root(4)
                pool.wait_ge(s["h_ready"], it * N_LN + 5)
                pool.tensor_tensor(x2[:, :, :], x2[:, :, :], h_tok[:, :, :], ALU.add).then_inc(s["h_pool"], 1)
            assert me.n == POOL_STEPS2, ("POOL_STEPS2", me.n)

        @block.scalar
        def _(act):
            act.dma_start(conv_w[:, :, :], t["conv_w"]).then_inc(s["small_in"], 16)
            act.dma_start(dt_bias[:, :], t["dt_bias"].partition_broadcast(P)).then_inc(s["small_in"], 16)
            act.dma_start(a_log[:, :], t["A_log"].partition_broadcast(P)).then_inc(s["small_in"], 16)
            for j in range(2):
                act.dma_start(norm_w[DH * j:DH * (j + 1), :], t["norm_weight"].rearrange("(d a) -> d a", a=1))\
                    .then_inc(s["small_in"], 16)
            act.dma_start(a_b1[:, :], t["a_b1"]).then_inc(s["small_in"], 16)
            for j, name in enumerate(("ln1_g", "ln1_b", "ln2_g", "ln2_b")):
                act.dma_start(ln_gb[:, j:j + 1], t[name].rearrange("(d a) -> d a", a=1)).then_inc(s["w_c_in"], 16)
            act.dma_start(a_wqkv[:, :], t["a_wqkv"]).then_inc(s["w_c_in"], 16)
            act.dma_start(a_wo[:, :], t["a_wo"]).then_inc(s["w_c_in"], 16)
            act.dma_start(a_w1[:, :], t["a_w1"]).then_inc(s["w_c_in"], 16)
            act.dma_start(a_w2[:, :, :], t["a_w2"]).then_inc(s["w_c_in"], 16)
            act.dma_start(a_b2[:, :], t["a_b2"].partition_broadcast(P)).then_inc(s["w_c_in"], 16)
            act.dma_start(m_up[:, 0, :], t["shared_up"][0, :, :]).then_inc(s["w_d_in"], 16)
            act.dma_start(m_up[:, 1:E + 1, :], t["routed_up"]).then_inc(s["w_d_in"], 16)
            act.dma_start(m_rt[:, :], t["router_w"]).then_inc(s["w_d_in"], 16)
            act.wait_ge(s["small_in"], 16 * 6)
            act.wait_ge(s["alog_split"], 2)
            act.activation(exp_a[:, :, :], exp_a[:, :, :], ACT.Exp).then_inc(s["setup_act"], 1)

            def turned_norm(i):
                act.wait_ge(s["d_hT_psum"], i + 1)
                act.activation(hT[:, 0:SEQ], ps[:, 7, 0:SEQ], ACT.Copy).then_inc(s["d_hT_ready"], 1)

            def exponentials(i):
                act.wait_ge(s["exp_in_ready"], i + 1)
                act.activation(exp_out[:, :, :], exp_in[:, :, :], ACT.Exp).then_inc(s["exp_done"], 1)

            def decays(i):
                act.wait_ge(s["logdec_ready"], i + 1)
                act.activation(decay[:, :, :], log_decay[:, :, :], ACT.Exp).then_inc(s["decay_ready"], 1)

            def seed(i, p, bank):
                act.wait_ge(s["mix_psum"], i * NP + p + 1)
                for j in range(2):
                    m = 2 * p + j
                    act.activation(conv_tile(m), ps[:, bank, j * SEQ:(j + 1) * SEQ], ACT.Copy,
                                   scale=conv_w[:, m, TAPS - 1:TAPS]).then_inc(s["seeded"], 1)

            def silu_v(i):
                for p in range(QK_TILES, NP):
                    act.wait_ge(s["conv_done"], i * NP + p + 1)
                    act.activation(mix[:, 2 * p:2 * p + 2, :], mix[:, 2 * p:2 * p + 2, :], ACT.Silu)\
                        .then_inc(s["v_silu"], 1)

            def silu_qk(i):
                for p in range(QK_TILES):
                    act.activation(mix[:, 2 * p:2 * p + 2, :], conv_next[:, 2 * p:2 * p + 2, :], ACT.Silu)\
                        .then_inc(s["qk_silu"], 1)

            def delta_rule(it, more):
                i = it + 1

                def v_tokens(c):
                    act.wait_ge(s["vtok_psum"], it * CH + c + 1)
                    for j in range(2):
                        act.activation(v_tok[:, c, 8 * j:8 * (j + 1), :],
                                       ps[:, 4 + j, :].rearrange("p (a b) -> p a b", b=DH), ACT.Copy)\
                            .then_inc(s["vtok_ready"], 1)

                def gate(c):
                    for j in range(2):
                        act.wait_ge(s["z_psum"], it * 2 * CH + 2 * c + j + 1)
                        act.activation(z_silu[:, c, 512 * j:512 * (j + 1)], ps[:, 6 + j, :], ACT.Silu)\
                            .then_inc(s["z_done"], 1)

                def level(c, l):
                    n = LEVELS[l]
                    for b in range(NB):
                        act.wait_ge(s["t_psum"], ((it * CH + c) * NL + l) * NB + b + 1)
                        act.activation(tm[b][:, :, :].rearrange("p h (b n) -> p h b n", n=n),
                                       even_odd(ps[:, b, :].rearrange("p (h m) -> p h m", h=BATCH), n, 0),
                                       ACT.Copy).then_inc(s["t_ready"], 1)

                def solutions(c):
                    for b in range(NB):
                        act.wait_ge(s["e_psum"], it * CH * NB + NB * c + b + 1)
                        act.activation(eps[:, BATCH * b:BATCH * (b + 1), :],
                                       ps[:, b, 0:BATCH * DH].rearrange("p (a b) -> p a b", b=DH), ACT.Copy)\
                            .then_inc(s["e_ready"], 1)

                def squares(c):
                    act.wait_ge(s["hz_ready"], it * CH + c + 1)
                    act.activation(hsq[:, :, :], hz[:, c, :, :], ACT.Square).then_inc(s["hz_sq"], 1)

                def turned_heads(c, j):
                    act.wait_ge(s["hzT_psum"], (it * CH + c) * 2 + j + 1)
                    bank = 6 if c == 0 else 6 + j
                    act.activation(hzT[:, 4 * j:4 * (j + 1), :], ps[:, bank, :].rearrange("p (a b) -> p a b", b=P),
                                   ACT.Copy).then_inc(s["hzT_ready"], 1)

                v_tokens(0)
                gate(0)
                v_tokens(1)
                gate(1)
                act.wait_ge(s["ktok_psum"], it + 1)
                act.activation(k_tok[:, :, :], ps[:, 4, :].rearrange("p (a b) -> p a b", b=P), ACT.Copy)\
                    .then_inc(s["ktok_ready"], 1)
                for l in range(NL):
                    level(0, l)
                    if more and l == 2:
                        turned_norm(i)
                    if more and l >= 3:
                        seed(i, l - 3, PAIR_BANK[l - 3])
                solutions(0)
                act.wait_ge(s["s_psum"], it + 1)
                act.activation(state[:, :, :], ps[:, 6, :].rearrange("p (a b) -> p a b", b=P), ACT.Copy)\
                    .then_inc(s["s_ready"], 1)
                if more:
                    seed(i, 3, PAIR_BANK[3])
                for l in range(NL):
                    level(1, l)
                    if l == 0:
                        act.wait_ge(s["we_ready"], (it + 1) * NB)
                        squares(0)
                    if l == 3:
                        turned_heads(0, 0)
                    if l == 4:
                        turned_heads(0, 1)
                    if more and 1 <= l <= 4:
                        seed(i, 3 + l, PAIR_BANK[3 + l])
                    if more and l == 2:
                        exponentials(i)
                if more:
                    decays(i)
                    silu_v(i)
                    act.wait_ge(s["qs_psum"], it + 1)
                    silu_qk(i)
                solutions(1)
                squares(1)
                turned_heads(1, 0)
                turned_heads(1, 1)

            turned_norm(0)
            exponentials(0)
            for p in range(4):
                seed(0, p, p)
            decays(0)
            for p in range(4, NP):
                seed(0, p, p)
            silu_v(0)
            silu_qk(0)
            with act.Fori(0, SEQS - 1) as it:
                delta_rule(it, True)
            delta_rule(SEQS - 1, False)

            with act.Fori(0, PAIRS) as it:
                def transpose_out(k, gb=None):
                    act.wait_ge(s["hT_psum"], it * N_HT + k + 1)
                    src = ps[:, 7, :]
                    if gb is None:
                        act.activation(hT[:, :], src, ACT.Copy).then_inc(s["hT_ready"], 1)
                    else:
                        act.activation(hT[:, :], src, ACT.Identity, bias=ln_gb[:, 2 * gb + 1:2 * gb + 2],
                                       scale=ln_gb[:, 2 * gb:2 * gb + 1]).then_inc(s["hT_ready"], 1)

                def router(k):
                    act.wait_ge(s["shift_ready"], it * N_RT + k + 1)
                    act.activation(rexp[:, :, :], logit[:, :, :], ACT.Exp).then_inc(s["rexp_done"], 1)

                transpose_out(0)
                router(0)
                act.wait_ge(s["w_b_in"], 16 * 9)
                act.wait_ge(s["w_c_in"], 16 * 9)
                for i in range(UP0):
                    act.wait_ge(s["up_psum"], it * UP0 + i + 1)
                    act.activation(gate3[i % 4], ps[:, 2 * (i % 3) + 1, :], ACT.Identity,
                                   bias=b3[:, i:i + 1]).then_inc(s["gate_done"], 1)
                    if i % 2 == 1:
                        act.wait_ge(s["prod_ready"], it * UP0 + i + 1)
                        act.activation(hid0[:, i - 1:i + 1, :], prod[(i // 2) % 2], ACT.Silu)\
                            .then_inc(s["hid_ready"], 1)
                transpose_out(1, gb=0)
                for c in range(G):
                    act.wait_ge(s["qkv_psum"], it * G + c + 1)
                    act.activation(v_aug[:, c, :, 0:AD],
                                   ps[:, c, 2 * P:3 * P].rearrange("p (h d) -> p h d", d=AD), ACT.Copy)\
                        .then_inc(s["vaug_ready"], 1)
                for c in range(G):
                    act.wait_ge(s["qkT_psum"], it * G + c + 1)
                    for q, dst in enumerate((qT, kT)):
                        act.activation(dst[:, :, c * P:(c + 1) * P],
                                       ps[:, 4 + 2 * (c % 2) + q, :].rearrange("p (g n) -> p g n", n=P), ACT.Copy)\
                            .then_inc(s["qT_ready"], 1)

                def probabilities(u):
                    c = unit(u)[1]
                    act.wait_ge(s["shifted_ready"], it * UNITS + u + 1)
                    act.activation(probs[u % 2][:, 0:c + 1, :, :], shifted[u % 2][:, 0:c + 1, :, :], ACT.Exp)\
                        .then_inc(s["probs_ready"], 1)

                def turned(u):
                    c = unit(u)[1]
                    act.wait_ge(s["pT_psum"], it * UNITS + u + 1)
                    act.activation(probsT[u % 2][:, 0:c + 1, :, :],
                                   ps[:, 4:5 + c, :].rearrange("p k (g n) -> p k g n", n=P), ACT.Copy)\
                        .then_inc(s["pT_ready"], 1)

                for u in range(UNITS):
                    probabilities(u)
                    if u >= 1:
                        turned(u - 1)
                turned(UNITS - 1)
                act.wait_ge(s["aoT_psum"], it + 1)
                act.activation(a_outT, ps[:, 4, :], ACT.Copy).then_inc(s["aoT_ready"], 1)
                transpose_out(2, gb=1)
                for i in range(HT1):
                    act.wait_ge(s["mup_psum"], it * N_UP + i + 1)
                    act.activation(hid1[0][:, i, :], ps[:, i, :], ACT.Gelu, bias=a_b1[:, i:i + 1])\
                        .then_inc(s["mgelu"], 1)
                transpose_out(3)
                router(1)
                for e in range(E + 1):
                    for i in range(HT1):
                        act.wait_ge(s["mup_psum"], it * N_UP + HT1 * (e + 1) + i + 1)
                        act.activation(hid1[e % 2][:, i, :], ps[:, i, :], ACT.Gelu).then_inc(s["mgelu"], 1)

        @block.tensor
        def _(pe):
            pe.wait_ge(s["consts_in"], 16)
            pe.wait_ge(s["setup_pool"], 1 + 2 * NL)
            pe.wait_ge(s["setup_dve"], 2)
            pe.wait_ge(s["w_a_in"], 64)
            pe.wait_ge(s["norm_scaled"], 1)

            def turn_norm(i):
                pe.wait_ge(s["d_h_ready"], i + 1)
                for c in range(CH):
                    mm = pe.transpose(ps[:, 7, c * P:(c + 1) * P], h_tok[:, c, :], ident)
                mm.then_inc(s["d_hT_psum"], 1)

            def beta_decay(i):
                for c in range(CH):
                    mm = pe.matmul(ps[:, 6, 32 * c:32 * (c + 1)], hT[:, c * P:(c + 1) * P], w_ba[:, :],
                                   start=True, stop=True)
                mm.then_inc(s["ba_psum"], 1)

            def project(i, p, bank):
                for j in range(2):
                    m = 2 * p + j
                    mm = pe.matmul(ps[:, bank, j * SEQ:(j + 1) * SEQ], w_mix[:, m * P:(m + 1) * P], hT[:, 0:SEQ],
                                   start=True, stop=True)
                mm.then_inc(s["mix_psum"], 1)

            def chunk_start(i, c, waits=True):
                cs = slice(c * P, (c + 1) * P)
                wave = i * CH * NB + NB * c
                for b in range(NB):
                    if waits:
                        pe.wait_ge(s["e_ready"], wave - NB + b + 1)
                    for h in range(BATCH):
                        mm = pe.matmul(ps[:, b, h * P:(h + 1) * P],
                                       decay[:, c, BATCH * b + h:BATCH * b + h + 1].to_broadcast([P, P]), ident0,
                                       start=True, stop=True)
                    mm.then_inc(s["arow_psum"], 1)
                if c == 0:
                    pe.wait_ge(s["qk_silu"], (i + 1) * QK_TILES)
                for b in range(NB):
                    pe.wait_ge(s["scan_done"], wave + b + 1)
                    for k in range(2):
                        m, r = khead(2 * b + k)
                        kk = mix[r:r + DH, QK_TILES + m, cs]
                        pe.matmul(ps[:, b, k * 2 * P:k * 2 * P + P], kk, kk, start=True, stop=True)
                        mm = pe.matmul(ps[:, b, k * 2 * P + P:(k + 1) * 2 * P], kk, mix[r:r + DH, m, cs],
                                       start=True, stop=True)
                    mm.then_inc(s["kk_psum"], 1)

            def delta_rule(it, more):
                i = it + 1

                def v_tokens(c):
                    for m in range(V_TILES):
                        mm = pe.transpose(ps[:, 4 + m // 4, (m % 4) * P:(m % 4 + 1) * P],
                                          mix[:, 2 * QK_TILES + m, c * P:(c + 1) * P], ident)
                    mm.then_inc(s["vtok_psum"], 1)

                def gate(c, j):
                    pe.matmul(ps[:, 6 + j, :], hT[:, c * P:(c + 1) * P], w_z[:, 512 * j:512 * (j + 1)],
                              start=True, stop=True).then_inc(s["z_psum"], 1)

                def level(c, l, between=None):
                    n = LEVELS[l]
                    step = ((it * CH + c) * NL + l) * NB
                    for b in range(NB):
                        if l > 0:
                            pe.wait_ge(s["u_ready"], step - NB + b + 1)
                        elif b in DVE_FIRST:
                            pe.wait_ge(s["u_first"], (it * CH + c) * 2 + DVE_FIRST.index(b) + 1)
                        else:
                            pe.wait_ge(s["u_first_pool"], (it * CH + c) * 2 + POOL_FIRST.index(b) + 1)
                        for h in range(BATCH):
                            mm = pe.transpose(ps[:, b, h * P:(h + 1) * P], um[b][:, h, :], ident)
                        mm.then_inc(s["t_psum"], 1)
                    for b in range(NB):
                        pe.wait_ge(s["t_ready"], step + b + 1)
                        for h in range(BATCH):
                            mm = pe.matmul(ps[:, b, h * DH:(h + 1) * DH], at[b][:, h, :], tm[b][:, h, :],
                                           start=True, stop=True)
                        mm.then_inc(s["x_psum"], 1)
                    if between:
                        between()
                    for b in range(NB):
                        pe.wait_ge(s["x_ready"], step + b + 1)
                        for h in range(BATCH):
                            mm = pe.matmul(ps[:, b, h * DH:(h + 1) * DH], xm[l][b % 2][:, h, :],
                                           even_odd1(um[b][:, h, :], n, 1), start=True, stop=True)
                        mm.then_inc(s["u_psum"], 1)

                def solve(c):
                    for b in range(NB):
                        pe.wait_ge(s["u_ready"], ((it * CH + c) * NL + NL - 1) * NB + b + 1)
                        if c == 1 and b % 2 == 0:
                            pe.wait_ge(s["r_ready"], it * 2 + b // 2 + 1)
                        for h in range(BATCH):
                            v = BATCH * b + h
                            mm = pe.matmul(ps[:, b, h * DH:(h + 1) * DH], um[b][:, h, :], v_tok[:, c, v, :],
                                           start=True, stop=True)
                        mm.then_inc(s["e_psum"], 1)

                def outputs(c):
                    for b in range(NB):
                        pe.wait_ge(s["e_ready"], it * CH * NB + NB * c + b + 1)
                        for h in range(BATCH):
                            v = BATCH * b + h
                            mm = pe.matmul(ps[:, 4 + v // 8, (v % 8) * DH:(v % 8 + 1) * DH], pt[b][:, h, :],
                                           eps[:, v, :], start=True, stop=True)
                    mm.then_inc(s["o_psum"], 1)

                def from_state():
                    pe.wait_ge(s["hz_ready"], it * CH + 1)
                    if more:
                        pe.wait_ge(s["conv_done"], (i + 1) * NP)
                    pe.wait_ge(s["s_ready"], it + 1)
                    for q, (base, done) in enumerate(((4, "ks_psum"), (6, "qs_psum"))):
                        if q == 1:
                            pe.wait_ge(s["x_updated"], it * CH + 2)
                        for k in range(KH):
                            m, r = khead(k)
                            mm = pe.matmul(ps[:, base + k // 4, m * P:(m + 1) * P],
                                           mix[r:r + DH, (QK_TILES if q == 0 else 0) + m, P:2 * P], state[r:r + DH, m, :],
                                           start=True, stop=True)
                        mm.then_inc(s[done], 1)

                def turn_heads(c, j):
                    bank = 6 if c == 0 else 6 + j
                    for m in range(4 * j, 4 * (j + 1)):
                        mm = pe.transpose(ps[:, bank, (m % 4) * P:(m % 4 + 1) * P],
                                          hz[:, c, 2 * m:2 * m + 2, :].rearrange("p a b -> p (a b)"), ident)
                    mm.then_inc(s["hzT_psum"], 1)

                def project_out(c):
                    pe.wait_ge(s["hzT_ready"], (it * CH + c + 1) * 2)
                    for m in range(V_TILES):
                        mm = pe.matmul(ps[:, 6 - 2 * c, 0:P], hzT[:, m, :], w_out[:, m, :], start=(m == 0),
                                       stop=(m == V_TILES - 1))
                    mm.then_inc(s["y_psum"], 1)

                pe.wait_ge(s["x_updated"], it * CH + 1)
                pe.wait_ge(s["v_silu"], (it + 1) * QK_TILES)
                v_tokens(0)
                gate(0, 0)
                gate(0, 1)
                pe.wait_ge(s["vtok_ready"], it * CH * 2 + 2)
                v_tokens(1)
                for j in range(2):
                    pe.wait_ge(s["z_done"], it * 2 * CH + j + 1)
                    gate(1, j)
                pe.wait_ge(s["vtok_ready"], (it + 1) * CH * 2)
                for m in range(QK_TILES):
                    mm = pe.transpose(ps[:, 4, m * P:(m + 1) * P], mix[:, QK_TILES + m, 0:P], ident)
                mm.then_inc(s["ktok_psum"], 1)
                pe.transpose(ps[0:VH, 5, 0:P], decay[:, 1, :], ident).then_inc(s["decT_psum"], 1)
                for l in range(NL):
                    level(0, l)
                    if l == 0:
                        pe.wait_ge(s["gamT_ready"], it + 1)
                        pe.transpose(ps[:, 5, 0:P], gamT[:, :], ident).then_inc(s["gam_psum"], 1)
                    if l == 1:
                        pe.wait_ge(s["z_done"], (it + 1) * 2 * CH)
                        if more:
                            turn_norm(i)
                    if more and l == 2:
                        pe.wait_ge(s["d_hT_ready"], i + 1)
                        project(i, 0, PAIR_BANK[0])
                    if more and l == 3:
                        project(i, 1, PAIR_BANK[1])
                    if l == 4:
                        pe.wait_ge(s["ktok_ready"], it + 1)
                        if more:
                            project(i, 2, PAIR_BANK[2])
                    if more and l == 5:
                        pe.wait_ge(s["conv_done"], i * NP + 2)
                        project(i, 3, PAIR_BANK[3])
                solve(0)
                pe.wait_ge(s["gam_ready"], it + 1)
                if more:
                    pe.wait_ge(s["conv_done"], i * NP + 3)
                outputs(0)
                for k in range(KH):
                    m, r = khead(k)
                    if k % 2 == 0:
                        pe.wait_ge(s["we_ready"], it * NB + k // 2 + 1)
                    mm = pe.matmul(ps[r:r + DH, 6, m * P:(m + 1) * P], k_tok[:, m, r:r + DH],
                                   w_eps[:, 2 * k:2 * k + 2, :].rearrange("p a b -> p (a b)"), start=True, stop=True)
                mm.then_inc(s["s_psum"], 1)
                chunk_start(it, 1)
                for l in range(NL):
                    level(1, l, from_state if l == NL - 1 else None)
                    if more and l == 0:
                        pe.wait_ge(s["hz_ready"], it * CH + 1)
                        project(i, 4, PAIR_BANK[4])
                        pe.wait_ge(s["s_ready"], it + 1)
                        beta_decay(i)
                    if more and l == 1:
                        project(i, 5, PAIR_BANK[5])
                    if l == 2:
                        if more:
                            pe.wait_ge(s["conv_done"], i * NP + 4)
                            project(i, 6, PAIR_BANK[6])
                            pe.wait_ge(s["exp_in_ready"], i + 1)
                        else:
                            pe.wait_ge(s["s_ready"], it + 1)
                        pe.wait_ge(s["hn_ready"], it * CH + 1)
                        turn_heads(0, 0)
                    if l == 3:
                        pe.wait_ge(s["hzT_ready"], it * CH * 2 + 1)
                        turn_heads(0, 1)
                        if more:
                            pe.wait_ge(s["conv_done"], i * NP + 5)
                            project(i, 7, PAIR_BANK[7])
                    if l == 4:
                        project_out(0)
                solve(1)
                outputs(1)
                if more:
                    pe.wait_ge(s["decay_ready"], i + 1)
                    chunk_start(i, 0)
                pe.wait_ge(s["qs_done"], it + 1)
                pe.wait_ge(s["hn_ready"], it * CH + 2)
                turn_heads(1, 0)
                turn_heads(1, 1)
                project_out(1)

            turn_norm(0)
            pe.wait_ge(s["d_hT_ready"], 1)
            beta_decay(0)
            for p in range(NP):
                if p == 6:
                    pe.wait_ge(s["exp_in_ready"], 1)
                project(0, p, p)
            pe.wait_ge(s["decay_ready"], 1)
            pe.wait_ge(s["conv_done"], NP)
            chunk_start(0, 0, waits=False)
            with pe.Fori(0, SEQS - 1) as it:
                delta_rule(it, True)
            delta_rule(SEQS - 1, False)

            with pe.Fori(0, PAIRS) as it:
                def turn_tokens(k, src, ln):
                    pe.wait_ge(s["h_ready"], it * N_LN + ln + 1)
                    for c in range(G):
                        mm = pe.transpose(ps[:, 7, c * P:(c + 1) * P], src[:, c, :], ident)
                    mm.then_inc(s["hT_psum"], 1)
                    pe.wait_ge(s["hT_ready"], it * N_HT + k + 1)

                def route(w):
                    for c in range(G):
                        mm = pe.matmul(ps[:, 6, E * c:E * (c + 1)], hT[:, c * P:(c + 1) * P], w, start=True, stop=True)
                    mm.then_inc(s["lg_psum"], 1)

                turn_tokens(0, h_tok, 0)
                pe.wait_ge(s["w_b_in"], 16 * 9)
                route(gate_w[:, :])
                for i in range(UP0):
                    if i >= 3:
                        pe.wait_ge(s["prod_ready"], it * UP0 + i - 2)
                    for j, w in enumerate((w1, w3)):
                        mm = pe.matmul(ps[:, 2 * (i % 3) + j, :], w[:, i * P:(i + 1) * P], hT[:, :], start=True, stop=True)
                    mm.then_inc(s["up_psum"], 1)
                pe.wait_ge(s["rw_ready"], it * N_RT + 1)
                for c in range(G):
                    mm = pe.transpose(ps[0:E + 1, 6, c * P:(c + 1) * P], rw[:, c, :], ident)
                mm.then_inc(s["rwT_psum"], 1)
                pe.wait_ge(s["hid_ready"], (it + 1) * UP0 // 2)
                for c in range(G):
                    cs = slice(c * P, (c + 1) * P)
                    if c >= 2:
                        pe.wait_ge(s["merged"], it * G + c - 1)
                    for e in range(E):
                        o = ps[:, DOWN0[c] + e % 2, (e // 2) * P:(e // 2 + 1) * P]
                        r = DH * (e % 2)
                        pe.matmul(o, hid0[:, e, cs], w2[:, e, :], start=True, stop=False)
                        pe.matmul(o, hid0[r:r + H1R, E + e // 2, cs], w2r[r:r + H1R, e // 2, :], start=False, stop=True)
                    if c == 0:
                        pe.wait_ge(s["rwT_ready"], it + 1)
                    o = ps[:, 7 - c % 2, 0:P]
                    pe.matmul(o, hid0[:, E + 4, cs], w2[:, E, :], start=True, stop=False)
                    pe.matmul(o, hid0[0:H1R, E + 5, cs], w2r[0:H1R, E // 2, :], start=False, stop=False)
                    pe.matmul(o, rwT[:, cs], b2[:, :], start=False, stop=True).then_inc(s["down_psum"], 1)
                turn_tokens(1, h_tok, 2)
                pe.wait_ge(s["w_c_in"], 16 * 9)
                for c in range(G):
                    pe.matmul(ps[:, c, 0:3 * P], hT[:, c * P:(c + 1) * P], a_wqkv[:, :], start=True, stop=True)\
                        .then_inc(s["qkv_psum"], 1)
                for c in range(G):
                    pe.wait_ge(s["rot_ready"], it * G + c + 1)
                    if c >= 2:
                        pe.wait_ge(s["qT_ready"], (it * G + c - 1) * 2)
                    for q in range(2):
                        for g in range(AG):
                            mm = pe.transpose(ps[:, 4 + 2 * (c % 2) + q, g * P:(g + 1) * P],
                                              qk_tok[:, c, q, AG * g:AG * (g + 1), :].rearrange("p h d -> p (h d)"),
                                              ident)
                    mm.then_inc(s["qkT_psum"], 1)
                pe.wait_ge(s["vaug_ready"], (it + 1) * G)

                def scores(u):
                    sq, c, j = unit(u)
                    if u >= 2:
                        pe.wait_ge(s["shifted_ready"], it * UNITS + u - 1)
                    queries = slice((sq * CH + c) * P, (sq * CH + c + 1) * P)
                    for kc in range(c + 1):
                        bank = 2 * (u % 2) + kc
                        keys = slice((sq * CH + kc) * P, (sq * CH + kc + 1) * P)
                        diagonal = kc == c
                        if diagonal:
                            pe.matmul(ps[:, bank, :], ident_bf[:, :], causal_bf[:, :, :].rearrange("p g n -> p (g n)"),
                                      start=True, stop=False, skip_group_check=True)
                        for g in range(AG):
                            mm = pe.matmul(ps[:, bank, g * P:(g + 1) * P], qT[32 * j:32 * j + AD, g, queries],
                                           kT[32 * j:32 * j + AD, g, keys],
                                           start=not diagonal, stop=True, skip_group_check=True)
                    mm.then_inc(s["s_scores"], 1)

                def turn_probs(u):
                    c = unit(u)[1]
                    pe.wait_ge(s["probs_ready"], it * UNITS + u + 1)
                    if u >= 1:
                        pe.wait_ge(s["pT_ready"], it * UNITS + u)
                    for kc in range(c + 1):
                        for g in range(AG):
                            mm = pe.transpose(ps[:, 4 + kc, g * P:(g + 1) * P], probs[u % 2][:, kc, g, :], ident)
                    mm.then_inc(s["pT_psum"], 1)

                def values(u):
                    sq, c, j = unit(u)
                    pe.wait_ge(s["pT_ready"], it * UNITS + u + 1)
                    for g in range(AG):
                        h = AG * g + j
                        for kc in range(c + 1):
                            mm = pe.matmul(ps[:, 6 + sq, (c * AH + h) * (AD + 1):(c * AH + h + 1) * (AD + 1)],
                                           probsT[u % 2][:, kc, g, :], v_aug[:, sq * CH + kc, h, :],
                                           start=(kc == 0), stop=(kc == c))
                    mm.then_inc(s["av_psum"], 1)

                pe.wait_ge(s["qT_ready"], (it + 1) * G * 2)
                for u in range(UNITS + 2):
                    if u < UNITS:
                        scores(u)
                    if 1 <= u <= UNITS:
                        turn_probs(u - 1)
                    if u >= 2:
                        values(u - 2)
                pe.wait_ge(s["aout_ready"], it + 1)
                for c in range(G):
                    mm = pe.transpose(ps[:, 4, c * P:(c + 1) * P],
                                      a_out[:, c, :, :].rearrange("p h d -> p (h d)"), ident)
                mm.then_inc(s["aoT_psum"], 1)
                pe.wait_ge(s["aoT_ready"], it + 1)
                for c in range(G):
                    mm = pe.matmul(ps[:, 0, c * P:(c + 1) * P], a_outT[:, c * P:(c + 1) * P], a_wo[:, :],
                                   start=True, stop=True)
                mm.then_inc(s["wo_psum"], 1)
                turn_tokens(2, h_tok, 3)
                for i in range(HT1):
                    pe.matmul(ps[:, i, :], a_w1[:, i * P:(i + 1) * P], hT[:, :], start=True, stop=True)\
                        .then_inc(s["mup_psum"], 1)
                pe.wait_ge(s["mgelu"], it * N_UP + HT1)
                for c in range(G):
                    for i in range(HT1):
                        mm = pe.matmul(ps[:, 4, c * P:(c + 1) * P], hid1[0][:, i, c * P:(c + 1) * P], a_w2[:, i, :],
                                       start=(i == 0), stop=(i == HT1 - 1))
                mm.then_inc(s["mdown_psum"], 1)
                turn_tokens(3, h_tok, 4)
                pe.wait_ge(s["w_d_in"], 16 * 3)
                pe.wait_ge(s["m_down_in"], 16 * 2)
                route(m_rt[:, :])

                def up(e):
                    for i in range(HT1):
                        if e >= 1:
                            pe.wait_ge(s["mgelu"], it * N_UP + HT1 * e + i + 1)
                        pe.matmul(ps[:, i, :], m_up[:, e, i * P:(i + 1) * P], hT[:, :], start=True, stop=True)\
                            .then_inc(s["mup_psum"], 1)

                def down(e):
                    pe.wait_ge(s["mgelu"], it * N_UP + HT1 * (e + 2))
                    if e >= 2:
                        pe.wait_ge(s["mdown_used"], it * E + e - 1)
                    for c in range(G):
                        for i in range(HT1):
                            mm = pe.matmul(ps[:, 4 + e % 2, c * P:(c + 1) * P], hid1[e % 2][:, i, c * P:(c + 1) * P],
                                           m_down[:, e, i, :], start=(i == 0), stop=(i == HT1 - 1))
                    mm.then_inc(s["mdown_psum"], 1)

                up(0)
                for e in range(E + 1):
                    if e < E:
                        up(e + 1)
                    down(e)

        @block.vector
        def _(dve):
            dve.wait_ge(s["consts_in"], 16)
            dve.tensor_copy(ident_bf[:, :], ident).then_inc(s["setup_dve"], 1)
            dve.tensor_copy(causal_bf[:, :, :], over_heads(con[:, C_CAUSAL:C_CAUSAL + P], AG)).then_inc(s["setup_dve"], 1)
            dve.wait_ge(s["setup_pool"], 1 + 2 * NL)
            dve.wait_ge(s["small_in"], 16 * 6)
            dve.tensor_scalar(exp_a[:, 0, :], a_log[:, :], A_MOST, None, ALU.min).then_inc(s["alog_split"], 1)
            dve.tensor_scalar(exp_a[:, 1, :], a_log[:, :], A_MOST + 70.0, A_MOST, ALU.min, ALU.subtract)\
                .then_inc(s["a_shifted"], 1)
            dve.wait_ge(s["a_shifted"], 1)
            dve.tensor_scalar(exp_a[:, 1, :], exp_a[:, 1, :], 0.0, None, ALU.max).then_inc(s["alog_split"], 1)
            dve.wait_ge(s["setup_act"], 1)

            def norm_before(me, src, n, prefix):
                for c in range(n):
                    me.did(dve.bn_stats(stats[:, c, :], src[:, c, :]))
                me.settle()
                dve.memset(pad[:, :], 0.0)
                for c in range(n):
                    me.did(dve.bn_aggr(mv[:, c, :], stats[:, c, :]))
                me.settle()
                dve.tensor_scalar(var_eps[:, 0:n], mv[:, 0:n, 1], 1e-5, None, ALU.add).then_inc(s[prefix + "ln_var"], 1)

            def norm_after(me, src, dst, n, prefix, count):
                dve.wait_ge(s[prefix + "ln_rstd"], count)
                for c in range(n):
                    ins = dve.tensor_scalar(dst[:, c, :], src[:, c, :], mv[:, c, 0:1], rstd[:, c:c + 1],
                                            ALU.subtract, ALU.mult)
                    if c < n - 1:
                        me.did(ins)
                ins.then_inc(s[prefix + "h_ready"], 1)

            def norm(me, src, dst, n, prefix, count):
                norm_before(me, src, n, prefix)
                norm_after(me, src, dst, n, prefix, count)

            def prepare(me, i, part):
                if part == 0:
                    dve.wait_ge(s["ln_loaded"], 16 * i + 16)
                    norm_before(me, x_ln, CH, "d_")
                else:
                    norm_after(me, x_ln, h_tok, CH, "d_", i + 1)

            def convolve(me, i, m, bank):
                dve.wait_ge(s["seeded"], i * MIX + 2 * (m // 2) + 2)
                for sh in range(1, TAPS):
                    if sh > 1:
                        me.settle()
                    ins = dve.scalar_tensor_tensor(
                        conv_tile(m)[:, sh:SEQ], ps[:, bank, (m % 2) * SEQ:(m % 2 + 1) * SEQ - sh],
                        conv_w[:, m, TAPS - 1 - sh:TAPS - sh], conv_tile(m)[:, sh:SEQ], ALU.mult, ALU.add)
                    if sh < TAPS - 1 or m % 2 == 0:
                        me.did(ins)
                if m % 2 == 1:
                    ins.then_inc(s["conv_done"], 1)

            def exponents(me, i):
                dve.wait_ge(s["ba_psum"], i + 1)
                ba = ps[:, 6, 0:CH * 2 * VH].rearrange("p (c n) -> p c n", c=CH)
                me.did(dve.tensor_scalar(exp_in[:, :, 0:VH], ba[:, :, 0:VH], -1.0, 88.0, ALU.mult, ALU.min))
                me.did(dve.tensor_tensor(pre[:, :, :], ba[:, :, VH:2 * VH], over_heads(dt_bias[:, :], CH), ALU.add))
                me.settle()
                dve.scalar_tensor_tensor(exp_in[:, :, VH:2 * VH], pre[:, :, :], -1.0, pre[:, :, :], ALU.mult, ALU.min)\
                    .then_inc(s["exp_in_ready"], 1)

            def log_decays(me, i, part):
                u = exp_out[:, :, VH:2 * VH]
                if part == 0:
                    dve.wait_ge(s["exp_done"], i + 1)
                    me.did(dve.tensor_scalar(sp_s[:, :, :], u, 2.0, None, ALU.add))
                    me.did(dve.tensor_scalar(beta[:, :, :], exp_out[:, :, 0:VH], 1.0, None, ALU.add))
                    me.settle(1)
                    me.did(dve.reciprocal(sp_s[:, :, :], sp_s[:, :, :]))
                    me.settle()
                    dve.reciprocal(beta[:, :, :], beta[:, :, :]).then_inc(s["beta_ready"], 1)
                if part == 1:
                    me.did(dve.tensor_tensor(sp_s[:, :, :], sp_s[:, :, :], u, ALU.mult))
                    me.settle()
                    me.did(dve.tensor_tensor(sp_z[:, :, :], sp_s[:, :, :], sp_s[:, :, :], ALU.mult))
                    me.settle()
                    me.did(dve.tensor_scalar(sp_p[:, :, :], sp_z[:, :, :], ATANH[0], None, ALU.mult))
                    for a in ATANH[1:]:
                        me.settle()
                        me.did(dve.scalar_tensor_tensor(sp_p[:, :, :], sp_p[:, :, :], a, sp_z[:, :, :], ALU.add, ALU.mult))
                if part == 2:
                    me.settle()
                    me.did(dve.scalar_tensor_tensor(sp_p[:, :, :], sp_p[:, :, :], 1.0, sp_s[:, :, :], ALU.add, ALU.mult))
                    me.did(dve.tensor_scalar(pre[:, :, :], pre[:, :, :], 0.0, None, ALU.max))
                    me.settle()
                    me.did(dve.scalar_tensor_tensor(sp_p[:, :, :], sp_p[:, :, :], 2.0, pre[:, :, :], ALU.mult, ALU.add))
                    me.settle()
                    me.did(dve.tensor_tensor(log_decay[:, :, :], sp_p[:, :, :], over_heads(exp_a[:, 0, :], CH), ALU.mult))
                    me.settle()
                    me.did(dve.tensor_scalar(log_decay[:, :, :], log_decay[:, :, :], 1e4, -1.0, ALU.min, ALU.mult))
                    me.settle()
                    me.did(dve.tensor_tensor(log_decay[:, :, :], log_decay[:, :, :], over_heads(exp_a[:, 1, :], CH), ALU.mult))
                    me.settle()
                    dve.tensor_scalar(log_decay[:, :, :], log_decay[:, :, :], -200.0, None, ALU.max)\
                        .then_inc(s["logdec_ready"], 1)

            def chunk_scans(i, c):
                wave = i * CH * NB + NB * c
                for b in range(NB):
                    dve.wait_ge(s["diag_ready"], wave + b + 1)
                    dve.wait_ge(s["arow_psum"], wave + b + 1)
                    d = dmat[b].rearrange("p h n -> p (h n)")
                    dve.tensor_tensor_scan(d, ps[:, b, :], d, 0.0, ALU.mult, ALU.add).then_inc(s["scan_done"], 1)

            def chunk_products(me, i, c, b):
                wave = i * CH * NB + NB * c
                dve.wait_ge(s["scan_done"], wave + b + 1)
                dve.wait_ge(s["kk_psum"], wave + b + 1)
                kq = ps[:, b, :].rearrange("p (k q n) -> p k q n", k=2, q=2)
                d = dmat[b].rearrange("p (k v) n -> p k v n", k=2)
                for q, dst in ((1, pt), (0, at)):
                    src = kq[:, :, q:q + 1, :].to_broadcast([P, 2, 2, P])
                    ins = dve.tensor_tensor(dst[b][:, :, :].rearrange("p (k v) n -> p k v n", k=2), src, d, ALU.mult)
                    if q == 1:
                        me.did(ins)
                ins.then_inc(s["at_ready"], 1)

            def first_blocks(me, i, c):
                for b in DVE_FIRST:
                    dve.wait_ge(s["at_ready"], i * CH * NB + NB * c + b + 1)
                    me.did(dve.tensor_tensor(um[b], at[b], over_heads(nm1, BATCH), ALU.mult))
                for k, b in enumerate(DVE_FIRST):
                    me.settle(len(DVE_FIRST) - 1 - k)
                    ins = dve.tensor_tensor(um[b], um[b], over_heads(ident, BATCH), ALU.add)
                    ins.then_inc(s["u_first"], 1)

            def delta_rule(it, more):
                me = Steps(dve, s["dve_step"], it, DVE_STEPS)
                i = it + 1

                def level(c, l, between=None):
                    n = LEVELS[l]
                    step = ((it * CH + c) * NL + l) * NB
                    mask = con[:, C_LM + 64 * l:C_LM + 64 * (l + 1)].rearrange("p (b n) -> p b n", n=n)\
                        .unsqueeze(1).to_broadcast([P, BATCH, DH // n, n])
                    for b in range(NB):
                        if b == 2 and between:
                            between()
                        dve.wait_ge(s["x_psum"], step + b + 1)
                        if b >= 2:
                            dve.wait_ge(s["u_psum"], step + b - 1)
                        dve.tensor_tensor(even_odd(xm[l][b % 2][:, :, :], n, 0), blocks(ps[:, b, 0:BATCH * DH], n),
                                          mask, ALU.mult).then_inc(s["x_ready"], 1)
                    for b in range(NB):
                        dve.wait_ge(s["u_psum"], step + b + 1)
                        uo = even_odd(um[b], n, 1)
                        dve.tensor_tensor(uo, blocks(ps[:, b, 0:BATCH * DH], n), uo, ALU.add)\
                            .then_inc(s["u_ready"], 1)

                def banks(first):
                    return ps[:, first:first + 2, :].rearrange("p k (h d) -> p (k h) d", d=DH)

                def gated(c):
                    dve.wait_ge(s["o_psum"], it * CH + c + 1)
                    z = z_silu[:, c, :].rearrange("p (h d) -> p h d", d=DH)
                    o = banks(4)
                    if c == 1:
                        me.did(dve.tensor_tensor(qstate[:, :, :], banks(4), qstate[:, :, :], ALU.add))
                        me.settle()
                        o = qstate[:, :, :]
                    dve.scalar_tensor_tensor(hz[:, c, :, :], o, DH ** -0.5, z, ALU.mult, ALU.mult)\
                        .then_inc(s["hz_ready"], 1)

                def sum_squares(c):
                    dve.wait_ge(s["hz_sq"], it * CH + c + 1)
                    me.did(dve.tensor_reduce(ssq[:, :], hsq[:, :, :], X_AXIS, ALU.add))
                    me.settle()
                    dve.tensor_scalar(ssq[:, :], ssq[:, :], 1.0 / DH, 1e-6, ALU.mult, ALU.add).then_inc(s["o_var"], 1)

                def normalise(c):
                    dve.wait_ge(s["o_rstd_ready"], it * CH + c + 1)
                    dve.tensor_tensor(hz[:, c, :, :], hz[:, c, :, :], over_last(o_rstd[:, :], DH), ALU.mult)\
                        .then_inc(s["hn_ready"], 1)

                def residual(c):
                    dve.wait_ge(s["y_psum"], it * CH + c + 1)
                    dve.tensor_tensor(x_res[:, c, :], ps[:, 6 - 2 * c, 0:P], x_in[:, c, :], ALU.add)\
                        .then_inc(s["x_updated"], 1)

                g16 = over_last(gam[:, :], DH)

                def less_state():
                    dve.wait_ge(s["ks_psum"], it + 1)
                    me.did(dve.tensor_tensor(kstate[:, :, :], banks(4), g16, ALU.mult))
                    me.settle()
                    for j in range(2):
                        hs = slice(8 * j, 8 * (j + 1))
                        dve.tensor_tensor(v_tok[:, 1, hs, :], v_tok[:, 1, hs, :], kstate[:, hs, :], ALU.subtract)\
                            .then_inc(s["r_ready"], 1)

                if more:
                    prepare(me, i, 0)
                dve.wait_ge(s["decT_psum"], it + 1)
                me.did(dve.tensor_copy(decT[:, :], ps[0:VH, 5, 0:P]))
                me.settle()
                dve.tensor_tensor_scan(gamT[0:VH, :], decT[:, :], zerosT[:, :], 1.0, ALU.mult, ALU.add)\
                    .then_inc(s["gamT_ready"], 1)
                for l in range(NL):
                    level(0, l, (lambda: prepare(me, i, 1)) if more and l == 1 else None)
                    if l == 0:
                        dve.wait_ge(s["gam_psum"], it + 1)
                        dve.tensor_copy(gam[:, :], ps[:, 5, 0:VH]).then_inc(s["gam_ready"], 1)
                    if more and l >= 3:
                        for m in (2 * (l - 3), 2 * (l - 3) + 1):
                            convolve(me, i, m, PAIR_BANK[m // 2])
                gated(0)
                chunk_scans(it, 1)
                for b in range(NB):
                    chunk_products(me, it, 1, b)
                first_blocks(me, it, 1)
                for l in range(NL):
                    level(1, l, (lambda: residual(0)) if l == NL - 1 else None)
                    if more and l < NL - 1:
                        for m in (6 + 2 * l, 7 + 2 * l):
                            convolve(me, i, m, PAIR_BANK[m // 2])
                    if l == 0:
                        sum_squares(0)
                    if l == 1:
                        normalise(0)
                    if more and l == 1:
                        exponents(me, i)
                    if more and 2 <= l <= 4:
                        log_decays(me, i, l - 2)
                    if l == NL - 2:
                        dve.wait_ge(s["x1_stored"], 16 * it + 1)
                        dve.wait_ge(s["x_loaded"], 16 * it + 16)
                less_state()
                dve.wait_ge(s["qs_psum"], it + 1)
                dve.tensor_tensor(qstate[:, :, :], banks(6), g16, ALU.mult).then_inc(s["qs_done"], 1)
                dve.wait_ge(s["qs_done"], it + 1)
                gated(1)
                if more:
                    chunk_scans(i, 0)
                sum_squares(1)
                if more:
                    chunk_products(me, i, 0, 0)
                    chunk_products(me, i, 0, 1)
                normalise(1)
                if more:
                    chunk_products(me, i, 0, 2)
                    chunk_products(me, i, 0, 3)
                    first_blocks(me, i, 0)
                residual(1)
                if more:
                    assert me.n == DVE_STEPS, ("DVE_STEPS", me.n)

            me = Steps(dve, s["pro_step"], 0, 0)
            prepare(me, 0, 0)
            prepare(me, 0, 1)
            exponents(me, 0)
            for part in range(3):
                log_decays(me, 0, part)
            for m in range(MIX):
                convolve(me, 0, m, m // 2)
            chunk_scans(0, 0)
            for b in range(NB):
                chunk_products(me, 0, 0, b)
            first_blocks(me, 0, 0)
            with dve.Fori(0, SEQS - 1) as it:
                delta_rule(it, True)
            delta_rule(SEQS - 1, False)

            with dve.Fori(0, PAIRS) as it:
                me = Steps(dve, s["dve_step2"], it, DVE_STEPS2)

                def route(k, with_bias):
                    dve.wait_ge(s["lg_psum"], it * N_RT + k + 1)
                    lg = ps[:, 6, 0:G * E].rearrange("p (c e) -> p c e", c=G)
                    me.did(dve.tensor_reduce(rmax[:, :], lg, X_AXIS, ALU.max))
                    me.settle()
                    dve.tensor_tensor(logit[:, :, :], lg, over_last(rmax[:, :], E), ALU.subtract)\
                        .then_inc(s["shift_ready"], 1)
                    dve.wait_ge(s["rexp_done"], it * N_RT + k + 1)
                    me.did(dve.tensor_reduce(rsum[:, :], rexp[:, :, :], X_AXIS, ALU.add))
                    me.settle()
                    me.did(dve.reciprocal(rsum[:, :], rsum[:, :]))
                    me.settle()
                    me.did(dve.tensor_tensor(score[:, :, :], rexp[:, :, :], over_last(rsum[:, :], E), ALU.mult))
                    me.settle()
                    chosen = score
                    if with_bias:
                        me.did(dve.tensor_tensor(biased[:, :, :], score[:, :, :], over_heads(gate_b[:, :], G), ALU.add))
                        me.settle()
                        chosen = biased
                    dve.memset(pad[:, :], 0.0)
                    for c in range(G):
                        me.did(dve.max(top[:, c, :], chosen[:, c, :]))
                    me.settle()
                    second = top[:, :, 1:2].to_broadcast([P, G, E])
                    me.did(dve.tensor_tensor(over2[:, :, :], chosen[:, :, :], second, ALU.is_gt))
                    me.did(dve.tensor_tensor(is2[:, :, :], chosen[:, :, :], second, ALU.is_equal))
                    me.settle()
                    me.did(dve.tensor_tensor_scan(rank[:, :, :].rearrange("p c e -> p (c e)"), reset,
                                                  is2[:, :, :].rearrange("p c e -> p (c e)"), 0.0, ALU.mult, ALU.add))
                    me.did(dve.tensor_reduce(room[:, :], over2[:, :, :], X_AXIS, ALU.add))
                    me.settle()
                    me.did(dve.tensor_scalar(room[:, :], room[:, :], -1.0, 2.0, ALU.mult, ALU.add))
                    me.settle()
                    me.did(dve.tensor_tensor(rank[:, :, :], rank[:, :, :], over_last(room[:, :], E), ALU.is_le))
                    me.settle()
                    me.did(dve.tensor_tensor(is2[:, :, :], is2[:, :, :], rank[:, :, :], ALU.mult))
                    me.settle()
                    me.did(dve.tensor_tensor(is2[:, :, :], is2[:, :, :], over2[:, :, :], ALU.add))
                    me.settle()
                    dve.tensor_tensor(rw[:, :, 0:E], score[:, :, :], is2[:, :, :], ALU.mult).then_inc(s["rw_ready"], 1)

                dve.wait_ge(s["pair_loaded"], 16 * it + 16)
                norm(me, pair_in, h_tok, G, "", it * N_LN + 1)
                dve.wait_ge(s["w_b_in"], 16 * 9)
                route(0, True)
                for i in range(UP0):
                    dve.wait_ge(s["gate_done"], it * UP0 + i + 1)
                    if i >= 4 and i % 2 == 0:
                        dve.wait_ge(s["hid_ready"], it * UP0 // 2 + i // 2 - 1)
                    dve.scalar_tensor_tensor(prod[(i // 2) % 2][:, i % 2, :], ps[:, 2 * (i % 3), :], b1[:, i:i + 1],
                                             gate3[i % 4], ALU.add, ALU.mult).then_inc(s["prod_ready"], 1)
                dve.wait_ge(s["rwT_psum"], it + 1)
                dve.tensor_copy(rwT[:, :], ps[0:E + 1, 6, :]).then_inc(s["rwT_ready"], 1)
                dve.wait_ge(s["rw_ready"], it * N_RT + 1)
                dve.wait_ge(s["x_stored"], 16 * it + 1)
                for c in range(G):
                    dve.wait_ge(s["down_psum"], it * G + c + 1)
                    me.did(dve.tensor_tensor(x2[:, c, :], pair_in[:, c, :], ps[:, 7 - c % 2, 0:P], ALU.add))
                    for e in range(E):
                        me.settle()
                        o = ps[:, DOWN0[c] + e % 2, (e // 2) * P:(e // 2 + 1) * P]
                        ins = dve.scalar_tensor_tensor(x2[:, c, :], o, rw[:, c, e:e + 1], x2[:, c, :], ALU.mult, ALU.add)
                        if e < E - 1:
                            me.did(ins)
                    ins.then_inc(s["merged"], 1)
                dve.wait_ge(s["merged"], it * G + G)
                norm(me, x2, h0, G, "", it * N_LN + 2)
                dve.wait_ge(s["h_ready"], it * N_LN + 2)
                norm(me, h0, h_tok, G, "", it * N_LN + 3)
                for c in range(G):
                    dve.wait_ge(s["vaug_ready"], it * G + c + 1)
                    qk = ps[:, c, 0:2 * P].rearrange("p (q h d) -> p q h d", q=2, d=AD)
                    at_c = (c % CH) * 2 * AD
                    cos = con[:, C_COS + at_c:C_COS + at_c + 2 * AD].rearrange("p (q d) -> p q d", d=AD)\
                        .unsqueeze(2).to_broadcast([P, 2, AH, AD])
                    sin = con[:, C_SIN + at_c:C_SIN + at_c + 2 * AD].rearrange("p (q d) -> p q d", d=AD)\
                        .unsqueeze(2).to_broadcast([P, 2, AH, AD])
                    if c > 0:
                        dve.wait_ge(s["rot_ready"], it * G + c)
                    me.did(dve.tensor_tensor(rot[:, :, :, :], qk, cos, ALU.mult))
                    for o in range(2):
                        me.did(dve.tensor_tensor(rot2[:, :, :, o::2], qk[:, :, :, 1 - o::2], sin[:, :, :, o::2], ALU.mult))
                    me.settle()
                    dve.tensor_tensor(qk_tok[:, c, :, :, 0:AD], rot[:, :, :, :], rot2[:, :, :, :], ALU.add)\
                        .then_inc(s["rot_ready"], 1)
                for u in range(UNITS):
                    c = unit(u)[1]
                    dve.wait_ge(s["s_scores"], it * UNITS + u + 1)
                    sc = ps[:, 2 * (u % 2):2 * (u % 2) + c + 1, :].rearrange("p k (g n) -> p g k n", n=P)
                    me.did(dve.tensor_reduce(smax[:, u % 2, :], sc, XY_AXIS, ALU.max))
                    me.settle()
                    if u >= 2:
                        dve.wait_ge(s["probs_ready"], it * UNITS + u - 1)
                    dve.tensor_tensor(shifted[u % 2][:, 0:c + 1, :, :].rearrange("p k g n -> p g k n"), sc,
                                      smax[:, u % 2, :].unsqueeze(2).unsqueeze(3).to_broadcast([P, AG, c + 1, P]),
                                      ALU.subtract).then_inc(s["shifted_ready"], 1)
                dve.wait_ge(s["av_psum"], (it + 1) * UNITS)
                av = [ps[:, 6 + q, 0:CH * AH * (AD + 1)].rearrange("p (c h d) -> p c h d", c=CH, d=AD + 1) for q in range(2)]
                for q in range(2):
                    me.did(dve.reciprocal(a_den[:, CH * q:CH * (q + 1), :], av[q][:, :, :, AD]))
                me.settle()
                for q in range(2):
                    ins = dve.tensor_tensor(a_out[:, CH * q:CH * (q + 1), :, :], av[q][:, :, :, 0:AD],
                                            over_last3(a_den[:, CH * q:CH * (q + 1), :], AD), ALU.mult)
                    if q == 0:
                        me.did(ins)
                ins.then_inc(s["aout_ready"], 1)
                dve.wait_ge(s["wo_psum"], it + 1)
                dve.tensor_tensor(xp[:, :, :], ps[:, 0, :].rearrange("p (c d) -> p c d", c=G), h0[:, :, :], ALU.add)\
                    .then_inc(s["xp_ready"], 1)
                dve.wait_ge(s["xp_ready"], it + 1)
                norm(me, xp, h_tok, G, "", it * N_LN + 4)
                dve.wait_ge(s["h_pool"], it * 2 + 1)
                dve.wait_ge(s["mdown_psum"], it * N_DOWN + 1)
                dve.tensor_tensor(x2[:, :, :], ps[:, 4, :].rearrange("p (c d) -> p c d", c=G), x2[:, :, :], ALU.add)\
                    .then_inc(s["mlp_added"], 1)
                dve.wait_ge(s["mlp_added"], it + 1)
                norm(me, x2, h_tok, G, "", it * N_LN + 5)
                route(1, False)
                dve.wait_ge(s["rw_ready"], it * N_RT + 2)
                dve.wait_ge(s["h_pool"], it * 2 + 2)
                for e in range(E + 1):
                    dve.wait_ge(s["mdown_psum"], it * N_DOWN + 2 + e)
                    if e > 0:
                        dve.wait_ge(s["mdown_used"], it * E + e)
                    if e == 0:
                        dve.tensor_tensor(x2[:, :, :], ps[:, 4, :].rearrange("p (c d) -> p c d", c=G), x2[:, :, :], ALU.add)\
                            .then_inc(s["mdown_used"], 1)
                        continue
                    for c in range(G):
                        ins = dve.scalar_tensor_tensor(x2[:, c, :], ps[:, 4 + e % 2, c * P:(c + 1) * P],
                                                       rw[:, c, e - 1:e], x2[:, c, :], ALU.mult, ALU.add)
                        if c < G - 1:
                            me.did(ins)
                    ins.then_inc(s["mdown_used" if e < E else "x_final"], 1)
            assert me.n == DVE_STEPS2, ("DVE_STEPS2", me.n)


def hidden_tiles(routed, shared):
    w = np.zeros((P, UP0, P), routed.dtype)
    w[:, 0:E] = routed[:, :, :P].transpose(1, 0, 2)
    w[:, E:E + 4, 0:H1R] = routed[0::2, :, P:].transpose(1, 0, 2)
    w[:, E:E + 4, DH:DH + H1R] = routed[1::2, :, P:].transpose(1, 0, 2)
    w[:, E + 4] = shared[:, :P]
    w[:, E + 5, 0:H1R] = shared[:, P:]
    return w.reshape(P, UP0 * P)


def bias_tiles(routed, shared):
    b = np.zeros((P, UP0), routed.dtype)
    b[:, 0:E] = routed[:, :P].T
    b[0:H1R, E:E + 4] = routed[0::2, P:].T
    b[DH:DH + H1R, E:E + 4] = routed[1::2, P:].T
    b[:, E + 4] = shared[:P]
    b[0:H1R, E + 5] = shared[P:]
    return b


def rest_rows(routed, shared):
    w = np.zeros((P, E // 2 + 1, P), routed.dtype)
    w[0:H1R, 0:4] = routed[0::2, P:].transpose(1, 0, 2)
    w[DH:DH + H1R, 0:4] = routed[1::2, P:].transpose(1, 0, 2)
    w[0:H1R, 4] = shared[P:]
    return w


def layouts(i):
    a = {k: np.asarray(v) for k, v in i.items()}
    L0, F0, A1, F1 = "L0_attn_", "L0_ffn_", "L1_attn_", "L1_ffn_"
    qk_order = np.concatenate([np.arange(DH) + DH * (m + QK_TILES * r) for m in range(QK_TILES) for r in range(2)])
    order = np.concatenate([qk_order, KH * DH + qk_order, np.arange(VH * DH) + 2 * KH * DH])
    return {
        "consts": constants(),
        "x": a[L0 + "hidden_states"],
        "w_mix": a[L0 + "W_qkv"][order].T,
        "conv_w": a[L0 + "conv_w"][order, 0].reshape(MIX, P, TAPS).transpose(1, 0, 2),
        "w_z": a[L0 + "W_z"].T,
        "w_ba": np.concatenate([a[L0 + "W_b"], a[L0 + "W_a"]]).T,
        "dt_bias": a[L0 + "dt_bias"], "A_log": a[L0 + "A_log"], "norm_weight": a[L0 + "norm_weight"],
        "w_out": a[L0 + "W_out"].T.reshape(V_TILES, P, P).transpose(1, 0, 2),
        "gate_w": a[F0 + "gate_w"].T, "gate_b": a[F0 + "gate_b"],
        "w1": hidden_tiles(a[F0 + "w1"], a[F0 + "sw1"]), "w3": hidden_tiles(a[F0 + "w3"], a[F0 + "sw3"]),
        "b1": bias_tiles(a[F0 + "b1"], a[F0 + "sb1"]), "b3": bias_tiles(a[F0 + "b3"], a[F0 + "sb3"]),
        "w2": np.concatenate([a[F0 + "w2"][:, :P], a[F0 + "sw2"][None, :P]]).transpose(1, 0, 2),
        "w2r": rest_rows(a[F0 + "w2"], a[F0 + "sw2"]),
        "b2": np.concatenate([a[F0 + "b2"], a[F0 + "sb2"][None]]),
        "ln1_g": a[A1 + "ln1_g"], "ln1_b": a[A1 + "ln1_b"], "ln2_g": a[A1 + "ln2_g"], "ln2_b": a[A1 + "ln2_b"],
        "a_wqkv": a[A1 + "Wqkv"], "a_wo": a[A1 + "Wo"], "a_w1": a[A1 + "W1"],
        "a_b1": a[A1 + "b1"].reshape(HT1, P).T, "a_w2": a[A1 + "W2"].reshape(HT1, P, P).transpose(1, 0, 2),
        "a_b2": a[A1 + "b2"],
        "shared_up": a[F1 + "shared_up"],
        "routed_up": a[F1 + "routed_up"].transpose(1, 0, 2),
        "shared_down": a[F1 + "shared_down"][0].reshape(HT1, P, P).transpose(1, 0, 2),
        "routed_down": a[F1 + "routed_down"].reshape(E, HT1, P, P).transpose(2, 0, 1, 3),
        "router_w": a[F1 + "router_w"],
    }


def kernel(**inputs):
    import concourse.bacc as _bacc
    from concourse.bass_utils import run_bass_kernel_spmd as _run

    nc = _bacc.Bacc("TRN2", target_bir_lowering=False, num_devices=1)
    arrays, t = {}, {}
    for name, v in layouts(inputs).items():
        v = np.ascontiguousarray(v)
        arrays[f"in_{name}"] = v
        t[name] = nc.dram_tensor(f"in_{name}", v.shape, mybir.dt.from_np(v.dtype), kind="ExternalInput").ap()
    out = nc.dram_tensor("out_x", (SEQS, SEQ, P), F32, kind="ExternalOutput").ap()
    program(nc, t, out)
    r = _run(nc, [arrays], core_ids=[0])
    return r.results[0]["out_x"]
```

```python
from contextlib import ExitStack

import numpy as np
import concourse.bass as bass
from concourse import mybir

F32 = mybir.dt.float32
BF16 = mybir.dt.bfloat16
ALU = mybir.AluOpType
ACT = mybir.ActivationFunctionType
X_AXIS = mybir.AxisListType.X
XY_AXIS = mybir.AxisListType.XY

P = 128
SEQS, SEQ = 8, 256
CH = SEQ // P
PAIRS, G = SEQS // 2, 2 * CH
KH, VH, DH = 8, 16, 64
QK_TILES, V_TILES = 4, 8
MIX = 2 * QK_TILES + V_TILES
NP = MIX // 2
TAPS = 4
BATCH = 4
NB = VH // BATCH
LEVELS = [2, 4, 8, 16, 32, 64]
NL = len(LEVELS)
E = 8
H1 = 176
H1R = H1 - P
UP0 = 14
AH, AD, AP = 16, 8, 32
AG = 4
HT1 = 4
NEG = -1e30

C_ID, C_ID0, C_NM1 = 0, 128, 256
C_LM = 384
C_COS = C_LM + 64 * NL
C_SIN = C_COS + CH * 2 * AD
C_CAUSAL = C_SIN + CH * 2 * AD
C_RESET = C_CAUSAL + 128
C_END = C_RESET + G * E

ATANH = [1.0 / k for k in (15, 13, 11, 9, 7, 5, 3)]

A_MOST = 80.0
NORMS = ((0, G), (0, CH), (0, CH), (CH, G), (CH, G), (0, G), (0, G))
N_LN, N_HT, N_RT = len(NORMS), 4, 2
UNITS = G * AG
N_UP = HT1 * (E + 2)
N_DOWN = E + 2
DVE_FIRST, POOL_FIRST = (0, 1, 2), (3,)
FIRST_ORDER = (3, 0, 1, 2)
GATE_BANK = (6, 5)
PAIR_BANK = (6, 7, 4, 7, 4, 5, 7, 4)
UP_ORDER = (*range(E, E + 4), *range(E), E + 4, E + 5)
AHEAD = 4
DOWN0 = (4, 0, 2, 4)
ARENA = 34816

DVE_STEPS = 76
DVE_STEPS2 = 173
POOL_STEPS = 2
POOL_STEPS2 = 1


def constants():
    c = np.zeros((P, C_END), np.float32)
    i = np.arange(P)
    c[:, C_ID:C_ID + P] = np.eye(P)
    c[:, C_ID0:C_ID0 + P] = np.eye(P)
    c[0, C_ID0] = 0
    c[i[0::2], C_NM1 + i[1::2]] = -1
    for l, n in enumerate(LEVELS):
        even = i[(i // n) % 2 == 0]
        row = i[:, None] // n
        c[:, C_LM + 64 * l:C_LM + 64 * (l + 1)] = -((row % 2 == 1) & (even[None, :] // n == row - 1)).astype(np.float32)
    inv_freq = np.float32(10000.0) ** (-(np.arange(0, AD, 2, dtype=np.float32) / np.float32(AD)))
    theta = np.arange(SEQ, dtype=np.float32)[:, None] * inv_freq[None, :].astype(np.float32)
    cos, sin = np.repeat(np.cos(theta), 2, 1), np.repeat(np.sin(theta), 2, 1)
    sin[:, 0::2] *= -1
    for j in range(CH):
        for q, scale in enumerate((AD ** -0.5, 1.0)):
            at = (j * 2 + q) * AD
            c[:, C_COS + at:C_COS + at + AD] = cos[j * P:(j + 1) * P] * scale
            c[:, C_SIN + at:C_SIN + at + AD] = sin[j * P:(j + 1) * P] * scale
    c[:, C_CAUSAL:C_CAUSAL + P] = np.where(i[None, :] > i[:, None], NEG, 0)
    c[:, C_RESET:] = 1
    c[:, C_RESET:C_END:E] = 0
    return c


class Steps:

    def __init__(self, engine, sem, seq, per_seq):
        self.engine, self.sem, self.seq, self.per_seq, self.n = engine, sem, seq, per_seq, 0

    def did(self, instruction):
        self.n += 1
        instruction.then_inc(self.sem, 1)

    def settle(self, but=0):
        if self.n > but:
            self.engine.wait_ge(self.sem, self.seq * self.per_seq + self.n - but)


def program(nc, t, out):
    with ExitStack() as ctx:
        def sb(name, shape, dt=F32):
            return ctx.enter_context(nc.sbuf_tensor(name, shape, dt))

        def sem(name):
            return ctx.enter_context(nc.semaphore(name))

        con = sb("con", [P, C_END])
        ident, ident0, nm1 = con[:, C_ID:C_ID + P], con[:, C_ID0:C_ID0 + P], con[:, C_NM1:C_NM1 + P]
        ident_bf = sb("ident_bf", [P, P], BF16)
        causal_bf = sb("causal_bf", [P, AG, P], BF16)
        reset = con[:, C_RESET:C_END]
        half_power = sb("half_power", [P, VH * CH])

        w_ba = sb("w_ba", [P, 2 * VH])
        conv_w = sb("conv_w", [P, MIX, TAPS])
        dt_bias = sb("dt_bias", [P, VH])
        a_log = sb("a_log", [P, VH])
        exp_a = sb("exp_a", [P, 2, VH])
        norm_w = sb("norm_w", [P, 1])

        gate_w = sb("gate_w", [P, E])
        gate_b = sb("gate_b", [P, E])
        w1 = sb("w1", [P, UP0 * P])
        w3 = sb("w3", [P, UP0 * P])
        b1 = sb("b1", [P, UP0])
        b3 = sb("b3", [P, UP0])
        w2 = sb("w2", [P, E + 1, P])
        w2r = sb("w2r", [P, E // 2 + 1, P])
        b2 = sb("b2", [E + 1, P])

        ln_gb = sb("ln_gb", [P, 4])
        a_wqkv = sb("a_wqkv", [P, 3 * P])
        a_wo = sb("a_wo", [P, P])
        a_w1 = sb("a_w1", [P, HT1 * P])
        a_b1 = sb("a_b1", [P, HT1])
        a_w2 = sb("a_w2", [P, HT1, P])
        a_b2 = sb("a_b2", [P, P])

        m_up = sb("m_up", [P, E + 1, HT1 * P])
        m_rt = sb("m_rt", [P, E])

        x_ln = sb("x_ln", [P, CH, P])
        x_in = sb("x_in", [P, CH, P])
        x_res = sb("x_res", [P, CH, P])
        h_tok = sb("h_tok", [P, G, P])
        hT = sb("hT", [P, G * P])
        stats = sb("stats", [P, G, 6])
        mv = sb("mv", [P, G, 2])
        var_eps = sb("var_eps", [P, G])
        rstd = sb("rstd", [P, G])

        arena = sb("arena", [P, ARENA])
        taken = {1: 0, 2: 0}

        def carve(phase, shape, at=None):
            n = int(np.prod(shape))
            if at is None:
                at = taken[phase]
            taken[phase] = max(taken[phase], at + n)
            assert at + n <= ARENA
            names = "abcd"[:len(shape)]
            v = arena[:, at:at + n]
            if len(shape) == 1:
                return v
            return v.rearrange(f"p ({' '.join(names)}) -> p {' '.join(names)}", **dict(zip(names[1:], shape[1:])))

        w_mix = carve(1, [MIX * P])
        w_z = carve(1, [VH * DH])
        w_out = carve(1, [V_TILES, P])
        conv_next = carve(1, [2 * QK_TILES, SEQ])
        mix = carve(1, [MIX, SEQ])
        z_silu = carve(1, [CH, VH * DH])
        exp_in = sb("exp_in", [P, CH, 2 * VH])
        exp_out = sb("exp_out", [P, CH, 2 * VH])
        pre = sb("pre", [P, CH, VH])
        sp_s = sb("sp_s", [P, CH, VH])
        sp_z = sb("sp_z", [P, CH, VH])
        sp_p = sb("sp_p", [P, CH, VH])
        beta = sb("beta", [P, CH, VH])
        decay = sb("decay", [P, CH, VH])
        log_decay = sb("log_decay", [P, CH, VH])
        decT = sb("decT", [VH, P])
        gamT = sb("gamT", [P, P])
        pad = sb("pad", [P, 1])
        zerosT = sb("zerosT", [VH, P])
        gam = sb("gam", [P, VH])
        dmat_all = carve(1, [NB, BATCH, P])
        at_all = carve(1, [NB, BATCH, P])
        pt_all = carve(1, [NB, BATCH, P])
        um_all = carve(1, [NB, BATCH, P])
        dmat = [dmat_all[:, b, :, :] for b in range(NB)]
        at = [at_all[:, b, :, :] for b in range(NB)]
        pt = [pt_all[:, b, :, :] for b in range(NB)]
        um = [um_all[:, b, :, :] for b in range(NB)]
        tm = [carve(1, [BATCH, P // 2]) for b in range(NB)]
        xm = [[carve(1, [BATCH, P]) for b in range(2)] for l in range(NL)]
        qk_raw = [carve(1, [BATCH // 2, P]) for b in range(NB)]
        k_tok = carve(1, [QK_TILES, P])
        v_tok = carve(1, [CH, VH, DH])
        eps = carve(1, [VH, DH])
        w_eps = carve(1, [VH, DH])
        state = carve(1, [QK_TILES, P])
        kstate = w_eps
        qstate = carve(1, [VH, DH])
        hz = z_silu[:, :, :].rearrange("p c (h d) -> p c h d", d=DH)
        hsq = eps
        ssq = sb("ssq", [P, VH])
        o_rstd = sb("o_rstd", [P, VH])
        hzT = w_eps[:, :, :].rearrange("p (m a) d -> p m (a d)", a=2)

        logit = sb("logit", [P, G, E])
        rmax = sb("rmax", [P, G])
        rexp = sb("rexp", [P, G, E])
        rsum = sb("rsum", [P, G])
        score = sb("score", [P, G, E])
        biased = sb("biased", [P, G, E])
        top = sb("top", [P, G, 8])
        over2 = sb("over2", [P, G, E])
        is2 = sb("is2", [P, G, E])
        rank = sb("rank", [P, G, E])
        room = sb("room", [P, G])
        rw = sb("rw", [P, G, E + 1])
        rwT = sb("rwT", [E + 1, G * P])
        hid0 = carve(2, [UP0, G * P])
        gate3 = [carve(2, [G * P]) for _ in range(4)]
        prod = [carve(2, [2, G * P]) for _ in range(2)]
        qk_tok = carve(2, [G * 2, AH, AP], at=0).rearrange("p (c q) h d -> p c q h d", q=2)
        qT = carve(2, [AG, G * P], at=G * 2 * AH * AP)
        kT = carve(2, [AG, G * P], at=G * 2 * AH * AP + AG * G * P)
        shifted = [carve(2, [CH, AG, P]) for _ in range(2)]
        probs = [carve(2, [CH, AG, P]) for _ in range(2)]
        probsT = [carve(2, [CH, AG, P]) for _ in range(2)]
        rot = carve(2, [2, AH, AD])
        rot2 = carve(2, [2, AH, AD])
        a_out = carve(2, [G, AH, AD])
        a_outT = carve(2, [G * P])
        pair_in = carve(2, [G, P])
        x2 = carve(2, [G, P])
        h0 = carve(2, [G, P])
        xp = carve(2, [G, P])
        hid1 = [carve(2, [HT1, G * P]) for _ in range(2)]
        act_pad = sb("act_pad", [P, 1])
        pool_pad = sb("pool_pad", [P, 3])
        hT0 = carve(2, [G * P])
        m_down = carve(2, [E + 1, HT1, P])
        v_aug = carve(2, [G, AH, AD + 1])
        smax = sb("smax", [P, 2, AG])
        a_den = sb("a_den", [P, G, AH])

        ps = ctx.enter_context(nc.psum_tensor("ps", [P, 8, 512], F32))

        names = (
            "consts_in small_in w_a_in w_b_in w_c_in w_d_in m_down_in setup_pool setup_dve setup_act "
            "alog_split "
            "act_step dve_step pool_step pro_step pro_step_pool dve_step2 pool_step2 "
            "x_loaded ln_loaded x_updated x1_stored d_ln_var d_ln_rstd d_h_ready d_hT_psum d_hT_ready "
            "ba_psum exp_in_ready exp_done logdec_ready decay_ready beta_ready mix_psum seeded "
            "conv_done qk_silu qk_out v_silu z_psum z_done decT_psum gamT_ready gam_psum gam_ready "
            "ktok_psum ktok_ready vtok_psum vtok_ready diag_ready arow_psum scan_done kk_psum at_ready "
            "pt_ready u_first u_first_pool t_psum t_ready x_psum x_ready merged u_psum u_ready s_psum "
            "s_ready ks_psum r_ready e_psum e_ready we_ready qs_psum qs_done o_psum hz_ready hz_sq "
            "o_var o_rstd_ready hn_ready hzT_psum gate_tokens_ready hzT_ready y_psum "
            "pair_loaded ln_var ln_rstd norm_scaled h_ready hT_psum hT_ready "
            "lg_psum shift_ready rexp_done rw_ready rwT_psum rwT_ready "
            "up_psum gate_done prod_ready hid_ready down_psum "
            "qkv_psum rot_ready vaug_ready qkT_psum qT_ready s_scores a_shifted shifted_ready "
            "probs_ready pT_psum pT_ready av_psum aout_ready aoT_psum aoT_ready wo_psum xp_ready h_pool "
            "mup_psum mgelu mdown_psum mlp_added mdown_used x_final x_stored "
        ).split()
        s = {n: sem(n) for n in names}

        block = ctx.enter_context(nc.Block())

        def even_odd(ap, n, odd):
            return ap.rearrange("p h (b r n) -> p h b r n", r=2, n=n)[:, :, :, odd, :]

        def even_odd1(ap, n, odd):
            return ap.rearrange("p (b r n) -> p b r n", r=2, n=n)[:, :, odd, :]

        def blocks(ap, n):
            return ap.rearrange("p (h b n) -> p h b n", h=BATCH, n=n)

        def over_heads(ap, n):
            return ap.unsqueeze(1).to_broadcast([ap.shape[0], n, ap.shape[1]])

        def over_last(ap, n):
            return ap.unsqueeze(2).to_broadcast([ap.shape[0], ap.shape[1], n])

        def over_last3(ap, n):
            return ap.unsqueeze(3).to_broadcast([ap.shape[0], ap.shape[1], ap.shape[2], n])

        def tokens(dram, seq):
            return dram[bass.ds(seq, 1), :, :].rearrange("a (c p) d -> p (a c) d", p=P)

        def pair(dram, i):
            return dram[bass.ds(2 * i, 2), :, :].rearrange("a (c p) d -> p (a c) d", p=P)

        def conv_tile(m):
            return conv_next[:, m, :] if m < 2 * QK_TILES else mix[:, m, :]

        def unit(u):
            return u // (CH * AG), u // AG % CH, u % AG

        def khead(k):
            return k % QK_TILES, DH * (k // QK_TILES)

        @block.sync
        def _(sp):
            sp.dma_start(con[:, :], t["consts"]).then_inc(s["consts_in"], 16)
            sp.dma_start(x_ln[:, :, :], tokens(t["x"], 0)).then_inc(s["ln_loaded"], 16)
            sp.dma_start(w_ba[:, :], t["w_ba"]).then_inc(s["w_a_in"], 16)
            sp.dma_start(w_mix, t["w_mix"]).then_inc(s["w_a_in"], 16)
            sp.dma_start(w_z, t["w_z"]).then_inc(s["w_a_in"], 16)
            sp.dma_start(w_out[:, :, :], t["w_out"]).then_inc(s["w_a_in"], 16)
            sp.dma_start(x_in[:, :, :], tokens(t["x"], 0)).then_inc(s["x_loaded"], 16)
            sp.wait_ge(s["d_h_ready"], 1)
            sp.dma_start(x_ln[:, :, :], tokens(t["x"], 1)).then_inc(s["ln_loaded"], 16)

            def delta_rule(it, ahead):
                if ahead > 1:
                    sp.wait_ge(s["d_h_ready"], it + 2)
                    sp.dma_start(x_ln[:, :, :], tokens(t["x"], it + 2)).then_inc(s["ln_loaded"], 16)
                sp.wait_ge(s["x_updated"], CH * it + CH + 1)
                sp.dma_start(tokens(out, it), x_res[:, :, :]).then_inc(s["x1_stored"], 16)
                if ahead > 0:
                    sp.dma_start(x_in[:, :, :], tokens(t["x"], it + 1)).then_inc(s["x_loaded"], 16)

            with sp.Fori(0, SEQS - 2) as it:
                delta_rule(it, 2)
            delta_rule(SEQS - 2, 1)
            delta_rule(SEQS - 1, 0)
            sp.wait_ge(s["x1_stored"], 16 * SEQS + 1)
            sp.dma_start(pair_in[:, :, :], pair(out, 0)).then_inc(s["pair_loaded"], 16)
            sp.dma_start(m_down[:, 0, :, :], t["shared_down"]).then_inc(s["m_down_in"], 16)
            sp.dma_start(m_down[:, 1:E + 1, :, :], t["routed_down"]).then_inc(s["m_down_in"], 16)
            with sp.Fori(0, PAIRS - 1) as it:
                sp.wait_ge(s["merged"], G * it + G)
                sp.dma_start(pair_in[:, :, :], pair(out, it + 1)).then_inc(s["pair_loaded"], 16)
                sp.wait_ge(s["x_final"], it + 2)
                sp.dma_start(pair(out, it), x2[:, :, :]).then_inc(s["x_stored"], 16)
            sp.wait_ge(s["x_final"], PAIRS + 1)
            sp.dma_start(pair(out, PAIRS - 1), x2[:, :, :]).then_inc(s["x_stored"], 16)
            sp.wait_ge(s["x_stored"], 16 * PAIRS + 1)

        @block.gpsimd
        def _(pool):
            for dst, name in ((w1[:, :], "w1"), (w3[:, :], "w3"), (b1[:, :], "b1"), (b3[:, :], "b3"),
                              (w2[:, :, :], "w2"), (w2r[:, :, :], "w2r"), (b2[:, :], "b2"), (gate_w[:, :], "gate_w")):
                pool.dma_start(dst, t[name]).then_inc(s["w_b_in"], 16)
            pool.dma_start(gate_b[:, :], t["gate_b"].partition_broadcast(P)).then_inc(s["w_b_in"], 16)
            pool.memset(half_power[:, :], -0.5)
            pool.memset(pool_pad[:, 0:1], 0.0).then_inc(s["x_updated"], 1)
            pool.memset(x_res[:, :, :], 0.0).then_inc(s["x1_stored"], 1)
            pool.memset(pool_pad[:, 1:2], 0.0).then_inc(s["x_stored"], 1)
            pool.memset(pool_pad[:, 2:3], 0.0).then_inc(s["x_final"], 1)
            pool.memset(act_pad[:, :], 0.0).then_inc(s["act_step"], 1)
            pool.memset(rw[:, :, E:E + 1], 1.0)
            pool.memset(gamT[:, :], 0.0)
            pool.memset(zerosT[:, :], 0.0).then_inc(s["setup_pool"], 1)
            for l in range(NL):
                for b in range(2):
                    pool.memset(xm[l][b][:, :, :], 0.0).then_inc(s["setup_pool"], 1)
            pool.wait_ge(s["w_a_in"], 64)
            pool.wait_ge(s["small_in"], 16 * 6)
            pool.tensor_scalar(w_out[:, :, :], w_out[:, :, :], norm_w[:, 0:1], None, ALU.mult)\
                .then_inc(s["norm_scaled"], 1)
            pool.wait_ge(s["consts_in"], 16)

            def inverse_root_of_norm(i):
                pool.wait_ge(s["d_ln_var"], i + 1)
                pool.tensor_tensor(rstd[:, 0:CH], var_eps[:, 0:CH], half_power[:, 0:CH], ALU.pow)\
                    .then_inc(s["d_ln_rstd"], 1)

            def diagonal(c, b):
                pool.tensor_tensor(dmat[b], over_heads(ident, BATCH),
                                   over_last(beta[:, c, BATCH * b:BATCH * (b + 1)], P), ALU.mult)\
                    .then_inc(s["diag_ready"], 1)

            def first_blocks(me, i, c):
                for b in POOL_FIRST:
                    pool.wait_ge(s["at_ready"], i * CH * NB + NB * c + FIRST_ORDER.index(b) + 1)
                    me.did(pool.tensor_tensor(um[b], at[b], over_heads(nm1, BATCH), ALU.mult))
                    me.settle()
                    pool.tensor_tensor(um[b], um[b], over_heads(ident, BATCH), ALU.add).then_inc(s["u_first_pool"], 1)

            def score_products(i, c):
                for k, b in enumerate(FIRST_ORDER):
                    pool.wait_ge(s["qk_out"], i * CH * NB + NB * c + k + 1)
                    pool.wait_ge(s["scan_done"], i * CH * NB + NB * c + k + 1)
                    pool.tensor_tensor(pt[b].rearrange("p (k v) n -> p k v n", k=2),
                                       qk_raw[b].unsqueeze(2).to_broadcast([P, 2, 2, P]),
                                       dmat[b].rearrange("p (k v) n -> p k v n", k=2), ALU.mult).then_inc(s["pt_ready"], 1)

            def delta_rule(it, more):
                me = Steps(pool, s["pool_step"], it, POOL_STEPS)
                i = it + 1
                if more:
                    inverse_root_of_norm(i)
                for b in range(NB):
                    pool.wait_ge(s["e_ready"], it * CH * NB + b + 1)
                    hs = slice(BATCH * b, BATCH * (b + 1))
                    pool.tensor_tensor(w_eps[:, hs, :], eps[:, hs, :],
                                       dmat[b][:, :, P - 1:P].to_broadcast([P, BATCH, DH]), ALU.mult)\
                        .then_inc(s["we_ready"], 1)
                for b in FIRST_ORDER:
                    pool.wait_ge(s["we_ready"], it * NB + b + 1)
                    diagonal(1, b)
                first_blocks(me, it, 1)
                score_products(it, 1)
                pool.wait_ge(s["o_var"], it * CH + 1)
                pool.tensor_tensor(o_rstd[:, :], ssq[:, :], half_power[:, 0:VH], ALU.pow).then_inc(s["o_rstd_ready"], 1)
                if more:
                    pool.wait_ge(s["beta_ready"], i + 1)
                    for k, b in enumerate(FIRST_ORDER):
                        pool.wait_ge(s["at_ready"], i * CH * NB - NB + k + 1)
                        pool.wait_ge(s["pt_ready"], i * CH * NB - NB + k + 1)
                        diagonal(0, b)
                pool.wait_ge(s["o_var"], it * CH + 2)
                pool.tensor_tensor(o_rstd[:, :], ssq[:, :], half_power[:, 0:VH], ALU.pow).then_inc(s["o_rstd_ready"], 1)
                if more:
                    first_blocks(me, i, 0)
                    score_products(i, 0)
                    assert me.n == POOL_STEPS, ("POOL_STEPS", me.n)

            me = Steps(pool, s["pro_step_pool"], 0, 0)
            inverse_root_of_norm(0)
            pool.wait_ge(s["beta_ready"], 1)
            for b in FIRST_ORDER:
                diagonal(0, b)
            first_blocks(me, 0, 0)
            score_products(0, 0)
            with pool.Fori(0, SEQS - 1) as it:
                delta_rule(it, True)
            delta_rule(SEQS - 1, False)

            def inverse_root(i, k):
                lo, hi = NORMS[k]
                pool.wait_ge(s["ln_var"], i * N_LN + k + 1)
                pool.tensor_tensor(rstd[:, lo:hi], var_eps[:, lo:hi], half_power[:, lo:hi], ALU.pow)\
                    .then_inc(s["ln_rstd"], 1)

            def pair_layers(it, more):
                me = Steps(pool, s["pool_step2"], it, POOL_STEPS2)
                for k in range(1, 6):
                    inverse_root(it, k)
                pool.wait_ge(s["xp_ready"], it + 1)
                me.did(pool.tensor_tensor(x2[:, :, :], x2[:, :, :], xp[:, :, :], ALU.add))
                me.settle()
                pool.tensor_tensor(x2[:, :, :], x2[:, :, :], over_heads(a_b2[:, :], G), ALU.add)\
                    .then_inc(s["h_pool"], 1)
                inverse_root(it, 6)
                pool.wait_ge(s["h_ready"], it * N_LN + 7)
                pool.tensor_tensor(x2[:, :, :], x2[:, :, :], h_tok[:, :, :], ALU.add).then_inc(s["h_pool"], 1)
                if more:
                    inverse_root(it + 1, 0)
                    assert me.n == POOL_STEPS2, ("POOL_STEPS2", me.n)

            inverse_root(0, 0)
            pool.memset(v_aug[:, :, :, AD:AD + 1], 1.0)
            with pool.Fori(0, PAIRS - 1) as it:
                pair_layers(it, True)
            pair_layers(PAIRS - 1, False)

        @block.scalar
        def _(act):
            act.dma_start(conv_w[:, :, :], t["conv_w"]).then_inc(s["small_in"], 16)
            act.dma_start(dt_bias[:, :], t["dt_bias"].partition_broadcast(P)).then_inc(s["small_in"], 16)
            act.dma_start(a_log[:, :], t["A_log"].partition_broadcast(P)).then_inc(s["small_in"], 16)
            for j in range(2):
                act.dma_start(norm_w[DH * j:DH * (j + 1), :], t["norm_weight"].rearrange("(d a) -> d a", a=1))\
                    .then_inc(s["small_in"], 16)
            act.dma_start(a_b1[:, :], t["a_b1"]).then_inc(s["small_in"], 16)
            for j, name in enumerate(("ln1_g", "ln1_b", "ln2_g", "ln2_b")):
                act.dma_start(ln_gb[:, j:j + 1], t[name].rearrange("(d a) -> d a", a=1)).then_inc(s["w_c_in"], 16)
            act.dma_start(a_wqkv[:, :], t["a_wqkv"]).then_inc(s["w_c_in"], 16)
            act.dma_start(a_wo[:, :], t["a_wo"]).then_inc(s["w_c_in"], 16)
            act.dma_start(a_w1[:, :], t["a_w1"]).then_inc(s["w_c_in"], 16)
            act.dma_start(a_w2[:, :, :], t["a_w2"]).then_inc(s["w_c_in"], 16)
            act.dma_start(a_b2[:, :], t["a_b2"].partition_broadcast(P)).then_inc(s["w_c_in"], 16)
            act.dma_start(m_up[:, 0, :], t["shared_up"][0, :, :]).then_inc(s["w_d_in"], 16)
            act.dma_start(m_up[:, 1:E + 1, :], t["routed_up"]).then_inc(s["w_d_in"], 16)
            act.dma_start(m_rt[:, :], t["router_w"]).then_inc(s["w_d_in"], 16)
            act.wait_ge(s["small_in"], 16 * 6)
            act.wait_ge(s["alog_split"], 2)
            act.activation(exp_a[:, :, :], exp_a[:, :, :], ACT.Exp).then_inc(s["setup_act"], 1)

            def turned_norm(i):
                act.wait_ge(s["d_hT_psum"], i + 1)
                act.activation(hT[:, 0:SEQ], ps[:, 7, 0:SEQ], ACT.Copy).then_inc(s["d_hT_ready"], 1)

            def keep_for_gate(i):
                act.wait_ge(s["d_hT_ready"], i + 1)
                act.activation(hT[:, SEQ:2 * SEQ], hT[:, 0:SEQ], ACT.Copy).then_inc(s["gate_tokens_ready"], 1)

            def raw_scores(i, c):
                for k, b in enumerate(FIRST_ORDER):
                    act.wait_ge(s["kk_psum"], i * CH * NB + NB * c + k + 1)
                    act.activation(qk_raw[b], ps[:, b, :].rearrange("p (k q n) -> p k q n", k=2, q=2)[:, :, 1, :],
                                   ACT.Copy).then_inc(s["qk_out"], 1)

            def exponentials(i):
                act.wait_ge(s["exp_in_ready"], i + 1)
                act.activation(exp_out[:, :, :], exp_in[:, :, :], ACT.Exp).then_inc(s["exp_done"], 1)

            def decays(i):
                act.wait_ge(s["logdec_ready"], i + 1)
                act.activation(decay[:, :, :], log_decay[:, :, :], ACT.Exp).then_inc(s["decay_ready"], 1)

            def seed(i, p, bank):
                act.wait_ge(s["mix_psum"], i * NP + p + 1)
                for j in range(2):
                    m = 2 * p + j
                    act.activation(conv_tile(m), ps[:, bank, j * SEQ:(j + 1) * SEQ], ACT.Copy,
                                   scale=conv_w[:, m, TAPS - 1:TAPS]).then_inc(s["seeded"], 1)

            def silu_v(i):
                for p in range(QK_TILES, NP):
                    act.wait_ge(s["conv_done"], i * NP + p + 1)
                    act.activation(mix[:, 2 * p:2 * p + 2, :], mix[:, 2 * p:2 * p + 2, :], ACT.Silu)\
                        .then_inc(s["v_silu"], 1)

            def silu_qk(i):
                for p in range(QK_TILES):
                    act.activation(mix[:, 2 * p:2 * p + 2, :], conv_next[:, 2 * p:2 * p + 2, :], ACT.Silu)\
                        .then_inc(s["qk_silu"], 1)

            def v_tokens(i, c):
                act.wait_ge(s["vtok_psum"], i * CH + c + 1)
                for j in range(2):
                    act.activation(v_tok[:, c, 8 * j:8 * (j + 1), :],
                                   ps[:, 4 + j, :].rearrange("p (a b) -> p a b", b=DH), ACT.Copy)\
                        .then_inc(s["vtok_ready"], 1)

            def gate(i, c):
                for j in range(2):
                    act.wait_ge(s["z_psum"], i * 2 * CH + 2 * c + j + 1)
                    act.activation(z_silu[:, c, 512 * j:512 * (j + 1)], ps[:, GATE_BANK[c] + j, :], ACT.Silu)\
                        .then_inc(s["z_done"], 1)

            def delta_rule(it, more):
                i = it + 1

                def level(c, l):
                    n = LEVELS[l]
                    for b in range(NB):
                        act.wait_ge(s["t_psum"], ((it * CH + c) * NL + l) * NB + b + 1)
                        act.activation(tm[b][:, :, :].rearrange("p h (b n) -> p h b n", n=n),
                                       even_odd(ps[:, b, :].rearrange("p (h m) -> p h m", h=BATCH), n, 0),
                                       ACT.Copy).then_inc(s["t_ready"], 1)

                def solutions(c):
                    for b in range(NB):
                        act.wait_ge(s["e_psum"], it * CH * NB + NB * c + b + 1)
                        act.activation(eps[:, BATCH * b:BATCH * (b + 1), :],
                                       ps[:, b, 0:BATCH * DH].rearrange("p (a b) -> p a b", b=DH), ACT.Copy)\
                            .then_inc(s["e_ready"], 1)

                def squares(c):
                    act.wait_ge(s["hz_ready"], it * CH + c + 1)
                    act.activation(hsq[:, :, :], hz[:, c, :, :], ACT.Square).then_inc(s["hz_sq"], 1)

                def turned_heads(c, j):
                    act.wait_ge(s["hzT_psum"], (it * CH + c) * 2 + j + 1)
                    bank = 6 if c == 0 else 6 + j
                    act.activation(hzT[:, 4 * j:4 * (j + 1), :], ps[:, bank, :].rearrange("p (a b) -> p a b", b=P),
                                   ACT.Copy).then_inc(s["hzT_ready"], 1)

                act.wait_ge(s["ktok_psum"], it + 1)
                act.activation(k_tok[:, :, :], ps[:, 5, :].rearrange("p (a b) -> p a b", b=P), ACT.Copy)\
                    .then_inc(s["ktok_ready"], 1)
                for l in range(NL):
                    level(0, l)
                    if more and l == 2:
                        turned_norm(i)
                    if more and l >= 3:
                        seed(i, l - 3, PAIR_BANK[l - 3])
                solutions(0)
                act.wait_ge(s["s_psum"], it + 1)
                act.activation(state[:, :, :], ps[:, 6, :].rearrange("p (a b) -> p a b", b=P), ACT.Copy)\
                    .then_inc(s["s_ready"], 1)
                if more:
                    seed(i, 3, PAIR_BANK[3])
                raw_scores(it, 1)
                gate(it, 1)
                for l in range(NL):
                    level(1, l)
                    if l == 0:
                        act.wait_ge(s["we_ready"], (it + 1) * NB)
                        squares(0)
                    if l == 3:
                        turned_heads(0, 0)
                    if l == 4:
                        turned_heads(0, 1)
                        if more:
                            keep_for_gate(i)
                    if more and 1 <= l <= 4:
                        seed(i, 3 + l, PAIR_BANK[3 + l])
                    if more and l == 2:
                        exponentials(i)
                if more:
                    decays(i)
                    silu_v(i)
                    act.wait_ge(s["qs_psum"], it + 1)
                    silu_qk(i)
                solutions(1)
                squares(1)
                if more:
                    raw_scores(i, 0)
                    gate(i, 0)
                    v_tokens(i, 0)
                turned_heads(1, 0)
                turned_heads(1, 1)
                if more:
                    v_tokens(i, 1)

            turned_norm(0)
            keep_for_gate(0)
            exponentials(0)
            for p in range(4):
                seed(0, p, p)
            decays(0)
            for p in range(4, NP):
                seed(0, p, p)
            silu_v(0)
            silu_qk(0)
            raw_scores(0, 0)
            gate(0, 0)
            v_tokens(0, 0)
            v_tokens(0, 1)
            with act.Fori(0, SEQS - 1) as it:
                delta_rule(it, True)
            delta_rule(SEQS - 1, False)

            def turned_first(i):
                act.wait_ge(s["hT_psum"], i * N_HT + 1)
                act.activation(hT0, ps[:, 7, :], ACT.Copy).then_inc(s["hT_ready"], 1)

            def pair_layers(it, more):
                def transpose_out(k, gb=None):
                    act.wait_ge(s["hT_psum"], it * N_HT + k + 1)
                    src = ps[:, 7, :]
                    if gb is None:
                        act.activation(hT[:, :], src, ACT.Copy).then_inc(s["hT_ready"], 1)
                    else:
                        act.activation(hT[:, :], src, ACT.Identity, bias=ln_gb[:, 2 * gb + 1:2 * gb + 2],
                                       scale=ln_gb[:, 2 * gb:2 * gb + 1]).then_inc(s["hT_ready"], 1)

                def load_table(function):
                    act.wait_ge(s["act_step"], it * 2 + (1 if function == ACT.Exp else 2))
                    act.activation(act_pad[:, :], act_pad[:, :], function).then_inc(s["act_step"], 1)

                def router(k):
                    act.wait_ge(s["shift_ready"], it * N_RT + k + 1)
                    act.activation(rexp[:, :, :], logit[:, :, :], ACT.Exp).then_inc(s["rexp_done"], 1)

                router(0)
                act.wait_ge(s["w_b_in"], 16 * 9)
                act.wait_ge(s["w_c_in"], 16 * 9)
                for k, i in enumerate(UP_ORDER):
                    act.wait_ge(s["up_psum"], it * UP0 + k + 1)
                    act.activation(gate3[k % 4], ps[:, 2 * (k % 3) + 1, :], ACT.Identity,
                                   bias=b3[:, i:i + 1]).then_inc(s["gate_done"], 1)
                    if k % 2 == 1:
                        act.wait_ge(s["prod_ready"], it * UP0 + k + 1)
                        act.activation(hid0[:, i - 1:i + 1, :], prod[(k // 2) % 2], ACT.Silu)\
                            .then_inc(s["hid_ready"], 1)
                load_table(ACT.Exp)
                transpose_out(1, gb=0)
                for c in range(G):
                    act.wait_ge(s["qkv_psum"], it * G + c + 1)
                    act.activation(v_aug[:, c, :, 0:AD],
                                   ps[:, c, 2 * P:3 * P].rearrange("p (h d) -> p h d", d=AD), ACT.Copy)\
                        .then_inc(s["vaug_ready"], 1)

                def turned_qk(c):
                    act.wait_ge(s["qkT_psum"], it * G + c + 1)
                    for q, dst in enumerate((qT, kT)):
                        act.activation(dst[:, :, c * P:(c + 1) * P],
                                       ps[:, 4 + 2 * (c % 2) + q, :].rearrange("p (g n) -> p g n", n=P), ACT.Copy)\
                            .then_inc(s["qT_ready"], 1)

                def probabilities(u):
                    c = unit(u)[1]
                    act.wait_ge(s["shifted_ready"], it * UNITS + u + 1)
                    act.activation(probs[u % 2][:, 0:c + 1, :, :], shifted[u % 2][:, 0:c + 1, :, :], ACT.Exp)\
                        .then_inc(s["probs_ready"], 1)

                def turned(u):
                    c = unit(u)[1]
                    act.wait_ge(s["pT_psum"], it * UNITS + u + 1)
                    act.activation(probsT[u % 2][:, 0:c + 1, :, :],
                                   ps[:, 4:5 + c, :].rearrange("p k (g n) -> p k g n", n=P), ACT.Copy)\
                        .then_inc(s["pT_ready"], 1)

                turned_qk(0)
                turned_qk(1)
                turned_qk(2)
                for u in range(UNITS):
                    probabilities(u)
                    if u == 0:
                        turned_qk(3)
                    else:
                        turned(u - 1)
                turned(UNITS - 1)
                act.wait_ge(s["aoT_psum"], it + 1)
                act.activation(a_outT, ps[:, 4, :], ACT.Copy).then_inc(s["aoT_ready"], 1)
                load_table(ACT.Gelu)
                transpose_out(2, gb=1)
                for i in range(HT1):
                    act.wait_ge(s["mup_psum"], it * N_UP + i + 1)
                    act.activation(hid1[0][:, i, :], ps[:, i, :], ACT.Gelu, bias=a_b1[:, i:i + 1])\
                        .then_inc(s["mgelu"], 1)
                transpose_out(3)
                router(1)
                for e in range(E + 1):
                    for i in range(HT1):
                        act.wait_ge(s["mup_psum"], it * N_UP + HT1 * (e + 1) + i + 1)
                        act.activation(hid1[e % 2][:, i, :], ps[:, i, :], ACT.Gelu).then_inc(s["mgelu"], 1)
                    if more and e == AHEAD + 1:
                        turned_first(it + 1)

            turned_first(0)
            with act.Fori(0, PAIRS - 1) as it:
                pair_layers(it, True)
            pair_layers(PAIRS - 1, False)

        @block.tensor
        def _(pe):
            pe.wait_ge(s["consts_in"], 16)
            pe.wait_ge(s["setup_pool"], 1 + 2 * NL)
            pe.wait_ge(s["setup_dve"], 2)
            pe.wait_ge(s["w_a_in"], 64)
            pe.wait_ge(s["norm_scaled"], 1)

            def turn_norm(i):
                pe.wait_ge(s["d_h_ready"], i + 1)
                for c in range(CH):
                    mm = pe.transpose(ps[:, 7, c * P:(c + 1) * P], h_tok[:, c, :], ident)
                mm.then_inc(s["d_hT_psum"], 1)

            def beta_decay(i):
                for c in range(CH):
                    mm = pe.matmul(ps[:, 6, 32 * c:32 * (c + 1)], hT[:, c * P:(c + 1) * P], w_ba[:, :],
                                   start=True, stop=True)
                mm.then_inc(s["ba_psum"], 1)

            def project(i, p, bank):
                for j in range(2):
                    m = 2 * p + j
                    mm = pe.matmul(ps[:, bank, j * SEQ:(j + 1) * SEQ], w_mix[:, m * P:(m + 1) * P], hT[:, 0:SEQ],
                                   start=True, stop=True)
                mm.then_inc(s["mix_psum"], 1)

            def chunk_start(i, c, waits=True):
                cs = slice(c * P, (c + 1) * P)
                wave = i * CH * NB + NB * c
                for b in FIRST_ORDER:
                    if waits:
                        pe.wait_ge(s["e_ready"], wave - NB + b + 1)
                    for h in range(BATCH):
                        mm = pe.matmul(ps[:, b, h * P:(h + 1) * P],
                                       decay[:, c, BATCH * b + h:BATCH * b + h + 1].to_broadcast([P, P]), ident0,
                                       start=True, stop=True)
                    mm.then_inc(s["arow_psum"], 1)
                if c == 0:
                    pe.wait_ge(s["qk_silu"], (i + 1) * QK_TILES)
                for n, b in enumerate(FIRST_ORDER):
                    pe.wait_ge(s["scan_done"], wave + n + 1)
                    for k in range(2):
                        m, r = khead(2 * b + k)
                        kk = mix[r:r + DH, QK_TILES + m, cs]
                        pe.matmul(ps[:, b, k * 2 * P:k * 2 * P + P], kk, kk, start=True, stop=True)
                        mm = pe.matmul(ps[:, b, k * 2 * P + P:(k + 1) * 2 * P], kk, mix[r:r + DH, m, cs],
                                       start=True, stop=True)
                    mm.then_inc(s["kk_psum"], 1)

            def v_tokens(i, c):
                for m in range(V_TILES):
                    mm = pe.transpose(ps[:, 4 + m // 4, (m % 4) * P:(m % 4 + 1) * P],
                                      mix[:, 2 * QK_TILES + m, c * P:(c + 1) * P], ident)
                mm.then_inc(s["vtok_psum"], 1)

            def gate(c, j):
                pe.matmul(ps[:, GATE_BANK[c] + j, :], hT[:, SEQ + c * P:SEQ + (c + 1) * P], w_z[:, 512 * j:512 * (j + 1)],
                          start=True, stop=True).then_inc(s["z_psum"], 1)

            def delta_rule(it, more):
                i = it + 1

                def level(c, l, between=None):
                    n = LEVELS[l]
                    step = ((it * CH + c) * NL + l) * NB
                    for b in range(NB):
                        if l > 0:
                            pe.wait_ge(s["u_ready"], step - NB + b + 1)
                        elif b in DVE_FIRST:
                            pe.wait_ge(s["u_first"], (it * CH + c) * len(DVE_FIRST) + DVE_FIRST.index(b) + 1)
                        else:
                            pe.wait_ge(s["u_first_pool"], (it * CH + c) * len(POOL_FIRST) + POOL_FIRST.index(b) + 1)
                        for h in range(BATCH):
                            mm = pe.transpose(ps[:, b, h * P:(h + 1) * P], um[b][:, h, :], ident)
                        mm.then_inc(s["t_psum"], 1)
                    for b in range(NB):
                        pe.wait_ge(s["t_ready"], step + b + 1)
                        for h in range(BATCH):
                            if n == DH and h > 0:
                                mm = pe.matmul(ps[DH:P, b, h * DH:(h + 1) * DH], at[b][0:DH, h, DH:P], tm[b][0:DH, h, :],
                                               start=True, stop=True)
                            else:
                                mm = pe.matmul(ps[:, b, h * DH:(h + 1) * DH], at[b][:, h, :], tm[b][:, h, :],
                                               start=True, stop=True)
                        mm.then_inc(s["x_psum"], 1)
                    if between:
                        between()
                    for b in range(NB):
                        pe.wait_ge(s["x_ready"], step + b + 1)
                        for h in range(BATCH):
                            if n == DH and h > 0:
                                mm = pe.matmul(ps[0:DH, b, h * DH:(h + 1) * DH], xm[l][b % 2][DH:P, h, 0:DH],
                                               um[b][DH:P, h, DH:P], start=True, stop=True)
                            else:
                                mm = pe.matmul(ps[:, b, h * DH:(h + 1) * DH], xm[l][b % 2][:, h, :],
                                               even_odd1(um[b][:, h, :], n, 1), start=True, stop=True)
                        mm.then_inc(s["u_psum"], 1)

                def solve(c):
                    for b in range(NB):
                        pe.wait_ge(s["u_ready"], ((it * CH + c) * NL + NL - 1) * NB + b + 1)
                        if c == 1 and b % 2 == 0:
                            pe.wait_ge(s["r_ready"], it * 2 + b // 2 + 1)
                        for h in range(BATCH):
                            v = BATCH * b + h
                            mm = pe.matmul(ps[:, b, h * DH:(h + 1) * DH], um[b][:, h, :], v_tok[:, c, v, :],
                                           start=True, stop=True)
                        mm.then_inc(s["e_psum"], 1)

                def outputs(c):
                    pe.wait_ge(s["pt_ready"], it * CH * NB + NB * (c + 1))
                    for b in range(NB):
                        pe.wait_ge(s["e_ready"], it * CH * NB + NB * c + b + 1)
                        for h in range(BATCH):
                            v = BATCH * b + h
                            mm = pe.matmul(ps[:, 4 + v // 8, (v % 8) * DH:(v % 8 + 1) * DH], pt[b][:, h, :],
                                           eps[:, v, :], start=True, stop=True)
                    mm.then_inc(s["o_psum"], 1)

                def from_state():
                    pe.wait_ge(s["hz_ready"], it * CH + 1)
                    if more:
                        pe.wait_ge(s["conv_done"], (i + 1) * NP)
                    pe.wait_ge(s["s_ready"], it + 1)
                    for q, (base, done) in enumerate(((4, "ks_psum"), (6, "qs_psum"))):
                        if q == 1:
                            pe.wait_ge(s["x_updated"], it * CH + 2)
                        for k in range(KH):
                            m, r = khead(k)
                            mm = pe.matmul(ps[:, base + k // 4, m * P:(m + 1) * P],
                                           mix[r:r + DH, (QK_TILES if q == 0 else 0) + m, P:2 * P], state[r:r + DH, m, :],
                                           start=True, stop=True)
                        mm.then_inc(s[done], 1)

                def turn_heads(c, j):
                    bank = 6 if c == 0 else 6 + j
                    for m in range(4 * j, 4 * (j + 1)):
                        mm = pe.transpose(ps[:, bank, (m % 4) * P:(m % 4 + 1) * P],
                                          hz[:, c, 2 * m:2 * m + 2, :].rearrange("p a b -> p (a b)"), ident)
                    mm.then_inc(s["hzT_psum"], 1)

                def project_out(c):
                    pe.wait_ge(s["hzT_ready"], (it * CH + c + 1) * 2)
                    for m in range(V_TILES):
                        mm = pe.matmul(ps[:, 6, 0:P], hzT[:, m, :], w_out[:, m, :], start=(m == 0),
                                       stop=(m == V_TILES - 1))
                    mm.then_inc(s["y_psum"], 1)

                pe.wait_ge(s["vtok_ready"], (it + 1) * CH * 2)
                for m in range(QK_TILES):
                    mm = pe.transpose(ps[:, 5, m * P:(m + 1) * P], mix[:, QK_TILES + m, 0:P], ident)
                mm.then_inc(s["ktok_psum"], 1)
                pe.transpose(ps[0:VH, 4, 0:P], decay[:, 1, :], ident).then_inc(s["decT_psum"], 1)
                for l in range(NL):
                    level(0, l)
                    if l == 0:
                        pe.wait_ge(s["gamT_ready"], it + 1)
                        pe.transpose(ps[:, 4, 0:P], gamT[:, :], ident).then_inc(s["gam_psum"], 1)
                    if more and l == 1:
                        turn_norm(i)
                    if more and l == 2:
                        pe.wait_ge(s["d_hT_ready"], i + 1)
                        pe.wait_ge(s["x_updated"], it * CH + 1)
                        project(i, 0, PAIR_BANK[0])
                    if more and l == 3:
                        project(i, 1, PAIR_BANK[1])
                    if l == 4:
                        pe.wait_ge(s["ktok_ready"], it + 1)
                        if more:
                            project(i, 2, PAIR_BANK[2])
                    if more and l == 5:
                        pe.wait_ge(s["conv_done"], i * NP + 2)
                        project(i, 3, PAIR_BANK[3])
                solve(0)
                pe.wait_ge(s["gam_ready"], it + 1)
                if more:
                    pe.wait_ge(s["conv_done"], i * NP + 3)
                outputs(0)
                if not more:
                    pe.wait_ge(s["x_updated"], it * CH + 1)
                for k in range(KH):
                    m, r = khead(k)
                    if k % 2 == 0:
                        pe.wait_ge(s["we_ready"], it * NB + k // 2 + 1)
                    mm = pe.matmul(ps[r:r + DH, 6, m * P:(m + 1) * P], k_tok[:, m, r:r + DH],
                                   w_eps[:, 2 * k:2 * k + 2, :].rearrange("p a b -> p (a b)"), start=True, stop=True)
                mm.then_inc(s["s_psum"], 1)
                chunk_start(it, 1)
                pe.wait_ge(s["hz_ready"], it * CH + 1)
                gate(1, 0)
                pe.wait_ge(s["s_ready"], it + 1)
                gate(1, 1)
                if more:
                    project(i, 4, PAIR_BANK[4])
                for l in range(NL):
                    level(1, l, from_state if l == NL - 1 else None)
                    if l == 0:
                        pe.wait_ge(s["z_done"], (it + 1) * 2 * CH)
                        if more:
                            beta_decay(i)
                    if more and l == 1:
                        project(i, 5, PAIR_BANK[5])
                    if l == 2:
                        if more:
                            pe.wait_ge(s["conv_done"], i * NP + 4)
                            project(i, 6, PAIR_BANK[6])
                            pe.wait_ge(s["exp_in_ready"], i + 1)
                        pe.wait_ge(s["hn_ready"], it * CH + 1)
                        turn_heads(0, 0)
                    if l == 3:
                        pe.wait_ge(s["hzT_ready"], it * CH * 2 + 1)
                        turn_heads(0, 1)
                        if more:
                            pe.wait_ge(s["conv_done"], i * NP + 5)
                            project(i, 7, PAIR_BANK[7])
                    if l == 4:
                        project_out(0)
                solve(1)
                outputs(1)
                if more:
                    pe.wait_ge(s["decay_ready"], i + 1)
                    chunk_start(i, 0)
                pe.wait_ge(s["qs_done"], it + 1)
                if more:
                    pe.wait_ge(s["gate_tokens_ready"], i + 1)
                    gate(0, 0)
                    gate(0, 1)
                    pe.wait_ge(s["hz_ready"], it * CH + 2)
                    pe.wait_ge(s["v_silu"], (i + 1) * QK_TILES)
                    v_tokens(i, 0)
                    pe.wait_ge(s["z_done"], i * 2 * CH + 2)
                pe.wait_ge(s["hn_ready"], it * CH + 2)
                turn_heads(1, 0)
                turn_heads(1, 1)
                if more:
                    pe.wait_ge(s["vtok_ready"], i * CH * 2 + 2)
                    v_tokens(i, 1)
                project_out(1)

            turn_norm(0)
            pe.wait_ge(s["d_hT_ready"], 1)
            beta_decay(0)
            for p in range(NP):
                if p == 6:
                    pe.wait_ge(s["exp_in_ready"], 1)
                project(0, p, p)
            pe.wait_ge(s["decay_ready"], 1)
            pe.wait_ge(s["conv_done"], NP)
            chunk_start(0, 0, waits=False)
            pe.wait_ge(s["gate_tokens_ready"], 1)
            gate(0, 0)
            gate(0, 1)
            pe.wait_ge(s["v_silu"], QK_TILES)
            v_tokens(0, 0)
            pe.wait_ge(s["vtok_ready"], 2)
            v_tokens(0, 1)
            with pe.Fori(0, SEQS - 1) as it:
                delta_rule(it, True)
            delta_rule(SEQS - 1, False)

            def turn_first(i):
                pe.wait_ge(s["h_ready"], i * N_LN + 1)
                for c in range(G):
                    mm = pe.transpose(ps[:, 7, c * P:(c + 1) * P], h_tok[:, c, :], ident)
                mm.then_inc(s["hT_psum"], 1)

            def pair_layers(it, more):
                def turn_tokens(k, src, ln):
                    pe.wait_ge(s["h_ready"], it * N_LN + ln + 1)
                    for c in range(G):
                        mm = pe.transpose(ps[:, 7, c * P:(c + 1) * P], src[:, c, :], ident)
                    mm.then_inc(s["hT_psum"], 1)
                    pe.wait_ge(s["hT_ready"], it * N_HT + k + 1)

                def route(src, w):
                    for c in range(G):
                        mm = pe.matmul(ps[:, 6, E * c:E * (c + 1)], src[:, c * P:(c + 1) * P], w, start=True, stop=True)
                    mm.then_inc(s["lg_psum"], 1)

                pe.wait_ge(s["w_b_in"], 16 * 9)
                pe.wait_ge(s["hT_ready"], it * N_HT + 1)
                route(hT0, gate_w[:, :])
                for k, i in enumerate(UP_ORDER):
                    if k >= 3:
                        pe.wait_ge(s["prod_ready"], it * UP0 + k - 2)
                    if k == 2:
                        pe.wait_ge(s["x_final"], it + 1)
                    for j, w in enumerate((w1, w3)):
                        mm = pe.matmul(ps[:, 2 * (k % 3) + j, :], w[:, i * P:(i + 1) * P], hT0, start=True, stop=True)
                    mm.then_inc(s["up_psum"], 1)
                pe.wait_ge(s["rw_ready"], it * N_RT + 1)
                for c in range(G):
                    mm = pe.transpose(ps[0:E + 1, 6, c * P:(c + 1) * P], rw[:, c, :], ident)
                mm.then_inc(s["rwT_psum"], 1)
                pe.wait_ge(s["prod_ready"], it * UP0 + UP0 - 2)
                for c in range(G):
                    cs = slice(c * P, (c + 1) * P)
                    if c == 3:
                        pe.wait_ge(s["merged"], it * G + 1)
                    for e in range(E):
                        if c == 0 and e % 2 == 0:
                            pe.wait_ge(s["hid_ready"], it * UP0 // 2 + 3 + e // 2)
                        o = ps[:, DOWN0[c] + e % 2, (e // 2) * P:(e // 2 + 1) * P]
                        r = DH * (e % 2)
                        pe.matmul(o, hid0[:, e, cs], w2[:, e, :], start=True, stop=False)
                        pe.matmul(o, hid0[r:r + H1R, E + e // 2, cs], w2r[r:r + H1R, e // 2, :], start=False, stop=True)
                    if c == 0:
                        pe.wait_ge(s["hid_ready"], (it + 1) * UP0 // 2)
                        pe.wait_ge(s["rwT_ready"], it + 1)
                    if c >= 2:
                        pe.wait_ge(s["merged"], it * G + c - 1)
                    o = ps[:, 7 - c % 2, 0:P]
                    pe.matmul(o, hid0[:, E + 4, cs], w2[:, E, :], start=True, stop=False)
                    pe.matmul(o, hid0[0:H1R, E + 5, cs], w2r[0:H1R, E // 2, :], start=False, stop=False)
                    pe.matmul(o, rwT[:, cs], b2[:, :], start=False, stop=True).then_inc(s["down_psum"], 1)
                turn_tokens(1, h_tok, 4)
                pe.wait_ge(s["w_c_in"], 16 * 9)
                for c in range(G):
                    pe.matmul(ps[:, c, 0:3 * P], hT[:, c * P:(c + 1) * P], a_wqkv[:, :], start=True, stop=True)\
                        .then_inc(s["qkv_psum"], 1)

                def turn_qk(c):
                    pe.wait_ge(s["rot_ready"], it * G + c + 1)
                    if c >= 2:
                        pe.wait_ge(s["qT_ready"], (it * G + c - 1) * 2)
                    for q in range(2):
                        for g in range(AG):
                            mm = pe.transpose(ps[:, 4 + 2 * (c % 2) + q, g * P:(g + 1) * P],
                                              qk_tok[:, c, q, AG * g:AG * (g + 1), :].rearrange("p h d -> p (h d)"),
                                              ident)
                    mm.then_inc(s["qkT_psum"], 1)

                def scores(u):
                    sq, c, j = unit(u)
                    if u >= 2:
                        pe.wait_ge(s["shifted_ready"], it * UNITS + u - 1)
                    if j == 0:
                        pe.wait_ge(s["qT_ready"], (it * G + sq * CH + c + 1) * 2)
                    queries = slice((sq * CH + c) * P, (sq * CH + c + 1) * P)
                    for kc in range(c + 1):
                        bank = 2 * (u % 2) + kc
                        keys = slice((sq * CH + kc) * P, (sq * CH + kc + 1) * P)
                        diagonal = kc == c
                        if diagonal:
                            pe.matmul(ps[:, bank, :], ident_bf[:, :], causal_bf[:, :, :].rearrange("p g n -> p (g n)"),
                                      start=True, stop=False, skip_group_check=True)
                        for g in range(AG):
                            mm = pe.matmul(ps[:, bank, g * P:(g + 1) * P], qT[32 * j:32 * j + AD, g, queries],
                                           kT[32 * j:32 * j + AD, g, keys],
                                           start=not diagonal, stop=True, skip_group_check=True)
                    mm.then_inc(s["s_scores"], 1)

                def turn_probs(u):
                    c = unit(u)[1]
                    pe.wait_ge(s["probs_ready"], it * UNITS + u + 1)
                    if u == 0:
                        pe.wait_ge(s["qT_ready"], (it * G + 3) * 2)
                    if u >= 1:
                        pe.wait_ge(s["pT_ready"], it * UNITS + u)
                    for kc in range(c + 1):
                        for g in range(AG):
                            mm = pe.transpose(ps[:, 4 + kc, g * P:(g + 1) * P], probs[u % 2][:, kc, g, :], ident)
                    mm.then_inc(s["pT_psum"], 1)

                def values(u):
                    sq, c, j = unit(u)
                    pe.wait_ge(s["pT_ready"], it * UNITS + u + 1)
                    if u == 0:
                        pe.wait_ge(s["qT_ready"], (it + 1) * G * 2)
                        pe.wait_ge(s["vaug_ready"], (it + 1) * G)
                    for g in range(AG):
                        h = AG * g + j
                        for kc in range(c + 1):
                            mm = pe.matmul(ps[:, 6 + sq, (c * AH + h) * (AD + 1):(c * AH + h + 1) * (AD + 1)],
                                           probsT[u % 2][:, kc, g, :], v_aug[:, sq * CH + kc, h, :],
                                           start=(kc == 0), stop=(kc == c))
                    mm.then_inc(s["av_psum"], 1)

                turn_qk(0)
                turn_qk(1)
                for u in range(UNITS + 2):
                    if u < UNITS:
                        scores(u)
                    if u < 2:
                        turn_qk(2 + u)
                    if 1 <= u <= UNITS:
                        turn_probs(u - 1)
                    if u >= 2:
                        values(u - 2)
                pe.wait_ge(s["aout_ready"], it + 1)
                for c in range(G):
                    mm = pe.transpose(ps[:, 4, c * P:(c + 1) * P],
                                      a_out[:, c, :, :].rearrange("p h d -> p (h d)"), ident)
                mm.then_inc(s["aoT_psum"], 1)
                pe.wait_ge(s["aoT_ready"], it + 1)
                for c in range(G):
                    mm = pe.matmul(ps[:, 0, c * P:(c + 1) * P], a_outT[:, c * P:(c + 1) * P], a_wo[:, :],
                                   start=True, stop=True)
                mm.then_inc(s["wo_psum"], 1)
                turn_tokens(2, h_tok, 5)
                for i in range(HT1):
                    pe.matmul(ps[:, i, :], a_w1[:, i * P:(i + 1) * P], hT[:, :], start=True, stop=True)\
                        .then_inc(s["mup_psum"], 1)
                pe.wait_ge(s["mgelu"], it * N_UP + HT1)
                for c in range(G):
                    for i in range(HT1):
                        mm = pe.matmul(ps[:, 4, c * P:(c + 1) * P], hid1[0][:, i, c * P:(c + 1) * P], a_w2[:, i, :],
                                       start=(i == 0), stop=(i == HT1 - 1))
                mm.then_inc(s["mdown_psum"], 1)
                turn_tokens(3, h_tok, 6)
                pe.wait_ge(s["w_d_in"], 16 * 3)
                pe.wait_ge(s["m_down_in"], 16 * 2)
                route(hT, m_rt[:, :])

                def up(e):
                    for i in range(HT1):
                        if e >= 1:
                            pe.wait_ge(s["mgelu"], it * N_UP + HT1 * e + i + 1)
                        pe.matmul(ps[:, i, :], m_up[:, e, i * P:(i + 1) * P], hT[:, :], start=True, stop=True)\
                            .then_inc(s["mup_psum"], 1)

                def down(e):
                    pe.wait_ge(s["mgelu"], it * N_UP + HT1 * (e + 2))
                    if e >= 2:
                        pe.wait_ge(s["mdown_used"], it * E + e - 1)
                    for c in range(G):
                        for i in range(HT1):
                            mm = pe.matmul(ps[:, 4 + e % 2, c * P:(c + 1) * P], hid1[e % 2][:, i, c * P:(c + 1) * P],
                                           m_down[:, e, i, :], start=(i == 0), stop=(i == HT1 - 1))
                    mm.then_inc(s["mdown_psum"], 1)

                up(0)
                for e in range(E + 1):
                    if e < E:
                        up(e + 1)
                    down(e)
                    if more and e == AHEAD:
                        turn_first(it + 1)

            turn_first(0)
            with pe.Fori(0, PAIRS - 1) as it:
                pair_layers(it, True)
            pair_layers(PAIRS - 1, False)

        @block.vector
        def _(dve):
            dve.wait_ge(s["consts_in"], 16)
            dve.tensor_copy(ident_bf[:, :], ident).then_inc(s["setup_dve"], 1)
            dve.tensor_copy(causal_bf[:, :, :], over_heads(con[:, C_CAUSAL:C_CAUSAL + P], AG)).then_inc(s["setup_dve"], 1)
            dve.wait_ge(s["setup_pool"], 1 + 2 * NL)
            dve.wait_ge(s["small_in"], 16 * 6)
            dve.tensor_scalar(exp_a[:, 0, :], a_log[:, :], A_MOST, None, ALU.min).then_inc(s["alog_split"], 1)
            dve.tensor_scalar(exp_a[:, 1, :], a_log[:, :], A_MOST + 70.0, A_MOST, ALU.min, ALU.subtract)\
                .then_inc(s["a_shifted"], 1)
            dve.wait_ge(s["a_shifted"], 1)
            dve.tensor_scalar(exp_a[:, 1, :], exp_a[:, 1, :], 0.0, None, ALU.max).then_inc(s["alog_split"], 1)
            dve.wait_ge(s["setup_act"], 1)

            def norm_before(me, src, chunks, prefix):
                lo, hi = chunks
                for c in range(lo, hi):
                    me.did(dve.bn_stats(stats[:, c, :], src[:, c, :]))
                me.settle()
                dve.memset(pad[:, :], 0.0)
                for c in range(lo, hi):
                    me.did(dve.bn_aggr(mv[:, c, :], stats[:, c, :]))
                me.settle()
                dve.tensor_scalar(var_eps[:, lo:hi], mv[:, lo:hi, 1], 1e-5, None, ALU.add).then_inc(s[prefix + "ln_var"], 1)

            def norm_after(me, src, dst, chunks, prefix, count):
                dve.wait_ge(s[prefix + "ln_rstd"], count)
                for c in range(*chunks):
                    ins = dve.tensor_scalar(dst[:, c, :], src[:, c, :], mv[:, c, 0:1], rstd[:, c:c + 1],
                                            ALU.subtract, ALU.mult)
                    if c < chunks[1] - 1:
                        me.did(ins)
                ins.then_inc(s[prefix + "h_ready"], 1)

            def prepare(me, i, part):
                if part == 0:
                    dve.wait_ge(s["ln_loaded"], 16 * i + 16)
                    norm_before(me, x_ln, (0, CH), "d_")
                else:
                    norm_after(me, x_ln, h_tok, (0, CH), "d_", i + 1)

            def convolve(me, i, m, bank):
                dve.wait_ge(s["seeded"], i * MIX + 2 * (m // 2) + 2)
                for sh in range(1, TAPS):
                    if sh > 1:
                        me.settle()
                    ins = dve.scalar_tensor_tensor(
                        conv_tile(m)[:, sh:SEQ], ps[:, bank, (m % 2) * SEQ:(m % 2 + 1) * SEQ - sh],
                        conv_w[:, m, TAPS - 1 - sh:TAPS - sh], conv_tile(m)[:, sh:SEQ], ALU.mult, ALU.add)
                    if sh < TAPS - 1 or m % 2 == 0:
                        me.did(ins)
                if m % 2 == 1:
                    ins.then_inc(s["conv_done"], 1)

            def exponents(me, i):
                dve.wait_ge(s["ba_psum"], i + 1)
                ba = ps[:, 6, 0:CH * 2 * VH].rearrange("p (c n) -> p c n", c=CH)
                me.did(dve.tensor_scalar(exp_in[:, :, 0:VH], ba[:, :, 0:VH], -1.0, 88.0, ALU.mult, ALU.min))
                me.did(dve.tensor_tensor(pre[:, :, :], ba[:, :, VH:2 * VH], over_heads(dt_bias[:, :], CH), ALU.add))
                me.settle()
                dve.scalar_tensor_tensor(exp_in[:, :, VH:2 * VH], pre[:, :, :], -1.0, pre[:, :, :], ALU.mult, ALU.min)\
                    .then_inc(s["exp_in_ready"], 1)

            def log_decays(me, i, part):
                u = exp_out[:, :, VH:2 * VH]
                if part == 0:
                    dve.wait_ge(s["exp_done"], i + 1)
                    me.did(dve.tensor_scalar(sp_s[:, :, :], u, 2.0, None, ALU.add))
                    me.did(dve.tensor_scalar(beta[:, :, :], exp_out[:, :, 0:VH], 1.0, None, ALU.add))
                    me.settle(1)
                    me.did(dve.reciprocal(sp_s[:, :, :], sp_s[:, :, :]))
                    me.settle()
                    dve.reciprocal(beta[:, :, :], beta[:, :, :]).then_inc(s["beta_ready"], 1)
                if part == 1:
                    me.did(dve.tensor_tensor(sp_s[:, :, :], sp_s[:, :, :], u, ALU.mult))
                    me.settle()
                    me.did(dve.tensor_tensor(sp_z[:, :, :], sp_s[:, :, :], sp_s[:, :, :], ALU.mult))
                    me.settle()
                    me.did(dve.tensor_scalar(sp_p[:, :, :], sp_z[:, :, :], ATANH[0], None, ALU.mult))
                    for a in ATANH[1:]:
                        me.settle()
                        me.did(dve.scalar_tensor_tensor(sp_p[:, :, :], sp_p[:, :, :], a, sp_z[:, :, :], ALU.add, ALU.mult))
                if part == 2:
                    me.settle()
                    me.did(dve.scalar_tensor_tensor(sp_p[:, :, :], sp_p[:, :, :], 1.0, sp_s[:, :, :], ALU.add, ALU.mult))
                    me.did(dve.tensor_scalar(pre[:, :, :], pre[:, :, :], 0.0, None, ALU.max))
                    me.settle()
                    me.did(dve.scalar_tensor_tensor(sp_p[:, :, :], sp_p[:, :, :], 2.0, pre[:, :, :], ALU.mult, ALU.add))
                    me.settle()
                    me.did(dve.tensor_tensor(log_decay[:, :, :], sp_p[:, :, :], over_heads(exp_a[:, 0, :], CH), ALU.mult))
                    me.settle()
                    me.did(dve.tensor_scalar(log_decay[:, :, :], log_decay[:, :, :], 1e4, -1.0, ALU.min, ALU.mult))
                    me.settle()
                    me.did(dve.tensor_tensor(log_decay[:, :, :], log_decay[:, :, :], over_heads(exp_a[:, 1, :], CH), ALU.mult))
                    me.settle()
                    dve.tensor_scalar(log_decay[:, :, :], log_decay[:, :, :], -200.0, None, ALU.max)\
                        .then_inc(s["logdec_ready"], 1)

            def chunk_scans(i, c):
                wave = i * CH * NB + NB * c
                for k, b in enumerate(FIRST_ORDER):
                    dve.wait_ge(s["diag_ready"], wave + k + 1)
                    dve.wait_ge(s["arow_psum"], wave + k + 1)
                    d = dmat[b].rearrange("p h n -> p (h n)")
                    dve.tensor_tensor_scan(d, ps[:, b, :], d, 0.0, ALU.mult, ALU.add).then_inc(s["scan_done"], 1)

            def chunk_products(me, i, c, b):
                wave = i * CH * NB + NB * c
                dve.wait_ge(s["scan_done"], wave + FIRST_ORDER.index(b) + 1)
                dve.wait_ge(s["qk_out"], wave + FIRST_ORDER.index(b) + 1)
                kk = ps[:, b, :].rearrange("p (k q n) -> p k q n", k=2, q=2)[:, :, 0:1, :]
                dve.tensor_tensor(at[b].rearrange("p (k v) n -> p k v n", k=2), kk.to_broadcast([P, 2, 2, P]),
                                  dmat[b].rearrange("p (k v) n -> p k v n", k=2), ALU.mult).then_inc(s["at_ready"], 1)
                if b in DVE_FIRST:
                    dve.wait_ge(s["at_ready"], wave + FIRST_ORDER.index(b) + 1)
                    me.did(dve.tensor_tensor(um[b], at[b], over_heads(nm1, BATCH), ALU.mult))
                    me.settle()
                    dve.tensor_tensor(um[b], um[b], over_heads(ident, BATCH), ALU.add).then_inc(s["u_first"], 1)

            def delta_rule(it, more):
                me = Steps(dve, s["dve_step"], it, DVE_STEPS)
                i = it + 1

                def level(c, l, between=None):
                    n = LEVELS[l]
                    step = ((it * CH + c) * NL + l) * NB
                    mask = con[:, C_LM + 64 * l:C_LM + 64 * (l + 1)].rearrange("p (b n) -> p b n", n=n)\
                        .unsqueeze(1).to_broadcast([P, BATCH, DH // n, n])
                    for b in range(NB):
                        if b == 2 and between:
                            between()
                        dve.wait_ge(s["x_psum"], step + b + 1)
                        if b >= 2:
                            dve.wait_ge(s["u_psum"], step + b - 1)
                        r = slice(DH, P) if n == DH else slice(0, P)
                        dve.tensor_tensor(even_odd(xm[l][b % 2][r, :, :], n, 0), blocks(ps[r, b, 0:BATCH * DH], n),
                                          mask[r], ALU.mult).then_inc(s["x_ready"], 1)
                    for b in range(NB):
                        dve.wait_ge(s["u_psum"], step + b + 1)
                        r = slice(0, DH) if n == DH else slice(0, P)
                        uo = even_odd(um[b][r], n, 1)
                        dve.tensor_tensor(uo, blocks(ps[r, b, 0:BATCH * DH], n), uo, ALU.add)\
                            .then_inc(s["u_ready"], 1)

                def banks(first):
                    return ps[:, first:first + 2, :].rearrange("p k (h d) -> p (k h) d", d=DH)

                def gated(c):
                    dve.wait_ge(s["o_psum"], it * CH + c + 1)
                    z = z_silu[:, c, :].rearrange("p (h d) -> p h d", d=DH)
                    o = banks(4)
                    if c == 1:
                        me.did(dve.tensor_tensor(qstate[:, :, :], banks(4), qstate[:, :, :], ALU.add))
                        me.settle()
                        o = qstate[:, :, :]
                    dve.scalar_tensor_tensor(hz[:, c, :, :], o, DH ** -0.5, z, ALU.mult, ALU.mult)\
                        .then_inc(s["hz_ready"], 1)

                def sum_squares(c):
                    dve.wait_ge(s["hz_sq"], it * CH + c + 1)
                    me.did(dve.tensor_reduce(ssq[:, :], hsq[:, :, :], X_AXIS, ALU.add))
                    me.settle()
                    dve.tensor_scalar(ssq[:, :], ssq[:, :], 1.0 / DH, 1e-6, ALU.mult, ALU.add).then_inc(s["o_var"], 1)

                def normalise(c):
                    dve.wait_ge(s["o_rstd_ready"], it * CH + c + 1)
                    dve.tensor_tensor(hz[:, c, :, :], hz[:, c, :, :], over_last(o_rstd[:, :], DH), ALU.mult)\
                        .then_inc(s["hn_ready"], 1)

                def residual(c):
                    dve.wait_ge(s["y_psum"], it * CH + c + 1)
                    dve.tensor_tensor(x_res[:, c, :], ps[:, 6, 0:P], x_in[:, c, :], ALU.add)\
                        .then_inc(s["x_updated"], 1)

                g16 = over_last(gam[:, :], DH)

                def take_state():
                    residual(0)
                    dve.wait_ge(s["ks_psum"], it + 1)
                    me.did(dve.tensor_tensor(kstate[:, :, :], banks(4), g16, ALU.mult))
                    me.settle()
                    for j in range(2):
                        hs = slice(8 * j, 8 * (j + 1))
                        dve.tensor_tensor(v_tok[:, 1, hs, :], v_tok[:, 1, hs, :], kstate[:, hs, :], ALU.subtract)\
                            .then_inc(s["r_ready"], 1)

                if more:
                    prepare(me, i, 0)
                dve.wait_ge(s["decT_psum"], it + 1)
                me.did(dve.tensor_copy(decT[:, :], ps[0:VH, 4, 0:P]))
                me.settle()
                dve.tensor_tensor_scan(gamT[0:VH, :], decT[:, :], zerosT[:, :], 1.0, ALU.mult, ALU.add)\
                    .then_inc(s["gamT_ready"], 1)
                for l in range(NL):
                    level(0, l, (lambda: prepare(me, i, 1)) if more and l == 1 else None)
                    if l == 0:
                        dve.wait_ge(s["gam_psum"], it + 1)
                        dve.tensor_copy(gam[:, :], ps[:, 4, 0:VH]).then_inc(s["gam_ready"], 1)
                    if more and l >= 3:
                        for m in (2 * (l - 3), 2 * (l - 3) + 1):
                            convolve(me, i, m, PAIR_BANK[m // 2])
                gated(0)
                chunk_scans(it, 1)
                for b in FIRST_ORDER:
                    chunk_products(me, it, 1, b)
                for l in range(NL):
                    level(1, l, take_state if l == NL - 1 else None)
                    if more and l < NL - 1:
                        for m in (6 + 2 * l, 7 + 2 * l):
                            convolve(me, i, m, PAIR_BANK[m // 2])
                    if l == 0:
                        sum_squares(0)
                    if l == 1:
                        normalise(0)
                    if more and l == 1:
                        exponents(me, i)
                    if more and 2 <= l <= 4:
                        log_decays(me, i, l - 2)
                    if l == NL - 2:
                        dve.wait_ge(s["x1_stored"], 16 * it + 1)
                        dve.wait_ge(s["x_loaded"], 16 * it + 16)
                dve.wait_ge(s["qs_psum"], it + 1)
                dve.tensor_tensor(qstate[:, :, :], banks(6), g16, ALU.mult).then_inc(s["qs_done"], 1)
                dve.wait_ge(s["qs_done"], it + 1)
                gated(1)
                if more:
                    chunk_scans(i, 0)
                sum_squares(1)
                if more:
                    for b in FIRST_ORDER[:2]:
                        chunk_products(me, i, 0, b)
                normalise(1)
                if more:
                    for b in FIRST_ORDER[2:]:
                        chunk_products(me, i, 0, b)
                residual(1)
                if more:
                    assert me.n == DVE_STEPS, ("DVE_STEPS", me.n)

            start = Steps(dve, s["pro_step"], 0, 0)
            prepare(start, 0, 0)
            prepare(start, 0, 1)
            exponents(start, 0)
            for part in range(3):
                log_decays(start, 0, part)
            for m in range(MIX):
                convolve(start, 0, m, m // 2)
            chunk_scans(0, 0)
            for b in FIRST_ORDER:
                chunk_products(start, 0, 0, b)
            with dve.Fori(0, SEQS - 1) as it:
                delta_rule(it, True)
            delta_rule(SEQS - 1, False)

            def first_norm(me, i, part):
                if part == 0:
                    dve.wait_ge(s["pair_loaded"], 16 * i + 16)
                    norm_before(me, pair_in, NORMS[0], "")
                else:
                    norm_after(me, pair_in, h_tok, NORMS[0], "", i * N_LN + 1)

            def pair_layers(it, more):
                me = Steps(dve, s["dve_step2"], it, DVE_STEPS2)

                def norm(k, src, dst):
                    norm_before(me, src, NORMS[k], "")
                    norm_after(me, src, dst, NORMS[k], "", it * N_LN + k + 1)

                def route(k, with_bias):
                    dve.wait_ge(s["lg_psum"], it * N_RT + k + 1)
                    lg = ps[:, 6, 0:G * E].rearrange("p (c e) -> p c e", c=G)
                    me.did(dve.tensor_reduce(rmax[:, :], lg, X_AXIS, ALU.max))
                    me.settle()
                    dve.tensor_tensor(logit[:, :, :], lg, over_last(rmax[:, :], E), ALU.subtract)\
                        .then_inc(s["shift_ready"], 1)
                    dve.wait_ge(s["rexp_done"], it * N_RT + k + 1)
                    me.did(dve.tensor_reduce(rsum[:, :], rexp[:, :, :], X_AXIS, ALU.add))
                    me.settle()
                    me.did(dve.reciprocal(rsum[:, :], rsum[:, :]))
                    me.settle()
                    me.did(dve.tensor_tensor(score[:, :, :], rexp[:, :, :], over_last(rsum[:, :], E), ALU.mult))
                    me.settle()
                    chosen = score
                    if with_bias:
                        me.did(dve.tensor_tensor(biased[:, :, :], score[:, :, :], over_heads(gate_b[:, :], G), ALU.add))
                        me.settle()
                        chosen = biased
                    dve.memset(pad[:, :], 0.0)
                    for c in range(G):
                        me.did(dve.max(top[:, c, :], chosen[:, c, :]))
                    me.settle()
                    second = top[:, :, 1:2].to_broadcast([P, G, E])
                    me.did(dve.tensor_tensor(over2[:, :, :], chosen[:, :, :], second, ALU.is_gt))
                    me.did(dve.tensor_tensor(is2[:, :, :], chosen[:, :, :], second, ALU.is_equal))
                    me.settle()
                    me.did(dve.tensor_tensor_scan(rank[:, :, :].rearrange("p c e -> p (c e)"), reset,
                                                  is2[:, :, :].rearrange("p c e -> p (c e)"), 0.0, ALU.mult, ALU.add))
                    me.did(dve.tensor_reduce(room[:, :], over2[:, :, :], X_AXIS, ALU.add))
                    me.settle()
                    me.did(dve.tensor_scalar(room[:, :], room[:, :], -1.0, 2.0, ALU.mult, ALU.add))
                    me.settle()
                    me.did(dve.tensor_tensor(rank[:, :, :], rank[:, :, :], over_last(room[:, :], E), ALU.is_le))
                    me.settle()
                    me.did(dve.tensor_tensor(is2[:, :, :], is2[:, :, :], rank[:, :, :], ALU.mult))
                    me.settle()
                    me.did(dve.tensor_tensor(is2[:, :, :], is2[:, :, :], over2[:, :, :], ALU.add))
                    me.settle()
                    dve.tensor_tensor(rw[:, :, 0:E], score[:, :, :], is2[:, :, :], ALU.mult).then_inc(s["rw_ready"], 1)

                dve.wait_ge(s["w_b_in"], 16 * 9)
                route(0, True)
                for k, i in enumerate(UP_ORDER):
                    dve.wait_ge(s["gate_done"], it * UP0 + k + 1)
                    if k >= 4 and k % 2 == 0:
                        dve.wait_ge(s["hid_ready"], it * UP0 // 2 + k // 2 - 1)
                    dve.scalar_tensor_tensor(prod[(k // 2) % 2][:, k % 2, :], ps[:, 2 * (k % 3), :], b1[:, i:i + 1],
                                             gate3[k % 4], ALU.add, ALU.mult).then_inc(s["prod_ready"], 1)
                dve.wait_ge(s["rwT_psum"], it + 1)
                dve.tensor_copy(rwT[:, :], ps[0:E + 1, 6, :]).then_inc(s["rwT_ready"], 1)
                dve.wait_ge(s["rw_ready"], it * N_RT + 1)
                dve.wait_ge(s["x_stored"], 16 * it + 1)
                for half in range(2):
                    chunks = range(CH * half, CH * (half + 1))
                    for c in chunks:
                        dve.wait_ge(s["down_psum"], it * G + c + 1)
                        me.did(dve.tensor_tensor(x2[:, c, :], pair_in[:, c, :], ps[:, 7 - c % 2, 0:P], ALU.add))
                    for e in range(E):
                        for c in chunks:
                            me.settle(0 if e == E - 1 and c == chunks[-1] else CH - 1)
                            o = ps[:, DOWN0[c] + e % 2, (e // 2) * P:(e // 2 + 1) * P]
                            ins = dve.scalar_tensor_tensor(x2[:, c, :], o, rw[:, c, e:e + 1], x2[:, c, :], ALU.mult, ALU.add)
                            if e < E - 1:
                                me.did(ins)
                            else:
                                ins.then_inc(s["merged"], 1)
                    k = 2 * half + 1
                    dve.wait_ge(s["merged"], it * G + CH * (half + 1))
                    norm(k, x2, h0)
                    dve.wait_ge(s["h_ready"], it * N_LN + k + 1)
                    norm(k + 1, h0, h_tok)
                for c in range(G):
                    dve.wait_ge(s["vaug_ready"], it * G + c + 1)
                    qk = ps[:, c, 0:2 * P].rearrange("p (q h d) -> p q h d", q=2, d=AD)
                    at_c = (c % CH) * 2 * AD
                    cos = con[:, C_COS + at_c:C_COS + at_c + 2 * AD].rearrange("p (q d) -> p q d", d=AD)\
                        .unsqueeze(2).to_broadcast([P, 2, AH, AD])
                    sin = con[:, C_SIN + at_c:C_SIN + at_c + 2 * AD].rearrange("p (q d) -> p q d", d=AD)\
                        .unsqueeze(2).to_broadcast([P, 2, AH, AD])
                    if c > 0:
                        dve.wait_ge(s["rot_ready"], it * G + c)
                    me.did(dve.tensor_tensor(rot[:, :, :, :], qk, cos, ALU.mult))
                    for o in range(2):
                        me.did(dve.tensor_tensor(rot2[:, :, :, o::2], qk[:, :, :, 1 - o::2], sin[:, :, :, o::2], ALU.mult))
                    me.settle()
                    dve.tensor_tensor(qk_tok[:, c, :, :, 0:AD], rot[:, :, :, :], rot2[:, :, :, :], ALU.add)\
                        .then_inc(s["rot_ready"], 1)
                for u in range(UNITS):
                    c = unit(u)[1]
                    dve.wait_ge(s["s_scores"], it * UNITS + u + 1)
                    sc = ps[:, 2 * (u % 2):2 * (u % 2) + c + 1, :].rearrange("p k (g n) -> p g k n", n=P)
                    me.did(dve.tensor_reduce(smax[:, u % 2, :], sc, XY_AXIS, ALU.max))
                    me.settle()
                    if u >= 2:
                        dve.wait_ge(s["probs_ready"], it * UNITS + u - 1)
                    dve.tensor_tensor(shifted[u % 2][:, 0:c + 1, :, :].rearrange("p k g n -> p g k n"), sc,
                                      smax[:, u % 2, :].unsqueeze(2).unsqueeze(3).to_broadcast([P, AG, c + 1, P]),
                                      ALU.subtract).then_inc(s["shifted_ready"], 1)
                dve.wait_ge(s["av_psum"], (it + 1) * UNITS)
                av = [ps[:, 6 + q, 0:CH * AH * (AD + 1)].rearrange("p (c h d) -> p c h d", c=CH, d=AD + 1) for q in range(2)]
                for q in range(2):
                    me.did(dve.reciprocal(a_den[:, CH * q:CH * (q + 1), :], av[q][:, :, :, AD]))
                me.settle()
                for q in range(2):
                    ins = dve.tensor_tensor(a_out[:, CH * q:CH * (q + 1), :, :], av[q][:, :, :, 0:AD],
                                            over_last3(a_den[:, CH * q:CH * (q + 1), :], AD), ALU.mult)
                    if q == 0:
                        me.did(ins)
                ins.then_inc(s["aout_ready"], 1)
                dve.wait_ge(s["wo_psum"], it + 1)
                dve.tensor_tensor(xp[:, :, :], ps[:, 0, :].rearrange("p (c d) -> p c d", c=G), h0[:, :, :], ALU.add)\
                    .then_inc(s["xp_ready"], 1)
                dve.wait_ge(s["xp_ready"], it + 1)
                norm(5, xp, h_tok)
                dve.wait_ge(s["h_pool"], it * 2 + 1)
                dve.wait_ge(s["mdown_psum"], it * N_DOWN + 1)
                dve.tensor_tensor(x2[:, :, :], ps[:, 4, :].rearrange("p (c d) -> p c d", c=G), x2[:, :, :], ALU.add)\
                    .then_inc(s["mlp_added"], 1)
                dve.wait_ge(s["mlp_added"], it + 1)
                norm(6, x2, h_tok)
                route(1, False)
                dve.wait_ge(s["rw_ready"], it * N_RT + 2)
                dve.wait_ge(s["h_pool"], it * 2 + 2)
                for e in range(E + 1):
                    dve.wait_ge(s["mdown_psum"], it * N_DOWN + 2 + e)
                    if e > 0:
                        dve.wait_ge(s["mdown_used"], it * E + e)
                    if more and e == AHEAD - 2:
                        first_norm(me, it + 1, 0)
                    if more and e == AHEAD - 1:
                        first_norm(me, it + 1, 1)
                    if e == 0:
                        dve.tensor_tensor(x2[:, :, :], ps[:, 4, :].rearrange("p (c d) -> p c d", c=G), x2[:, :, :], ALU.add)\
                            .then_inc(s["mdown_used"], 1)
                        continue
                    for c in range(G):
                        ins = dve.scalar_tensor_tensor(x2[:, c, :], ps[:, 4 + e % 2, c * P:(c + 1) * P],
                                                       rw[:, c, e - 1:e], x2[:, c, :], ALU.mult, ALU.add)
                        if c < G - 1:
                            me.did(ins)
                    ins.then_inc(s["mdown_used" if e < E else "x_final"], 1)
                if more:
                    assert me.n == DVE_STEPS2, ("DVE_STEPS2", me.n)

            first_norm(start, 0, 0)
            first_norm(start, 0, 1)
            with dve.Fori(0, PAIRS - 1) as it:
                pair_layers(it, True)
            pair_layers(PAIRS - 1, False)


def hidden_tiles(routed, shared):
    w = np.zeros((P, UP0, P), routed.dtype)
    w[:, 0:E] = routed[:, :, :P].transpose(1, 0, 2)
    w[:, E:E + 4, 0:H1R] = routed[0::2, :, P:].transpose(1, 0, 2)
    w[:, E:E + 4, DH:DH + H1R] = routed[1::2, :, P:].transpose(1, 0, 2)
    w[:, E + 4] = shared[:, :P]
    w[:, E + 5, 0:H1R] = shared[:, P:]
    return w.reshape(P, UP0 * P)


def bias_tiles(routed, shared):
    b = np.zeros((P, UP0), routed.dtype)
    b[:, 0:E] = routed[:, :P].T
    b[0:H1R, E:E + 4] = routed[0::2, P:].T
    b[DH:DH + H1R, E:E + 4] = routed[1::2, P:].T
    b[:, E + 4] = shared[:P]
    b[0:H1R, E + 5] = shared[P:]
    return b


def rest_rows(routed, shared):
    w = np.zeros((P, E // 2 + 1, P), routed.dtype)
    w[0:H1R, 0:4] = routed[0::2, P:].transpose(1, 0, 2)
    w[DH:DH + H1R, 0:4] = routed[1::2, P:].transpose(1, 0, 2)
    w[0:H1R, 4] = shared[P:]
    return w


def layouts(i):
    a = {k: np.asarray(v) for k, v in i.items()}
    L0, F0, A1, F1 = "L0_attn_", "L0_ffn_", "L1_attn_", "L1_ffn_"
    qk_order = np.concatenate([np.arange(DH) + DH * (m + QK_TILES * r) for m in range(QK_TILES) for r in range(2)])
    order = np.concatenate([qk_order, KH * DH + qk_order, np.arange(VH * DH) + 2 * KH * DH])
    return {
        "consts": constants(),
        "x": a[L0 + "hidden_states"],
        "w_mix": a[L0 + "W_qkv"][order].T,
        "conv_w": a[L0 + "conv_w"][order, 0].reshape(MIX, P, TAPS).transpose(1, 0, 2),
        "w_z": a[L0 + "W_z"].T,
        "w_ba": np.concatenate([a[L0 + "W_b"], a[L0 + "W_a"]]).T,
        "dt_bias": a[L0 + "dt_bias"], "A_log": a[L0 + "A_log"], "norm_weight": a[L0 + "norm_weight"],
        "w_out": a[L0 + "W_out"].T.reshape(V_TILES, P, P).transpose(1, 0, 2),
        "gate_w": a[F0 + "gate_w"].T, "gate_b": a[F0 + "gate_b"],
        "w1": hidden_tiles(a[F0 + "w1"], a[F0 + "sw1"]), "w3": hidden_tiles(a[F0 + "w3"], a[F0 + "sw3"]),
        "b1": bias_tiles(a[F0 + "b1"], a[F0 + "sb1"]), "b3": bias_tiles(a[F0 + "b3"], a[F0 + "sb3"]),
        "w2": np.concatenate([a[F0 + "w2"][:, :P], a[F0 + "sw2"][None, :P]]).transpose(1, 0, 2),
        "w2r": rest_rows(a[F0 + "w2"], a[F0 + "sw2"]),
        "b2": np.concatenate([a[F0 + "b2"], a[F0 + "sb2"][None]]),
        "ln1_g": a[A1 + "ln1_g"], "ln1_b": a[A1 + "ln1_b"], "ln2_g": a[A1 + "ln2_g"], "ln2_b": a[A1 + "ln2_b"],
        "a_wqkv": a[A1 + "Wqkv"], "a_wo": a[A1 + "Wo"], "a_w1": a[A1 + "W1"],
        "a_b1": a[A1 + "b1"].reshape(HT1, P).T, "a_w2": a[A1 + "W2"].reshape(HT1, P, P).transpose(1, 0, 2),
        "a_b2": a[A1 + "b2"],
        "shared_up": a[F1 + "shared_up"],
        "routed_up": a[F1 + "routed_up"].transpose(1, 0, 2),
        "shared_down": a[F1 + "shared_down"][0].reshape(HT1, P, P).transpose(1, 0, 2),
        "routed_down": a[F1 + "routed_down"].reshape(E, HT1, P, P).transpose(2, 0, 1, 3),
        "router_w": a[F1 + "router_w"],
    }


def kernel(**inputs):
    import concourse.bacc as _bacc
    from concourse.bass_utils import run_bass_kernel_spmd as _run

    nc = _bacc.Bacc("TRN2", target_bir_lowering=False, num_devices=1)
    arrays, t = {}, {}
    for name, v in layouts(inputs).items():
        v = np.ascontiguousarray(v)
        arrays[f"in_{name}"] = v
        t[name] = nc.dram_tensor(f"in_{name}", v.shape, mybir.dt.from_np(v.dtype), kind="ExternalInput").ap()
    out = nc.dram_tensor("out_x", (SEQS, SEQ, P), F32, kind="ExternalOutput").ap()
    program(nc, t, out)
    r = _run(nc, [arrays], core_ids=[0])
    return r.results[0]["out_x"]
```
